# Optimizing a Trainium2 kernel written in Bass

```python
import numpy as np
import jax
import jax.numpy as jnp

def _softmax(x, axis=-1):
    return jax.nn.softmax(x, axis=axis)

def _gelu(x):
    return jax.nn.gelu(x, approximate=True)

def _silu(x):
    return jax.nn.silu(x)

def _sigmoid(x):
    return jax.nn.sigmoid(x)

def _layernorm(x, axis=-1, eps=1e-05):
    m = jnp.mean(x, axis=axis, keepdims=True)
    v = jnp.var(x, axis=axis, keepdims=True)
    return (x - m) / jnp.sqrt(v + eps)

def _scatter_add(tgt, idx, src, axis=0):
    return tgt.at[idx].add(src)

def _segment_sum(src, seg, n):
    return jax.ops.segment_sum(src, seg, n)
kernel_name = 'mk_cond_seq_d2_seqx_r2_1e7950'

def setup_inputs(seed: int=0):
    np.random.seed(seed)
    _w = jnp.asarray

    def _rec_inputs():
        import jax
        import jax.numpy as jnp
        _rk = jax.random.key(seed)
        x = 7.22e-05 + 1 * jax.random.normal(jax.random.fold_in(_rk, 1), (32, 128, 512), jnp.float32)
        _lenS = 128 - jax.random.randint(jax.random.fold_in(_rk, 7), (32,), 0, max(1, 128 // 4) + 1, jnp.int32)
        _lenS2 = 128 - jax.random.randint(jax.random.fold_in(_rk, 8), (32,), 0, max(1, 128 // 4) + 1, jnp.int32)
        cond_2048 = 0.00386106 + 1.00199 * jax.random.normal(jax.random.fold_in(_rk, 11), (32, 1024), jnp.float32)
        _validS = jnp.arange(128)[None, :] < _lenS[:, None]
        _validS2 = jnp.arange(128)[None, :] < _lenS2[:, None]
        _causal = jnp.tril(jnp.ones((128, 128), dtype=bool))
        mask_BxS_ff1 = jnp.where(jnp.ones((32, 128), dtype=bool), 1.0, 0.0).astype(jnp.float32)
        mask_BxSx1_fk1 = jnp.where(jnp.ones((32, 128, 1), dtype=bool), 1.0, 0.0).astype(jnp.float32)
        return (x, cond_2048, mask_BxS_ff1, mask_BxSx1_fk1)
    x, cond_2048, mask_BxS_ff1, mask_BxSx1_fk1 = _rec_inputs()

    def _L0_cond_setup():
        import jax, jax.numpy as jnp
        import numpy as np
        B, T, D, H, TE = (8, 512, 512, 16, 1024)
        LN_EPS = 1e-05

        def layer_norm(x, w, b):
            m = jnp.mean(x, axis=-1, keepdims=True)
            v = jnp.var(x, axis=-1, keepdims=True)
            return (x - m) / jnp.sqrt(v + LN_EPS) * w + b
        key = jax.random.key(seed)
        ks = jax.random.split(key, 8)
        s = lambda k, sh: jax.random.normal(k, sh, jnp.float32) * 0.02
        return dict(x=jax.random.normal(ks[0], (B, T, D), jnp.float32), emb=jax.random.normal(ks[1], (B, TE), jnp.float32), src_mask=jnp.ones((B, T), jnp.float32), norm_w=jnp.ones((D,), jnp.float32), norm_b=jnp.zeros((D,), jnp.float32), q_w=s(ks[2], (D, D)), q_b=jnp.zeros((D,), jnp.float32), k_w=s(ks[3], (D, D)), k_b=jnp.zeros((D,), jnp.float32), v_w=s(ks[4], (D, D)), v_b=jnp.zeros((D,), jnp.float32), emb_w=s(ks[5], (TE, 2 * D)), emb_b=jnp.zeros((2 * D,), jnp.float32), sb_norm_w=jnp.ones((D,), jnp.float32), sb_norm_b=jnp.zeros((D,), jnp.float32), out_w=s(ks[6], (D, D)), out_b=jnp.zeros((D,), jnp.float32))
    _L0_cond_all = _L0_cond_setup()
    _L0_cond_in = {k: v for k, v in _L0_cond_all.items() if k in ('norm_w', 'norm_b', 'q_w', 'q_b', 'k_w', 'k_b', 'v_w', 'v_b', 'emb_w', 'emb_b', 'sb_norm_w', 'sb_norm_b', 'out_w', 'out_b')}
    del _L0_cond_all

    def _L1_cond_setup():
        import jax, jax.numpy as jnp
        import numpy as np
        B, T, D, H, TE = (4, 1024, 512, 8, 1024)
        EPS = 1e-05

        def _ln(x, w, b):
            m = jnp.mean(x, axis=-1, keepdims=True)
            v = jnp.mean((x - m) ** 2, axis=-1, keepdims=True)
            return (x - m) * jax.lax.rsqrt(v + EPS) * w + b
        key = jax.random.key(seed)
        ks = jax.random.split(key, 16)
        s = 0.02
        inp = {'x': jax.random.normal(ks[0], (B, T, D), jnp.float32), 'emb': jax.random.normal(ks[1], (B, TE), jnp.float32), 'src_mask': (jax.random.uniform(ks[2], (B, T, 1)) > 0.2).astype(jnp.float32), 'num_head': H, 'ln_w': jnp.ones((D,), jnp.float32), 'ln_b': jnp.zeros((D,), jnp.float32), 'Wq': jax.random.normal(ks[3], (D, D), jnp.float32) * s, 'bq': jnp.zeros((D,), jnp.float32), 'Wk': jax.random.normal(ks[4], (D, D), jnp.float32) * s, 'bk': jnp.zeros((D,), jnp.float32), 'Wv': jax.random.normal(ks[5], (D, D), jnp.float32) * s, 'bv': jnp.zeros((D,), jnp.float32), 'W_emb': jax.random.normal(ks[6], (TE, 2 * D), jnp.float32) * s, 'b_emb': jnp.zeros((2 * D,), jnp.float32), 'ln2_w': jnp.ones((D,), jnp.float32), 'ln2_b': jnp.zeros((D,), jnp.float32), 'W_out': jax.random.normal(ks[7], (D, D), jnp.float32) * s, 'b_out': jnp.zeros((D,), jnp.float32)}
        return inp
    _L1_cond_all = _L1_cond_setup()
    _L1_cond_in = {k: v for k, v in _L1_cond_all.items() if k in ('ln_w', 'ln_b', 'Wq', 'bq', 'Wk', 'bk', 'Wv', 'bv', 'W_emb', 'b_emb', 'ln2_w', 'ln2_b', 'W_out', 'b_out')}
    del _L1_cond_all
    return {'x': x, 'cond_2048': cond_2048, 'mask_BxS_ff1': mask_BxS_ff1, 'mask_BxSx1_fk1': mask_BxSx1_fk1, 'L0_cond_norm_w': _L0_cond_in['norm_w'], 'L0_cond_norm_b': _L0_cond_in['norm_b'], 'L0_cond_q_w': _L0_cond_in['q_w'], 'L0_cond_q_b': _L0_cond_in['q_b'], 'L0_cond_k_w': _L0_cond_in['k_w'], 'L0_cond_k_b': _L0_cond_in['k_b'], 'L0_cond_v_w': _L0_cond_in['v_w'], 'L0_cond_v_b': _L0_cond_in['v_b'], 'L0_cond_emb_w': _L0_cond_in['emb_w'], 'L0_cond_emb_b': _L0_cond_in['emb_b'], 'L0_cond_sb_norm_w': _L0_cond_in['sb_norm_w'], 'L0_cond_sb_norm_b': _L0_cond_in['sb_norm_b'], 'L0_cond_out_w': _L0_cond_in['out_w'], 'L0_cond_out_b': _L0_cond_in['out_b'], 'L1_cond_ln_w': _L1_cond_in['ln_w'], 'L1_cond_ln_b': _L1_cond_in['ln_b'], 'L1_cond_Wq': _L1_cond_in['Wq'], 'L1_cond_bq': _L1_cond_in['bq'], 'L1_cond_Wk': _L1_cond_in['Wk'], 'L1_cond_bk': _L1_cond_in['bk'], 'L1_cond_Wv': _L1_cond_in['Wv'], 'L1_cond_bv': _L1_cond_in['bv'], 'L1_cond_W_emb': _L1_cond_in['W_emb'], 'L1_cond_b_emb': _L1_cond_in['b_emb'], 'L1_cond_ln2_w': _L1_cond_in['ln2_w'], 'L1_cond_ln2_b': _L1_cond_in['ln2_b'], 'L1_cond_W_out': _L1_cond_in['W_out'], 'L1_cond_b_out': _L1_cond_in['b_out']}

def reference(x, cond_2048, mask_BxS_ff1, mask_BxSx1_fk1, L0_cond_norm_w, L0_cond_norm_b, L0_cond_q_w, L0_cond_q_b, L0_cond_k_w, L0_cond_k_b, L0_cond_v_w, L0_cond_v_b, L0_cond_emb_w, L0_cond_emb_b, L0_cond_sb_norm_w, L0_cond_sb_norm_b, L0_cond_out_w, L0_cond_out_b, L1_cond_ln_w, L1_cond_ln_b, L1_cond_Wq, L1_cond_bq, L1_cond_Wk, L1_cond_bk, L1_cond_Wv, L1_cond_bv, L1_cond_W_emb, L1_cond_b_emb, L1_cond_ln2_w, L1_cond_ln2_b, L1_cond_W_out, L1_cond_b_out):
    import jax
    import jax.numpy as jnp

    def _L0_cond_ref(x, emb, src_mask, norm_w, norm_b, q_w, q_b, k_w, k_b, v_w, v_b, emb_w, emb_b, sb_norm_w, sb_norm_b, out_w, out_b):
        import jax, jax.numpy as jnp
        import numpy as np
        B, T, D, H, TE = (8, 512, 512, 16, 1024)
        LN_EPS = 1e-05

        def layer_norm(x, w, b):
            m = jnp.mean(x, axis=-1, keepdims=True)
            v = jnp.var(x, axis=-1, keepdims=True)
            return (x - m) / jnp.sqrt(v + LN_EPS) * w + b
        Bx, Tx, Dx = x.shape
        xn = layer_norm(x, norm_w, norm_b)
        q = (xn @ q_w + q_b).reshape(Bx, Tx, H, -1)
        k = (xn @ k_w + k_b).reshape(Bx, Tx, H, -1)
        att = jnp.einsum('bnhl,bmhl->bnmh', q, k)
        mask = src_mask.reshape(Bx, 1, Tx, 1)
        att = att + (1.0 - mask) * -1000000.0
        att = jax.nn.softmax(att, axis=2)
        v = ((xn @ v_w + v_b) * src_mask[:, :, None]).reshape(Bx, Tx, H, -1)
        y = jnp.einsum('bnmh,bmhl->bnhl', att, v).reshape(Bx, Tx, Dx)
        e = jax.nn.silu(emb) @ emb_w + emb_b
        scale, shift = jnp.split(e[:, None, :], 2, axis=2)
        h = layer_norm(y, sb_norm_w, sb_norm_b) * (1.0 + scale) + shift
        h = jax.nn.silu(h) @ out_w + out_b
        return x + h

    def _L1_cond_ref(x, emb, src_mask, num_head, ln_w, ln_b, Wq, bq, Wk, bk, Wv, bv, W_emb, b_emb, ln2_w, ln2_b, W_out, b_out):
        import jax, jax.numpy as jnp
        import numpy as np
        B, T, D, H, TE = (4, 1024, 512, 8, 1024)
        EPS = 1e-05

        def _ln(x, w, b):
            m = jnp.mean(x, axis=-1, keepdims=True)
            v = jnp.mean((x - m) ** 2, axis=-1, keepdims=True)
            return (x - m) * jax.lax.rsqrt(v + EPS) * w + b
        b, t, d = x.shape
        h = num_head
        dh = d // h
        xn = _ln(x, ln_w, ln_b)
        q = xn @ Wq + bq
        k = xn @ Wk + bk + (1.0 - src_mask) * -1000000.0
        q = jax.nn.softmax(q.reshape(b, t, h, dh), axis=-1)
        k = jax.nn.softmax(k.reshape(b, t, h, dh), axis=1)
        v = ((xn @ Wv + bv) * src_mask).reshape(b, t, h, dh)
        att = jnp.einsum('bnhd,bnhl->bhdl', k, v)
        y = jnp.einsum('bnhd,bhdl->bnhl', q, att).reshape(b, t, d)
        emb_out = (jax.nn.silu(emb) @ W_emb + b_emb)[:, None, :]
        scale, shift = jnp.split(emb_out, 2, axis=2)
        hh = _ln(y, ln2_w, ln2_b) * (1.0 + scale) + shift
        hh = jax.nn.silu(hh) @ W_out + b_out
        return x + hh
    x = _L0_cond_ref(x, cond_2048, mask_BxS_ff1, L0_cond_norm_w, L0_cond_norm_b, L0_cond_q_w, L0_cond_q_b, L0_cond_k_w, L0_cond_k_b, L0_cond_v_w, L0_cond_v_b, L0_cond_emb_w, L0_cond_emb_b, L0_cond_sb_norm_w, L0_cond_sb_norm_b, L0_cond_out_w, L0_cond_out_b)
    x = _L1_cond_ref(x, cond_2048, mask_BxSx1_fk1, 8, L1_cond_ln_w, L1_cond_ln_b, L1_cond_Wq, L1_cond_bq, L1_cond_Wk, L1_cond_bk, L1_cond_Wv, L1_cond_bv, L1_cond_W_emb, L1_cond_b_emb, L1_cond_ln2_w, L1_cond_ln2_b, L1_cond_W_out, L1_cond_b_out)
    return x

_drawn_inputs = setup_inputs


def setup_inputs(seed=0):
    import zlib

    import numpy as np

    out = dict(_drawn_inputs(seed))
    spreads = {'L0_cond_norm_w': (1.0, 0.2),
     'L0_cond_norm_b': (0.0, 0.1),
     'L0_cond_q_b': (0.0, 0.1),
     'L0_cond_k_b': (0.0, 0.8),
     'L0_cond_v_b': (0.0, 0.1),
     'L0_cond_emb_b': (0.0, 0.1),
     'L0_cond_sb_norm_w': (1.0, 0.2),
     'L0_cond_sb_norm_b': (0.0, 0.1),
     'L0_cond_out_b': (0.0, 0.1),
     'L1_cond_ln_w': (1.0, 0.2),
     'L1_cond_ln_b': (0.0, 0.1),
     'L1_cond_bq': (0.0, 0.8),
     'L1_cond_bk': (0.0, 0.8),
     'L1_cond_bv': (0.0, 0.1),
     'L1_cond_b_emb': (0.0, 0.1),
     'L1_cond_ln2_w': (1.0, 0.2),
     'L1_cond_ln2_b': (0.0, 0.295),
     'L1_cond_b_out': (0.0, 0.1)}
    factors = {'L1_cond_Wq': 8.0, 'L1_cond_Wk': 8.0}
    for name, (base, spread) in spreads.items():
        noise = np.random.default_rng([zlib.crc32(name.encode()), seed]).standard_normal(out[name].shape)
        drawn = base * np.exp(spread * noise) if base else spread * noise
        out[name] = jnp.asarray(drawn.astype(out[name].dtype))
    for name, factor in factors.items():
        out[name] = (out[name] * factor).astype(out[name].dtype)
    return out
```

```python
from contextlib import ExitStack

import concourse.bass as bass
from concourse import mybir

F32 = mybir.dt.float32
F32R = mybir.dt.float32r
BF16 = mybir.dt.bfloat16
ALU = mybir.AluOpType
ACT = mybir.ActivationFunctionType
AX = mybir.AxisListType

P = 128
GROUP = 2
EPS = 1e-5
MASKED = -1000000.0
PART_ROWS = (0, 32, 64)
K_ON_ACT = 2


class At:

    def __init__(self, reg, const):
        self.reg, self.const = reg, const

    def __add__(self, n):
        return At(self.reg, self.const + n)

    def value(self):
        return self.const if self.reg is None else self.reg + self.const


class Stage:

    always = None

    def __init__(self, sem, earlier):
        self.sem, self.earlier = sem, earlier


def done(stage, at):
    if at.reg is None and at.const < 0:
        return stage.always
    return stage.sem, (at + (1 + stage.earlier)).value()


def landed(stage, group, slot=0):
    if group.reg is None and group.const < 0:
        return stage[slot].always
    return stage[slot].sem, (group + stage[slot].earlier).value() * (16 // GROUP) + 16


def upto(stage, value):
    return stage.sem, stage.earlier + value


def build(nc, t, out):
    B, T, D = t["x"].shape
    TE = t["cond_2048"].shape[1]
    C = D // P
    KE = TE // P
    N = GROUP * P
    assert T == P and B % (2 * GROUP) == 0
    layers = [
        dict(H=16, nw=t["L0_cond_norm_w"], nb=t["L0_cond_norm_b"],
             W=[t["L0_cond_q_w"], t["L0_cond_k_w"], t["L0_cond_v_w"], t["L0_cond_out_w"]],
             b=[t["L0_cond_q_b"], t["L0_cond_k_b"], t["L0_cond_v_b"], t["L0_cond_out_b"]],
             ew=t["L0_cond_emb_w"], eb=t["L0_cond_emb_b"], w2=t["L0_cond_sb_norm_w"], b2=t["L0_cond_sb_norm_b"],
             mask=t["mask_BxS_ff1"]),
        dict(H=8, nw=t["L1_cond_ln_w"], nb=t["L1_cond_ln_b"],
             W=[t["L1_cond_Wq"], t["L1_cond_Wk"], t["L1_cond_Wv"], t["L1_cond_W_out"]],
             b=[t["L1_cond_bq"], t["L1_cond_bk"], t["L1_cond_bv"], t["L1_cond_b_out"]],
             ew=t["L1_cond_W_emb"], eb=t["L1_cond_b_emb"], w2=t["L1_cond_ln2_w"], b2=t["L1_cond_ln2_b"],
             mask=t["mask_BxSx1_fk1"].rearrange("b s o -> b (s o)")),
    ]
    H0, H1 = layers[0]["H"], layers[1]["H"]
    DH0, DH1 = D // H0, D // H1
    HC0 = P // DH0
    WQ, WK, WV, WO = range(4)

    middle = nc.dram_tensor("between_layers", [B, T, D], F32, kind="Internal").ap()

    with ExitStack() as ctx:
        def sb(name, shape, dt=F32):
            return ctx.enter_context(nc.sbuf_tensor(name, shape, dt))

        def sem(name):
            return ctx.enter_context(nc.semaphore(name))

        w_hi = sb("w_hi", [P, 4, C, D], F32R)
        w_lo = sb("w_lo", [P, 4, C, D], F32R)
        k_blocks = sb("k_blocks", [P, 2, C, GROUP, HC0, P])
        w_raw = k_blocks[:].rearrange("p a b c d e -> p (a b c d e)").rearrange("p (w c n) -> p w c n", w=4, c=C)
        col = sb("col", [P, 6, C])
        NW, NBI, W2, B2, QB, KB = range(6)
        bias_wide = sb("bias_wide", [P, 4, D])
        film_a = sb("film_a", [P, C, B])
        film_b = sb("film_b", [P, C, B])
        silu_cond = sb("silu_cond", [P, KE, B])
        mask_rows = sb("mask_rows", [B, P])
        mask_parts = sb("mask_parts", [B, 3, P], BF16)
        mask_tmp = sb("mask_tmp", [B, 2, P])
        mask_wide = sb("mask_wide", [P, B * P], BF16)
        ones_parts = sb("ones_parts", [P, P], BF16)
        mask_col = sb("mask_col", [P, B])
        mask_now = sb("mask_now", [P, 1])
        ident = sb("ident", [P, P])
        minus_half = sb("minus_half", [P, 1])
        x_in = sb("x_in", [P, 2, D])
        xn = sb("xn", [P, 2, D])
        stat = sb("stat", [P, 2, 2, 16])
        xt_hi = sb("xt_hi", [P, 2, C, N], F32R)
        xt_lo = sb("xt_lo", [P, 2, C, N], F32R)
        q_t = sb("q_t", [P, 2, C * N])
        v_s = sb("v_s", [P, 2, GROUP, D])
        prob = sb("prob", [P, 2, H0, P])
        emb_ring = prob[:].rearrange("p a h n -> p (a h n)").rearrange("p (k n) -> p k n", k=4)
        prob_t = sb("prob_t", [P, 2, D])
        row_max = sb("row_max", [P, 2, H0])
        row_sum = sb("row_sum", [P, 2, H0])
        y_t = sb("y_t", [P, D])
        norm_b_wide = y_t[:].rearrange("p (c n) -> p c n", c=C)
        y_s = sb("y_s", [P, D])
        yn = sb("yn", [P, 2, D])
        z_a = sb("z_a", [P, D])
        z_s = sb("z_s", [P, 2, D])
        th = sb("th", [P, D])
        s_s = th
        s_hi = sb("s_hi", [P, 2, D], F32R)
        s_lo = sb("s_lo", [P, 2, D], F32R)
        x_res = sb("x_res", [P, 2, D])
        x_out = x_res

        bank = [ctx.enter_context(nc.psum_tensor(f"bank{i}", [P, D], F32)) for i in range(8)]

        def chunks(ap):
            return ap.rearrange("p (c n) -> p c n", c=C)

        k_exp = q_t
        q_exp = k_blocks[:, 0].rearrange("p a b c d -> p (a b c d)")[:, 0:2 * GROUP * D] \
            .rearrange("p (s b d) -> p s b d", s=2, b=GROUP)
        k_tmp = k_blocks[:, 1].rearrange("p a b c d -> p (a b c d)")[:, 0:2 * D].rearrange("p (s d) -> p s d", s=2)
        q_tmp = k_blocks[:, 1].rearrange("p a b c d -> p (a b c d)")[:, 2 * D:3 * D]
        k_tok = prob_t[:, 0, :]
        q_feat = prob_t[:, 1, :]
        kv_blocks = prob[:].rearrange("p a h n -> p (a h n)")[:, 0:D]
        k_max = sb("k_max", [P, 2, 2 * GROUP])
        k_sum = sb("k_sum", [P, 2, 2, 2 * GROUP])
        k_rec = sb("k_rec", [P, 2, 2, 2 * GROUP])
        q_max = sb("q_max", [P, H1])
        q_sum = sb("q_sum", [P, H1])
        q_rec = sb("q_rec", [P, 2, GROUP, H1])
        rec0 = sb("rec0", [P, 2, H0])

        once = sem("once")
        consts = sem("consts")
        Stage.always = (consts, 1)
        cond_in = sem("cond_in")
        cond_dve = sem("cond_dve")
        cond_act = sem("cond_act")
        cond_pe = sem("cond_pe")
        finished = [sem(f"layer{l}_finished") for l in range(2)]

        def stages(names, earlier=0):
            return {n: Stage(sem(n), earlier) for n in names.split()}

        def counted_on(these, earlier):
            return {n: Stage(v.sem, earlier) for n, v in these.items()}

        SETUP = dict(par_in=16 * 9, mask_in=16, mask_moved=16 * len(PART_ROWS), mask_dve=6, mask_pe=1, mask_col_ready=1,
                     beta_wide=1, bias_pe=3, bias_dve=3, scaled=4, w_high=4, w_split=4, raw_free=1, zeroed=1,
                     tr_pe=2, tr_dve=2, emb_pe=KE, emb_dve=2, film_pe=1, film_dve=4,
                     ready_dve=1, ready_act=1, ready_pool=1, ready_pe=1)
        SETUP |= {f"w_in{j}": 16 for j in range(4)} | {f"emb_in{k}": 16 * KE // 4 for k in range(4)}
        STAGES = ("stats aggr rstd_a rstd_b neg_mean xn_full xn_turned xt_high xt_low "
                  "pa_pe pb_pe pa_out pb_out ka_pe kb_pe ka_out ka_out2 kb_out kb_out2 v_pe v_add v_mask mask_now "
                  "y_norm stats2 aggr2 rstd2_a rstd2_b neg_mean2 yn_full h_pe z_a_full z_full tanh_full s_full "
                  "s_high s_low o_pe o_out res_full y_pe")
        only0 = ("s_pe0 s_pe1 s_pe2 s_pe3 smax0 smax1 smax2 smax3 sub0 sub1 sub2 sub3 exp0 exp1 exp2 exp3 "
                 "sum0 sum1 sum2 sum3 rec pt_pe0 pt_pe1 pt_pe2 pt_pe3 pt_out0 pt_out1 pt_out2 pt_out3 pv0 pv1 pv2 pv3 "
                 "pv_out")
        only1 = ("kt_pe qt_pe kt_out qt_out att_pe att_out kbias0 kbias1 kmax0 kmax1 ksub0 ksub1 kexp0 kexp1 ksum0 ksum1 krec "
                 "q_pe q_add qmax qsub qexp qsum qrec")
        both = stages(STAGES)
        moved = {n: [sem(f"{n}{b}") for b in range(GROUP)] for n in ("x_in_full", "res_in", "stored")}
        setup = [{n: Stage(sem(n), 0) for n in SETUP}]
        setup.append({n: Stage(v.sem, SETUP[n]) for n, v in setup[0].items()})
        S = [setup[0] | both | stages(only0), setup[1] | counted_on(both, B) | stages(only1)]
        for l in range(2):
            S[l] |= {n: [Stage(v, B * l) for v in places] for n, places in moved.items()}

        src = [t["x"], middle]
        dst = [middle, out]

        def program(eng, l, front, step, back):
            front(At(None, 0), 0)
            step(At(None, GROUP), 1, At(None, 0), 0)
            with eng.Fori(GROUP, B - 3 * GROUP + 1, 2 * GROUP) as r:
                step(At(r, GROUP), 0, At(r, 0), 1)
                step(At(r, 2 * GROUP), 1, At(r, GROUP), 0)
            back(At(None, B - GROUP), 1)

        def sequence(dram, at):
            if at.reg is None:
                return dram[at.const]
            return dram[bass.ds(at.value(), 1)].rearrange("o t d -> (o t) d")

        def batch_cols(tile, at, width):
            if at.reg is None:
                return tile[:, at.const * width:(at.const + 1) * width]
            return tile[:, bass.ds(at.value() * width, width)]

        def film_of(tile, at):
            if at.reg is None:
                v = tile[:, :, at.const:at.const + 1]
            else:
                v = tile[:, :, bass.ds(at.value(), 1)]
            return v.broadcast_to([P, C, P])

        block = ctx.enter_context(nc.Block())

        @block.sync
        def _(sp):
            for l, L in enumerate(layers):
                s = S[l]
                if l == 1:
                    sp.wait_ge(finished[0], 4)
                for j, p in enumerate(("nw", "nb", "w2", "b2")):
                    sp.dma_start(col[:, j, :], L[p].rearrange("(c p) -> p c", p=P), allow_slow_non_contiguous=True
                                 ).then_inc(s["par_in"].sem, 16)
                for j in range(4):
                    sp.dma_start(w_raw[:, j], L["W"][j].rearrange("(c p) n -> p c n", p=P)).then_inc(s[f"w_in{j}"].sem, 16)
                    sp.dma_start(bias_wide[:, j, :], L["b"][j].rearrange("(o n) -> o n", o=1).broadcast_to([P, D])
                                 ).then_inc(s["par_in"].sem, 16)
                sp.dma_start(mask_rows[:], L["mask"]).then_inc(s["mask_in"].sem, 16)
                if l == 0:
                    sp.dma_start(x_in[0:B, :, :].rearrange("p a b -> p (a b)"), t["cond_2048"]).then_inc(cond_in, 16)
                sp.dma_start(x_out[0:B].rearrange("p a n -> p (a n)"),
                             L["eb"].rearrange("(o n) -> o n", o=1).broadcast_to([B, 2 * D])).then_inc(s["par_in"].sem, 16)
                for k in range(KE):
                    if k >= 4:
                        sp.wait_ge(*upto(s["emb_pe"], k - 3))
                    sp.dma_start(emb_ring[:, k % 4], L["ew"][k * P:(k + 1) * P, :]).then_inc(s[f"emb_in{k % 4}"].sem, 16)
                sp.wait_ge(*upto(s["mask_dve"], 6))
                for j, row in enumerate(PART_ROWS):
                    sp.dma_start(mask_wide[row:row + 1, :].rearrange("o (b n) -> o b n", b=B),
                                 mask_parts[:, j, :]).then_inc(s["mask_moved"].sem, 16)
                for n in ("ready_dve", "ready_act", "ready_pool", "ready_pe"):
                    sp.wait_ge(*upto(s[n], 1))

                def load_front(f, slot):
                    for b in range(GROUP):
                        sp.wait_ge(*done(s["xn_full"], f + (b - 2)))
                        sp.wait_ge(*done(s["stats"], f + (b - 2)))
                        sp.dma_start(x_in[:, b, :], sequence(src[l], f + b)).then_inc(s["x_in_full"][b].sem, 16)

                def load_back(k, slot):
                    for b in range(GROUP):
                        sp.wait_ge(*landed(s["stored"], k + (-GROUP), b))
                        sp.dma_start(x_res[:, b, :], sequence(src[l], k + b)).then_inc(s["res_in"][b].sem, 16)

                def store_back(k, slot):
                    for b in range(GROUP):
                        sp.wait_ge(*done(s["o_out"], k + b))
                        sp.dma_start(sequence(dst[l], k + b), x_out[:, b, :]).then_inc(s["stored"][b].sem, 16)

                def step(f, fslot, k, kslot):
                    load_front(f, fslot)
                    load_back(k, kslot)
                    store_back(k, kslot)

                def back(k, kslot):
                    load_back(k, kslot)
                    store_back(k, kslot)

                program(sp, l, load_front, step, back)
                for b in range(GROUP):
                    sp.wait_ge(*landed(s["stored"], At(None, B - GROUP), b))
                if l == 0:
                    sp.wait_ge(finished[0], 4)

        @block.gpsimd
        def _(pool):
            pool.memset(ident[:], 0.0).then_inc(once, 1)
            pool.wait_ge(once, 1)
            pool.affine_select(out=ident[:], in_=ident[:], compare_op=ALU.not_equal, fill=1.0, base=0,
                               pattern=[[-1, P]], channel_multiplier=1).then_inc(once, 1)
            pool.memset(minus_half[:], -0.5).then_inc(once, 1)
            pool.memset(mask_wide[:], 0.0).then_inc(once, 1)
            pool.memset(ones_parts[:], 0.0).then_inc(once, 1)
            pool.wait_ge(once, 5)
            for r0 in PART_ROWS:
                last = pool.memset(ones_parts[r0:r0 + 1, :], 1.0)
            last.then_inc(once, 1)
            pool.wait_ge(once, 6)
            pool.memset(k_max[:], 0.0).then_inc(consts, 1)
            for l, L in enumerate(layers):
                s = S[l]
                if l == 1:
                    pool.wait_ge(finished[0], 4)
                pool.wait_ge(*upto(s["raw_free"], 1))
                pool.wait_ge(*upto(s["w_high"], 4))
                pool.wait_ge(*upto(s["bias_pe"], 3))
                if l == 0:
                    pool.memset(k_blocks[:], 0.0).then_inc(s["zeroed"].sem, 1)
                else:
                    pool.wait_ge(*upto(s["emb_pe"], KE))
                    pool.memset(kv_blocks, 0.0).then_inc(s["zeroed"].sem, 1)
                pool.wait_ge(*upto(s["mask_col_ready"], 1))
                pool.wait_ge(*upto(s["par_in"], 16 * 9))
                pool.wait_ge(*upto(s["zeroed"], 1))
                pool.drain().then_inc(s["ready_pool"].sem, 1)
                for n in ("ready_dve", "ready_act", "ready_pe"):
                    pool.wait_ge(*upto(s[n], 1))

                def rsqrt_norm(b, which, mv, a_in, rs, nm, full, src_ap, dst_ap, at, dst_free):
                    v = stat[:, which, b, :]
                    pool.wait_ge(*done(s[mv], at))
                    pool.nop(nofuse=True)
                    pool.tensor_scalar(v[:, 8:9], v[:, 7:8], EPS, None, ALU.add).then_inc(s[a_in].sem, 1)
                    pool.tensor_scalar(v[:, 10:11], v[:, 6:7], -1.0, None, ALU.mult).then_inc(s[nm].sem, 1)
                    pool.wait_ge(*done(s[a_in], at))
                    pool.tensor_tensor(v[:, 9:10], v[:, 8:9], minus_half[:], ALU.pow).then_inc(s[rs].sem, 1)
                    pool.wait_ge(*done(s[rs], at))
                    pool.wait_ge(*done(s[nm], at))
                    for d in dst_free:
                        pool.wait_ge(*done(d, at + (-2)))
                    pool.nop(nofuse=True)
                    pool.tensor_scalar(dst_ap, src_ap, v[:, 10:11], v[:, 9:10], ALU.add, ALU.mult
                                       ).then_inc(s[full].sem, 1)

                def norm1(f, b):
                    pool.wait_ge(*landed(s["x_in_full"], f, b))
                    rsqrt_norm(b, 0, "aggr", "rstd_a", "rstd_b", "neg_mean", "xn_full",
                               x_in[:, b, :], xn[:, b, :], f + b, [s["xn_turned"]])

                def norm2(k, b):
                    rsqrt_norm(b, 1, "aggr2", "rstd2_a", "rstd2_b", "neg_mean2", "yn_full",
                               y_s[:], yn[:, b, :], k + b, [s["h_pe"]])

                def v_mask(f, slot, b):
                    pool.wait_ge(*done(s["v_mask"], f + (b - 1)))
                    pool.tensor_copy(mask_now[:], mask_at(f + b)).then_inc(s["mask_now"].sem, 1)
                    pool.wait_ge(*done(s["mask_now"], f + b))
                    pool.wait_ge(*done(s["v_add"], f + b))
                    pool.nop(nofuse=True)
                    pool.tensor_scalar(v_s[:, slot, b, :], v_s[:, slot, b, :], mask_now[:], None,
                                       ALU.mult).then_inc(s["v_mask"].sem, 1)

                def mask_at(at):
                    if at.reg is None:
                        return mask_col[:, at.const:at.const + 1]
                    return mask_col[:, bass.ds(at.value(), 1)]

                def add_shift(k, b):
                    pool.wait_ge(*done(s["z_a_full"], k + b))
                    pool.wait_ge(*done(s["s_full"], k + (b - 2)))
                    pool.tensor_tensor(chunks(z_s[:, b, :]), chunks(z_a[:]), film_of(film_b, k + b), ALU.add
                                       ).then_inc(s["z_full"].sem, 1)

                def residual(k, b):
                    pool.wait_ge(*landed(s["res_in"], k, b))
                    pool.tensor_tensor(x_res[:, b, :], x_res[:, b, :], bias_wide[:, WO, :], ALU.add
                                       ).then_inc(s["res_full"].sem, 1)

                def front(f, slot):
                    for b in range(GROUP):
                        norm1(f, b)
                    for b in range(GROUP):
                        v_mask(f, slot, b)

                def step(f, fslot, k, kslot):
                    norm1(f, 0)
                    norm1(f, 1)
                    residual(k, 0)
                    residual(k, 1)
                    norm2(k, 0)
                    add_shift(k, 0)
                    v_mask(f, fslot, 0)
                    norm2(k, 1)
                    add_shift(k, 1)
                    v_mask(f, fslot, 1)

                def back(k, kslot):
                    for b in range(GROUP):
                        residual(k, b)
                    norm2(k, 0)
                    add_shift(k, 0)
                    norm2(k, 1)
                    add_shift(k, 1)

                program(pool, l, front, step, back)
                if l == 0:
                    pool.wait_ge(*done(s["z_full"], At(None, B - 1)))
                    pool.drain().then_inc(finished[0], 1)

        @block.scalar
        def _(act):
            act.wait_ge(consts, 1)
            act.wait_ge(cond_in, 16)
            act.activation(xn[0:B].rearrange("p a n -> p (a n)"), x_in[0:B].rearrange("p a n -> p (a n)"), ACT.Tanh,
                           scale=0.5).then_inc(cond_act, 1)
            for l, L in enumerate(layers):
                s = S[l]
                if l == 1:
                    act.wait_ge(finished[0], 4)
                for j in range(4):
                    act.wait_ge(*upto(s["scaled"], j + 1))
                    act.activation(w_hi[:, j], w_raw[:, j], ACT.Copy).then_inc(s["w_high"].sem, 1)
                act.wait_ge(*upto(s["w_high"], 4))
                act.drain().then_inc(s["ready_act"].sem, 1)
                for n in ("ready_dve", "ready_pool", "ready_pe"):
                    act.wait_ge(*upto(s[n], 1))

                def xt_high(f, slot, b):
                    act.wait_ge(*done(s["xn_turned"], f + b))
                    act.wait_ge(*done(s["v_pe" if l == 0 else "q_pe"], f + (-GROUP - 1)))
                    act.activation(xt_hi[:, slot, :, b * P:(b + 1) * P], chunks(bank[6 + b][:]), ACT.Copy
                                   ).then_inc(s["xt_high"].sem, 1)

                def q_out(f, slot, pair):
                    act.wait_ge(*done(s["pa_pe" if pair == 0 else "pb_pe"], f))
                    src_bank = bank[6 + pair][:].rearrange("p (c n) -> p c n", c=2)
                    qv = q_t[:, slot, :].rearrange("p (c n) -> p c n", c=C)
                    for j in range(2):
                        c = 2 * pair + j
                        last = act.activation(qv[:, c, :], src_bank[:, j, :], ACT.Identity,
                                              bias=col[:, QB, c:c + 1])
                    last.then_inc(s["pa_out" if pair == 0 else "pb_out"].sem, GROUP)

                def k_out(f, slot, pair):
                    act.wait_ge(*done(s["ka_pe" if pair == 0 else "kb_pe"], f))
                    src_bank = bank[7][:].rearrange("p (c b n) -> p c b n", c=2, b=GROUP)
                    for j in range(2):
                        c = 2 * pair + j
                        for r in range(K_ON_ACT):
                            q4 = slice(DH0 * r, DH0 * (r + 1))
                            last = act.activation(k_blocks[q4, slot, c, :, r, :], src_bank[q4, j], ACT.Identity,
                                                  bias=col[q4, KB, c:c + 1])
                    last.then_inc(s["ka_out" if pair == 0 else "kb_out"].sem, GROUP)

                def exps(k, b):
                    for c in range(C):
                        act.wait_ge(*done(s[f"sub{c}"], k + b))
                        v = prob[:, b, 4 * c:4 * c + 4, :]
                        act.activation(v, v, ACT.Exp).then_inc(s[f"exp{c}"].sem, 1)

                def prob_turned(k, b):
                    for c in range(C):
                        act.wait_ge(*done(s[f"pt_pe{c}"], k + b))
                        if c >= 2:
                            act.wait_ge(*done(s[f"pv{c - 2}"], k + b))
                        else:
                            act.wait_ge(*done(s[f"pv{c + 2}"], k + (b - 1)))
                        act.activation(prob_t[:, c % 2, :], bank[4 + c % 2][:], ACT.Copy).then_inc(s[f"pt_out{c}"].sem, 1)

                def y_t_out(k, b):
                    act.wait_ge(*done(s["pv3"], k + b))
                    act.wait_ge(*done(s["y_pe"], k + (b - 1)))
                    act.activation(y_t[:], bank[6][:], ACT.Copy).then_inc(s["pv_out"].sem, 1)

                def tanh(k, b):
                    act.wait_ge(*done(s["z_full"], k + b))
                    act.wait_ge(*done(s["s_low"], k + (b - 1)))
                    act.wait_ge(*done(s["s_high"], k + (b - 1)))
                    act.activation(th[:], z_s[:, b, :], ACT.Tanh, scale=0.5).then_inc(s["tanh_full"].sem, 1)

                def s_high(k, b):
                    act.wait_ge(*done(s["s_full"], k + b))
                    act.wait_ge(*done(s["o_pe"], k + (b - 2)))
                    act.activation(s_hi[:, b, :], s_s[:], ACT.Copy).then_inc(s["s_high"].sem, 1)

                def k_bias(f, slot, pair):
                    act.wait_ge(*done(s["ka_pe" if pair == 0 else "kb_pe"], f))
                    src_bank = bank[6 + pair][:].rearrange("p (c n) -> p c n", c=2)
                    act.wait_ge(*done(s[f"ksub{pair}"], f + (-GROUP)))
                    kt = k_tmp[:, pair, :].rearrange("p (c n) -> p c n", c=2)
                    for j in range(2):
                        c = 2 * pair + j
                        last = act.activation(kt[:, j, :], src_bank[:, j, :], ACT.Identity,
                                              bias=col[:, KB, c:c + 1])
                    last.then_inc(s[f"kbias{pair}"].sem, GROUP)

                def k_exps(f, slot, pair):
                    act.wait_ge(*done(s[f"ksub{pair}"], f))
                    v = k_exp[:, slot, pair * D:(pair + 1) * D]
                    act.activation(v, v, ACT.Exp).then_inc(s[f"kexp{pair}"].sem, GROUP)

                def q_exps(f, slot, b):
                    act.wait_ge(*done(s["qsub"], f + b))
                    v = q_exp[:, slot, b, :]
                    act.activation(v, v, ACT.Exp).then_inc(s["qexp"].sem, 1)

                def kt_out(k, b):
                    act.wait_ge(*done(s["kt_pe"], k + b))
                    act.wait_ge(*done(s["att_pe"], k + (b - 1)))
                    act.activation(k_tok, bank[0][:], ACT.Copy).then_inc(s["kt_out"].sem, 1)

                def qt_out(k, b):
                    act.wait_ge(*done(s["qt_pe"], k + b))
                    act.wait_ge(*done(s["y_pe"], k + (b - 1)))
                    act.activation(q_feat, bank[1][:], ACT.Copy).then_inc(s["qt_out"].sem, 1)

                def step0(f, fslot, k, kslot):
                    if f:
                        xt_high(f, fslot, 0)
                        xt_high(f, fslot, 1)
                    if k:
                        exps(k, 0)
                    if f:
                        q_out(f, fslot, 0)
                        q_out(f, fslot, 1)
                    if k:
                        prob_turned(k, 0)
                        y_t_out(k, 0)
                        exps(k, 1)
                    if f:
                        k_out(f, fslot, 0)
                        k_out(f, fslot, 1)
                    if k:
                        prob_turned(k, 1)
                        y_t_out(k, 1)
                        for b in range(GROUP):
                            tanh(k, b)
                            s_high(k, b)

                def step1(f, fslot, k, kslot):
                    if k:
                        kt_out(k, 0)
                        qt_out(k, 0)
                    if f:
                        xt_high(f, fslot, 0)
                        xt_high(f, fslot, 1)
                        k_bias(f, fslot, 0)
                        k_exps(f, fslot, 0)
                        k_bias(f, fslot, 1)
                        k_exps(f, fslot, 1)
                    if k:
                        kt_out(k, 1)
                        qt_out(k, 1)
                        tanh(k, 0)
                        s_high(k, 0)
                    if f:
                        q_exps(f, fslot, 0)
                    if k:
                        tanh(k, 1)
                    if f:
                        q_exps(f, fslot, 1)
                    if k:
                        s_high(k, 1)

                st = step0 if l == 0 else step1
                program(act, l, lambda f, sl: st(f, sl, None, None), st, lambda k, sl: st(None, None, k, sl))
                if l == 0:
                    act.wait_ge(*done(s["s_high"], At(None, B - 1)))
                    act.drain().then_inc(finished[0], 1)

        @block.vector
        def _(dve):
            dve.wait_ge(consts, 1)
            flat = lambda v: v[0:B].rearrange("p a n -> p (a n)")
            dve.wait_ge(cond_act, 1)
            dve.scalar_tensor_tensor(out=flat(yn[:]), in0=flat(xn[:]), scalar=1.0, in1=flat(x_in[:]),
                                     op0=ALU.add, op1=ALU.mult).then_inc(cond_dve, 1)
            dve.wait_ge(cond_dve, 1)
            dve.tensor_scalar(flat(z_s[:]), flat(yn[:]), 0.5, None, ALU.mult).then_inc(cond_dve, 1)
            dve.wait_ge(cond_pe, 1)
            dve.tensor_copy(silu_cond[:].rearrange("p k b -> p (k b)"), bank[0][:, 0:KE * B]).then_inc(cond_dve, 1)
            for l, L in enumerate(layers):
                s = S[l]
                if l == 1:
                    dve.wait_ge(finished[0], 4)
                dve.wait_ge(*upto(s["mask_in"], 16))
                md = s["mask_dve"]
                dve.tensor_scalar(mask_tmp[:, 0, :], mask_rows[:], -1.0, 1.0, ALU.mult, ALU.add).then_inc(md.sem, 1)
                dve.wait_ge(*upto(md, 1))
                dve.tensor_scalar(mask_tmp[:, 1, :], mask_tmp[:, 0, :], MASKED, None, ALU.mult).then_inc(md.sem, 1)
                dve.wait_ge(*upto(md, 2))
                dve.tensor_copy(mask_parts[:, 0, :], mask_tmp[:, 1, :]).then_inc(md.sem, 1)
                dve.wait_ge(*upto(md, 3))
                dve.tensor_tensor(mask_tmp[:, 0, :], mask_tmp[:, 1, :], mask_parts[:, 0, :], ALU.subtract).then_inc(md.sem, 1)
                dve.wait_ge(*upto(md, 4))
                dve.tensor_copy(mask_parts[:, 1, :], mask_tmp[:, 0, :]).then_inc(md.sem, 1)
                dve.wait_ge(*upto(md, 5))
                dve.tensor_tensor(mask_parts[:, 2, :], mask_tmp[:, 0, :], mask_parts[:, 1, :], ALU.subtract).then_inc(md.sem, 1)
                dve.wait_ge(*upto(s["mask_pe"], 1))
                dve.tensor_copy(mask_col[:], bank[5][:, 0:B]).then_inc(s["mask_col_ready"].sem, 1)
                dve.wait_ge(*upto(s["par_in"], 16 * 9))
                dve.tensor_copy(norm_b_wide, col[:, NBI, :].rearrange("p (c o) -> p c o", o=1).broadcast_to([P, C, P])
                                ).then_inc(s["beta_wide"].sem, 1)
                for j in range(4):
                    dve.wait_ge(*upto(s[f"w_in{j}"], 16))
                    if j < 3:
                        dve.wait_ge(*upto(s["bias_pe"], j + 1))
                        dve.tensor_tensor(bias_wide[:, j, :], bias_wide[:, j, :], bank[j][:], ALU.add
                                          ).then_inc(s["bias_dve"].sem, 1)
                        for c in range(C):
                            last = dve.tensor_scalar(w_raw[:, j, c], w_raw[:, j, c], col[:, NW, c:c + 1], None, ALU.mult)
                    else:
                        last = dve.tensor_scalar(w_raw[:, j], w_raw[:, j], 0.5, None, ALU.mult)
                    last.then_inc(s["scaled"].sem, 1)
                    dve.wait_ge(*upto(s["scaled"], j + 1))
                    dve.wait_ge(*upto(s["w_high"], j + 1))
                    dve.tensor_tensor(w_lo[:, j], w_raw[:, j], w_hi[:, j].bitcast(F32), ALU.subtract
                                      ).then_inc(s["w_split"].sem, 1)
                dve.wait_ge(*upto(s["w_split"], 4))
                dve.drain().then_inc(s["raw_free"].sem, 1)
                for j in range(2):
                    dve.wait_ge(*upto(s["tr_pe"], j + 1))
                    dve.tensor_copy(col[:, QB + j, :], chunks(bank[3 + j][:])[:, :, 0]).then_inc(s["tr_dve"].sem, 1)
                e_rows = yn[0:B].rearrange("p a n -> p (a n)")
                eb_rows = x_out[0:B].rearrange("p a n -> p (a n)")
                dve.wait_ge(*upto(s["emb_pe"], KE))
                for h in range(2):
                    dve.tensor_tensor(e_rows[:, h * D:(h + 1) * D], bank[6 + h][0:B, :], eb_rows[:, h * D:(h + 1) * D],
                                      ALU.add).then_inc(s["emb_dve"].sem, 1)
                dve.wait_ge(*upto(s["film_pe"], 1))
                et = xn[:].rearrange("p a n -> p (a n)")[:, 0:2 * C * B].rearrange("p (c b) -> p c b", b=B)
                fd = s["film_dve"]
                dve.tensor_copy(et.rearrange("p c b -> p (c b)"), bank[0][:, 0:2 * C * B]).then_inc(fd.sem, 1)
                dve.wait_ge(*upto(fd, 1))
                wide = lambda i: col[:, i, :].rearrange("p (c o) -> p c o", o=1).broadcast_to([P, C, B])
                dve.scalar_tensor_tensor(out=film_a[:], in0=et[:, 0:C, :], scalar=1.0, in1=wide(W2),
                                         op0=ALU.add, op1=ALU.mult).then_inc(fd.sem, 1)
                dve.scalar_tensor_tensor(out=film_b[:], in0=et[:, 0:C, :], scalar=1.0, in1=wide(B2),
                                         op0=ALU.add, op1=ALU.mult).then_inc(fd.sem, 1)
                dve.wait_ge(*upto(fd, 3))
                dve.tensor_tensor(film_b[:], film_b[:], et[:, C:2 * C, :], ALU.add).then_inc(fd.sem, 1)
                dve.wait_ge(*upto(fd, 4))
                dve.wait_ge(*upto(s["tr_dve"], 2))
                dve.wait_ge(*upto(s["zeroed"], 1))
                dve.drain().then_inc(s["ready_dve"].sem, 1)
                for n in ("ready_pool", "ready_act", "ready_pe"):
                    dve.wait_ge(*upto(s[n], 1))

                def moments(which, b, src_ap, st, ag, at):
                    v = stat[:, which, b, :]
                    dve.bn_stats(v[:, 0:6], src_ap).then_inc(s[st].sem, 1)
                    dve.wait_ge(*done(s[st], at))
                    dve.wait_ge(*done(s["xn_full" if which == 0 else "yn_full"], at + (-2)))
                    dve.nop(nofuse=True)
                    dve.bn_aggr(v[:, 6:8], v[:, 0:6]).then_inc(s[ag].sem, 1)

                def stats1(f, b):
                    dve.wait_ge(*landed(s["x_in_full"], f, b))
                    moments(0, b, x_in[:, b, :], "stats", "aggr", f + b)

                def xt_low(f, slot, b):
                    dve.wait_ge(*done(s["xt_high"], f + b))
                    hs = xt_hi[:, slot, :, b * P:(b + 1) * P]
                    dve.tensor_tensor(xt_lo[:, slot, :, b * P:(b + 1) * P], chunks(bank[6 + b][:]), hs.bitcast(F32),
                                      ALU.subtract).then_inc(s["xt_low"].sem, 1)

                def softmax(k, b):
                    for c in range(C):
                        sc = bank[c][:].rearrange("p (r n) -> p r n", r=4)
                        mx = row_max[:, b, 4 * c:4 * c + 4]
                        dve.wait_ge(*done(s[f"s_pe{c}"], k + b))
                        dve.tensor_reduce(mx, sc, AX.X, ALU.max).then_inc(s[f"smax{c}"].sem, 1)
                        dve.wait_ge(*done(s[f"smax{c}"], k + b))
                        dve.wait_ge(*done(s[f"pt_pe{c}"], k + (b - 2)))
                        dve.wait_ge(*done(s[f"sum{c}"], k + (b - 2)))
                        dve.tensor_tensor(prob[:, b, 4 * c:4 * c + 4, :], sc,
                                          mx.rearrange("p (r o) -> p r o", o=1).broadcast_to([P, 4, P]),
                                          ALU.subtract).then_inc(s[f"sub{c}"].sem, 1)

                def sums(k, b):
                    for c in range(C):
                        dve.wait_ge(*done(s[f"exp{c}"], k + b))
                        dve.tensor_reduce(row_sum[:, b, 4 * c:4 * c + 4], prob[:, b, 4 * c:4 * c + 4, :], AX.X, ALU.add
                                          ).then_inc(s[f"sum{c}"].sem, 1)
                    for c in range(C):
                        dve.wait_ge(*done(s[f"sum{c}"], k + b))
                    dve.reciprocal(rec0[:, b, :], row_sum[:, b, :]).then_inc(s["rec"].sem, 1)

                def k_out(f, slot, pair):
                    dve.wait_ge(*done(s["ka_pe" if pair == 0 else "kb_pe"], f))
                    dve.wait_ge(*done(s["ka_out" if pair == 0 else "kb_out"], f))
                    src_bank = bank[7][:].rearrange("p (c b n) -> p c b n", c=2, b=GROUP)
                    for j in range(2):
                        c = 2 * pair + j
                        for r in range(K_ON_ACT, HC0):
                            q4 = slice(DH0 * r, DH0 * (r + 1))
                            last = dve.tensor_scalar(k_blocks[q4, slot, c, :, r, :], src_bank[q4, j],
                                                     col[q4, KB, c:c + 1], None, ALU.add)
                    last.then_inc(s["ka_out2" if pair == 0 else "kb_out2"].sem, GROUP)

                def v_add(f, slot, b):
                    dve.wait_ge(*done(s["v_pe"], f + b))
                    dve.wait_ge(*done(s["pv3" if l == 0 else "att_pe"], f + (b - 2 * GROUP)))
                    vb = bank[6]
                    dve.tensor_tensor(v_s[:, slot, b, :], vb[:], bias_wide[:, WV, :], ALU.add).then_inc(s["v_add"].sem, 1)

                def y_norm(k, kslot, b):
                    dve.wait_ge(*done(s["y_pe"], k + b))
                    dve.wait_ge(*done(s["stats2"], k + (b - 1)))
                    dve.wait_ge(*done(s["yn_full"], k + (b - 1)))
                    if l == 0:
                        dve.wait_ge(*done(s["rec"], k + b))
                        yb, h, rc = bank[6 + b], H0, rec0[:, b, :]
                    else:
                        yb, h, rc = bank[3], H1, q_rec[:, kslot, b, :]
                        dve.wait_ge(*done(s["qrec"], k + b))
                    hv = lambda ap: ap.rearrange("p (h e) -> p h e", h=h)
                    dve.tensor_tensor(hv(y_s[:]), hv(yb[:]),
                                      rc.rearrange("p (h o) -> p h o", o=1).broadcast_to([P, h, D // h]),
                                      ALU.mult).then_inc(s["y_norm"].sem, 1)
                    dve.wait_ge(*done(s["y_norm"], k + b))
                    moments(1, b, y_s[:], "stats2", "aggr2", k + b)

                def film_scale(k, b):
                    dve.wait_ge(*done(s["h_pe"], k + b))
                    dve.wait_ge(*done(s["z_full"], k + (b - 1)))
                    dve.tensor_tensor(chunks(z_a[:]), chunks(bank[7 if l == 0 else 4][:]), film_of(film_a, k + b), ALU.mult
                                      ).then_inc(s["z_a_full"].sem, 1)

                def silu(k, b):
                    dve.wait_ge(*done(s["tanh_full"], k + b))
                    dve.wait_ge(*done(s["s_high"], k + (b - 1)))
                    dve.wait_ge(*done(s["s_low"], k + (b - 1)))
                    dve.scalar_tensor_tensor(out=s_s[:], in0=th[:], scalar=1.0, in1=z_s[:, b, :],
                                             op0=ALU.add, op1=ALU.mult).then_inc(s["s_full"].sem, 1)

                def s_low_part(k, b):
                    dve.wait_ge(*done(s["s_high"], k + b))
                    dve.wait_ge(*done(s["o_pe"], k + (b - 2)))
                    dve.tensor_tensor(s_lo[:, b, :], s_s[:], s_hi[:, b, :].bitcast(F32), ALU.subtract
                                      ).then_inc(s["s_low"].sem, 1)

                def output(k, b):
                    dve.wait_ge(*done(s["o_pe"], k + b))
                    dve.wait_ge(*done(s["res_full"], k + b))
                    dve.tensor_tensor(x_out[:, b, :], bank[6 + b if l == 0 else 5][:], x_res[:, b, :], ALU.add
                                      ).then_inc(s["o_out"].sem, 1)

                def k_soft(f, slot, pair):
                    dve.wait_ge(*done(s[f"kbias{pair}"], f))
                    kt = k_tmp[:, pair, :].rearrange("p (g n) -> p g n", n=P)
                    km = k_max[:, pair, :]
                    dve.tensor_reduce(km, kt, AX.X, ALU.max).then_inc(s[f"kmax{pair}"].sem, GROUP)
                    dve.wait_ge(*done(s[f"kmax{pair}"], f))
                    dve.wait_ge(*done(s["kt_pe"], f + (-GROUP - 1)))
                    dve.wait_ge(*done(s[f"ksum{pair}"], f + (-2 * GROUP)))
                    dve.tensor_tensor(k_exp[:, slot, pair * D:(pair + 1) * D].rearrange("p (g n) -> p g n", n=P), kt,
                                      km.rearrange("p (g o) -> p g o", o=1).broadcast_to([P, 2 * GROUP, P]),
                                      ALU.subtract).then_inc(s[f"ksub{pair}"].sem, GROUP)

                def k_sums(f, slot):
                    for pair in range(2):
                        dve.wait_ge(*done(s[f"kexp{pair}"], f))
                        dve.tensor_reduce(k_sum[:, slot, pair, :],
                                          k_exp[:, slot, pair * D:(pair + 1) * D].rearrange("p (g n) -> p g n", n=P),
                                          AX.X, ALU.add).then_inc(s[f"ksum{pair}"].sem, GROUP)
                    for pair in range(2):
                        dve.wait_ge(*done(s[f"ksum{pair}"], f))
                    dve.wait_ge(*done(s["att_out"], f + (-GROUP - 1)))
                    dve.reciprocal(k_rec[:, slot].rearrange("p a g -> p (a g)"),
                                   k_sum[:, slot].rearrange("p a g -> p (a g)")).then_inc(s["krec"].sem, GROUP)

                def q_soft(f, slot, b):
                    dve.wait_ge(*done(s["q_pe"], f + b))
                    dve.wait_ge(*done(s["qsub"], f + (b - 1)))
                    dve.tensor_tensor(q_tmp, bank[7][:], bias_wide[:, WQ, :], ALU.add).then_inc(s["q_add"].sem, 1)
                    dve.wait_ge(*done(s["q_add"], f + b))
                    qv = q_tmp.rearrange("p (h e) -> p h e", h=H1)
                    dve.tensor_reduce(q_max[:], qv, AX.X, ALU.max).then_inc(s["qmax"].sem, 1)
                    dve.wait_ge(*done(s["qmax"], f + b))
                    dve.wait_ge(*done(s["qt_pe"], f + (b - 2 * GROUP)))
                    dve.wait_ge(*done(s["qsum"], f + (b - 2 * GROUP)))
                    dve.tensor_tensor(q_exp[:, slot, b, :].rearrange("p (h e) -> p h e", h=H1), qv,
                                      q_max[:].rearrange("p (h o) -> p h o", o=1).broadcast_to([P, H1, DH1]),
                                      ALU.subtract).then_inc(s["qsub"].sem, 1)

                def q_sums(f, slot, b):
                    dve.wait_ge(*done(s["qexp"], f + b))
                    dve.wait_ge(*done(s["qrec"], f + (b - 1)))
                    dve.tensor_reduce(q_sum[:], q_exp[:, slot, b, :].rearrange("p (h e) -> p h e", h=H1), AX.X, ALU.add
                                      ).then_inc(s["qsum"].sem, 1)
                    dve.wait_ge(*done(s["qsum"], f + b))
                    dve.wait_ge(*done(s["y_norm"], f + (b - 2 * GROUP)))
                    dve.reciprocal(q_rec[:, slot, b, :], q_sum[:]).then_inc(s["qrec"].sem, 1)

                def kv_out(k, kslot, b):
                    dve.wait_ge(*done(s["att_pe"], k + b))
                    dve.wait_ge(*done(s["y_pe"], k + (b - 1)))
                    dve.wait_ge(*done(s["krec"], k))
                    for h in range(2):
                        q2 = slice(DH1 * h, DH1 * (h + 1))
                        rc = k_rec[q2, kslot].rearrange("p a (j g) -> p (a j) g", g=GROUP)[:, :, b:b + 1]
                        last = dve.tensor_tensor(chunks(kv_blocks)[q2, :, q2], chunks(bank[2][:])[q2, :, q2],
                                                 rc.broadcast_to([DH1, C, DH1]), ALU.mult)
                    last.then_inc(s["att_out"].sem, 1)

                def step0(f, fslot, k, kslot):
                    if f:
                        stats1(f, 0)
                        stats1(f, 1)
                    if k:
                        softmax(k, 0)
                    if f:
                        xt_low(f, fslot, 0)
                        xt_low(f, fslot, 1)
                    if k:
                        sums(k, 0)
                        softmax(k, 1)
                    if f:
                        k_out(f, fslot, 0)
                    if k:
                        y_norm(k, kslot, 0)
                    if f:
                        k_out(f, fslot, 1)
                    if k:
                        sums(k, 1)
                        film_scale(k, 0)
                    if f:
                        v_add(f, fslot, 0)
                    if k:
                        silu(k, 0)
                        s_low_part(k, 0)
                        y_norm(k, kslot, 1)
                        output(k, 0)
                        film_scale(k, 1)
                    if f:
                        v_add(f, fslot, 1)
                    if k:
                        silu(k, 1)
                        s_low_part(k, 1)
                        output(k, 1)

                def step1(f, fslot, k, kslot):
                    if f:
                        stats1(f, 0)
                        stats1(f, 1)
                        xt_low(f, fslot, 0)
                        xt_low(f, fslot, 1)
                    if k:
                        kv_out(k, kslot, 0)
                    if f:
                        k_soft(f, fslot, 0)
                    if k:
                        y_norm(k, kslot, 0)
                    if f:
                        k_soft(f, fslot, 1)
                    if k:
                        film_scale(k, 0)
                    if f:
                        k_sums(f, fslot)
                        v_add(f, fslot, 0)
                    if k:
                        kv_out(k, kslot, 1)
                        silu(k, 0)
                        s_low_part(k, 0)
                    if f:
                        q_soft(f, fslot, 0)
                    if k:
                        y_norm(k, kslot, 1)
                        output(k, 0)
                    if f:
                        v_add(f, fslot, 1)
                    if k:
                        film_scale(k, 1)
                    if f:
                        q_sums(f, fslot, 0)
                        q_soft(f, fslot, 1)
                    if k:
                        silu(k, 1)
                        s_low_part(k, 1)
                    if f:
                        q_sums(f, fslot, 1)
                    if k:
                        output(k, 1)

                st = step0 if l == 0 else step1
                program(dve, l, lambda f, sl: st(f, sl, None, None), st, lambda k, sl: st(None, None, k, sl))
                if l == 0:
                    dve.wait_ge(*done(s["o_out"], At(None, B - 1)))
                    dve.drain().then_inc(finished[0], 1)

        @block.tensor
        def _(pe):
            pe.wait_ge(consts, 1)
            pe.wait_ge(cond_dve, 2)
            for k in range(KE):
                last = pe.transpose(bank[0][:, k * B:(k + 1) * B],
                                    z_s[0:B].rearrange("p a n -> p (a n)")[:, k * P:(k + 1) * P], ident[0:B, 0:B])
            last.then_inc(cond_pe, 1)
            pe.wait_ge(cond_dve, 3)
            for l, L in enumerate(layers):
                s = S[l]
                if l == 1:
                    pe.wait_ge(finished[0], 4)
                pe.wait_ge(*upto(s["mask_in"], 16))
                pe.transpose(bank[5][:, 0:B], mask_rows[:], ident[0:B, 0:B]).then_inc(s["mask_pe"].sem, 1)
                pe.wait_ge(*upto(s["beta_wide"], 1))
                for j in range(3):
                    pe.wait_ge(*upto(s[f"w_in{j}"], 16))
                    for c in range(C):
                        last = pe.matmul(bank[j][:], norm_b_wide[:, c, :], w_raw[:, j, c, :], start=(c == 0), stop=(c == C - 1))
                    last.then_inc(s["bias_pe"].sem, 1)
                for j in range(2):
                    pe.wait_ge(*upto(s["bias_dve"], j + 1))
                    for c in range(C):
                        last = pe.transpose(bank[3 + j][:, c * P:(c + 1) * P], bias_wide[:, j, c * P:(c + 1) * P], ident[:])
                    last.then_inc(s["tr_pe"].sem, 1)
                for k in range(KE):
                    pe.wait_ge(*upto(s[f"emb_in{k % 4}"], 16 * (k // 4 + 1)))
                    for h in range(2):
                        last = pe.matmul(bank[6 + h][0:B, :], silu_cond[:, k, :], emb_ring[:, k % 4, h * D:(h + 1) * D],
                                         start=(k == 0), stop=(k == KE - 1))
                    last.then_inc(s["emb_pe"].sem, 1)
                pe.wait_ge(*upto(s["emb_dve"], 2))
                pe.wait_ge(*upto(s["bias_dve"], 3))
                for k in range(2 * C):
                    last = pe.transpose(bank[0][:, k * B:(k + 1) * B],
                                        yn[0:B].rearrange("p a n -> p (a n)")[:, k * P:(k + 1) * P], ident[0:B, 0:B])
                last.then_inc(s["film_pe"].sem, 1)
                pe.wait_ge(*upto(s["mask_moved"], 48))
                pe.drain().then_inc(s["ready_pe"].sem, 1)
                for n in ("ready_dve", "ready_act", "ready_pool"):
                    pe.wait_ge(*upto(s[n], 1))

                before = {}

                def claim(b, *readers):
                    for sm, at in before.get(b, ()):
                        pe.wait_ge(*done(s[sm], at))
                    before[b] = readers

                def turn(f, b):
                    claim(6 + b, ("xt_low", f + b))
                    pe.wait_ge(*done(s["xn_full"], f + b))
                    for c in range(C):
                        last = pe.transpose(bank[6 + b][:, c * P:(c + 1) * P], xn[:, b, c * P:(c + 1) * P], ident[:])
                    last.then_inc(s["xn_turned"].sem, 1)

                def three(o, hi, lo, w_h, w_l, first, stop):
                    pe.matmul(o, hi, w_h, start=first, stop=False)
                    pe.matmul(o, hi, w_l, start=False, stop=False)
                    return pe.matmul(o, lo, w_h, start=False, stop=stop)

                def project(f, slot, w, pair, bk, sm, readers, masked=False):
                    claim(bk, *readers)
                    pe.wait_ge(*done(s["xt_low"], f + (GROUP - 1)))
                    for j in range(2):
                        c = 2 * pair + j
                        o = bank[bk][:, j * N:(j + 1) * N]
                        if masked:
                            cols = (mask_wide[:, f.const * P:f.const * P + N] if f.reg is None
                                    else mask_wide[:, bass.ds(f.value() * P, N)])
                            pe.matmul(o, ones_parts[:], cols, start=True, stop=False)
                        for kc in range(C):
                            last = three(o, w_hi[:, w, kc, c * P:(c + 1) * P], w_lo[:, w, kc, c * P:(c + 1) * P],
                                         xt_hi[:, slot, kc, :], xt_lo[:, slot, kc, :],
                                         kc == 0 and not masked, kc == C - 1)
                    last.then_inc(s[sm].sem, GROUP)

                def project_rows(f, slot, b, w, bk, sm, reader):
                    claim(bk, reader)
                    for kc in range(C):
                        last = three(bank[bk][:], xt_hi[:, slot, kc, b * P:(b + 1) * P], xt_lo[:, slot, kc, b * P:(b + 1) * P],
                                     w_hi[:, w, kc, :], w_lo[:, w, kc, :], kc == 0, kc == C - 1)
                    last.then_inc(s[sm].sem, 1)

                def values(f, slot, b):
                    project_rows(f, slot, b, WV, 6, "v_pe", ("v_add", f + b))

                def scores(k, kslot, b):
                    qv = q_t[:, kslot, :].rearrange("p (c n) -> p c n", c=C)
                    if b == 0:
                        for n in ("pa_out", "pb_out", "ka_out", "kb_out", "ka_out2", "kb_out2"):
                            pe.wait_ge(*done(s[n], k))
                    for c in range(C):
                        pe.wait_ge(*done(s[f"sub{c}"], k + (b - 1)))
                        o = bank[c][:].rearrange("p (r n) -> p r n", r=HC0)
                        mrow = batch_cols(mask_wide, k + b, P).rearrange("p (o n) -> p o n", o=1).broadcast_to([P, HC0, P])
                        pe.matmul(o, ones_parts[:], mrow, start=True, stop=False)
                        pe.matmul(o, qv[:, c, b * P:(b + 1) * P], k_blocks[:, kslot, c, b], start=False, stop=True
                                  ).then_inc(s[f"s_pe{c}"].sem, 1)

                def weigh(k, kslot, b):
                    claim(6, ("pv_out", k + b))
                    pe.wait_ge(*done(s["v_mask"], k + b))

                    def turn_probs(c):
                        pe.wait_ge(*done(s[f"exp{c}"], k + b))
                        if c >= 2:
                            pe.wait_ge(*done(s[f"pt_out{c - 2}"], k + b))
                        else:
                            pe.wait_ge(*done(s[f"pt_out{c + 2}"], k + (b - 1)))
                        for r in range(HC0):
                            last = pe.transpose(bank[4 + c % 2][:, r * P:(r + 1) * P], prob[:, b, 4 * c + r, :], ident[:])
                        last.then_inc(s[f"pt_pe{c}"].sem, 1)

                    turn_probs(0)
                    for c in range(C):
                        if c + 1 < C:
                            turn_probs(c + 1)
                        pe.wait_ge(*done(s[f"pt_out{c}"], k + b))
                        for r in range(HC0):
                            h = HC0 * c + r
                            last = pe.matmul(bank[6][DH0 * r:DH0 * (r + 1), c * P:(c + 1) * P],
                                             v_s[:, kslot, b, h * DH0:(h + 1) * DH0], prob_t[:, c % 2, r * P:(r + 1) * P],
                                             start=True, stop=True, tile_position=(0, DH0 * r))
                        last.then_inc(s[f"pv{c}"].sem, 1)

                def y_rows(k, b):
                    bk = 6 + b
                    claim(bk, ("stats2", k + b))
                    pe.wait_ge(*done(s["pv_out"], k + b))
                    for c in range(C):
                        last = pe.transpose(bank[bk][:, c * P:(c + 1) * P], y_t[:, c * P:(c + 1) * P], ident[:])
                    last.then_inc(s["y_pe"].sem, 1)

                def turn_yn(k, b):
                    bk = 7 if l == 0 else 4
                    claim(bk, ("z_a_full", k + b))
                    pe.wait_ge(*done(s["yn_full"], k + b))
                    for c in range(C):
                        last = pe.transpose(bank[bk][:, c * P:(c + 1) * P], yn[:, b, c * P:(c + 1) * P], ident[:])
                    last.then_inc(s["h_pe"].sem, 1)

                def output(k, b):
                    bk = 6 + b if l == 0 else 5
                    claim(bk, ("o_out", k + b))
                    pe.wait_ge(*done(s["s_low"], k + b))
                    for kc in range(C):
                        last = three(bank[bk][:], s_hi[:, b, kc * P:(kc + 1) * P], s_lo[:, b, kc * P:(kc + 1) * P],
                                     w_hi[:, WO, kc, :], w_lo[:, WO, kc, :], kc == 0, kc == C - 1)
                    last.then_inc(s["o_pe"].sem, 1)

                def turn_k(k, kslot, b):
                    claim(0, ("kt_out", k + b))
                    for pair in range(2):
                        pe.wait_ge(*done(s[f"kexp{pair}"], k))
                    kv = k_exp[:, kslot, :].rearrange("p (c g n) -> p c g n", c=C, g=GROUP)
                    for c in range(C):
                        last = pe.transpose(bank[0][:, c * P:(c + 1) * P], kv[:, c, b, :], ident[:])
                    last.then_inc(s["kt_pe"].sem, 1)

                def turn_q(k, kslot, b):
                    claim(1, ("qt_out", k + b))
                    pe.wait_ge(*done(s["qexp"], k + b))
                    for c in range(C):
                        last = pe.transpose(bank[1][:, c * P:(c + 1) * P], q_exp[:, kslot, b, c * P:(c + 1) * P], ident[:])
                    last.then_inc(s["qt_pe"].sem, 1)

                def keys_values(k, kslot, b):
                    claim(2, ("att_out", k + b))
                    pe.wait_ge(*done(s["kt_out"], k + b))
                    pe.wait_ge(*done(s["v_mask"], k + b))
                    for c in range(C):
                        last = pe.matmul(bank[2][:, c * P:(c + 1) * P], k_tok[:, c * P:(c + 1) * P],
                                         v_s[:, kslot, b, c * P:(c + 1) * P], start=True, stop=True)
                    last.then_inc(s["att_pe"].sem, 1)

                def query(k, b):
                    claim(3, ("y_norm", k + b))
                    pe.wait_ge(*done(s["att_out"], k + b))
                    pe.wait_ge(*done(s["qt_out"], k + b))
                    for c in range(C):
                        last = pe.matmul(bank[3][:, c * P:(c + 1) * P], q_feat[:, c * P:(c + 1) * P],
                                         kv_blocks[:, c * P:(c + 1) * P], start=True, stop=True)
                    last.then_inc(s["y_pe"].sem, 1)

                def step0(f, fslot, k, kslot):
                    if k:
                        scores(k, kslot, 0)
                    if f:
                        turn(f, 0)
                        turn(f, 1)
                        project(f, fslot, WQ, 0, 6, "pa_pe", [("pa_out", f)])
                        project(f, fslot, WQ, 1, 7, "pb_pe", [("pb_out", f)])
                    if k:
                        scores(k, kslot, 1)
                        weigh(k, kslot, 0)
                    if f:
                        project(f, fslot, WK, 0, 7, "ka_pe", [("ka_out", f), ("ka_out2", f)])
                    if k:
                        y_rows(k, 0)
                    if f:
                        project(f, fslot, WK, 1, 7, "kb_pe", [("kb_out", f), ("kb_out2", f)])
                    if k:
                        weigh(k, kslot, 1)
                        turn_yn(k, 0)
                    if f:
                        values(f, fslot, 0)
                    if k:
                        y_rows(k, 1)
                        output(k, 0)
                        turn_yn(k, 1)
                    if f:
                        values(f, fslot, 1)
                    if k:
                        output(k, 1)

                def step1(f, fslot, k, kslot):
                    if k:
                        turn_k(k, kslot, 0)
                        turn_q(k, kslot, 0)
                    if f:
                        turn(f, 0)
                        turn(f, 1)
                    if k:
                        keys_values(k, kslot, 0)
                    if f:
                        project(f, fslot, WK, 0, 6, "ka_pe", [("kbias0", f)], True)
                    if k:
                        query(k, 0)
                    if f:
                        project(f, fslot, WK, 1, 7, "kb_pe", [("kbias1", f)], True)
                    if k:
                        turn_k(k, kslot, 1)
                        turn_q(k, kslot, 1)
                        turn_yn(k, 0)
                    if f:
                        values(f, fslot, 0)
                    if k:
                        keys_values(k, kslot, 1)
                    if f:
                        project_rows(f, fslot, 0, WQ, 7, "q_pe", ("q_add", f))
                    if k:
                        query(k, 1)
                        output(k, 0)
                    if f:
                        values(f, fslot, 1)
                    if k:
                        turn_yn(k, 1)
                    if f:
                        project_rows(f, fslot, 1, WQ, 7, "q_pe", ("q_add", f + 1))
                    if k:
                        output(k, 1)

                st = step0 if l == 0 else step1

                def front(f, sl):
                    st(f, sl, None, None)

                def step(f, fsl, k, ksl):
                    if f.reg is not None and fsl == 0:
                        for b, readers in before.items():
                            before[b] = tuple((n, At(f.reg, at.const - GROUP)) for n, at in readers)
                        step.entry = dict(before)
                    st(f, fsl, k, ksl)

                def back(k, sl):
                    for b, readers in before.items():
                        before[b] = tuple((n, At(None, at.const + B - 3 * GROUP)) for n, at in readers)
                    st(None, None, k, sl)

                program(pe, l, front, step, back)
                if l == 0:
                    pe.drain().then_inc(finished[0], 1)


_OUT = ((32, 128, 512), 'float32')


def kernel(**inputs):
    import numpy as _np
    import concourse.bacc as _bacc
    from concourse import mybir as _mybir
    from concourse.bass_utils import run_bass_kernel_spmd as _run

    nc = _bacc.Bacc("TRN2", target_bir_lowering=False, num_devices=1)
    arrays, args = {}, {}
    for name, value in inputs.items():
        a = _np.ascontiguousarray(value)
        arrays[f"in_{name}_dram"] = a
        args[name] = nc.dram_tensor(f"in_{name}_dram", a.shape, _mybir.dt.from_np(a.dtype), kind="ExternalInput").ap()
    out = nc.dram_tensor("out_0_dram", _OUT[0], _mybir.dt.from_np(_np.dtype(_OUT[1])), kind="ExternalOutput").ap()
    build(nc, args, out)
    r = _run(nc, [arrays], core_ids=[0])
    return r.results[0]["out_0_dram"]
```

```python
from contextlib import ExitStack

import concourse.bass as bass
from concourse import mybir

F32 = mybir.dt.float32
F32R = mybir.dt.float32r
BF16 = mybir.dt.bfloat16
ALU = mybir.AluOpType
ACT = mybir.ActivationFunctionType
AX = mybir.AxisListType

P = 128
GROUP = 2
EPS = 1e-5
MASKED = -1000000.0
PART_ROWS = (0, 32, 64)


class At:

    def __init__(self, reg, const):
        self.reg, self.const = reg, const

    def __add__(self, n):
        return At(self.reg, self.const + n)

    def value(self):
        return self.const if self.reg is None else self.reg + self.const


class Stage:

    always = None

    def __init__(self, sem, earlier):
        self.sem, self.earlier = sem, earlier


def done(stage, at):
    if at.reg is None and at.const < 0:
        return stage.always
    return stage.sem, (at + (1 + stage.earlier)).value()


def landed(stage, group, slot=0):
    if group.reg is None and group.const < 0:
        return stage[slot].always
    return stage[slot].sem, (group + stage[slot].earlier).value() * (16 // GROUP) + 16


def upto(stage, value):
    return stage.sem, stage.earlier + value


def build(nc, t, out):
    B, T, D = t["x"].shape
    TE = t["cond_2048"].shape[1]
    C = D // P
    KE = TE // P
    N = GROUP * P
    assert T == P and B % (2 * GROUP) == 0
    layers = [
        dict(H=16, nw=t["L0_cond_norm_w"], nb=t["L0_cond_norm_b"],
             W=[t["L0_cond_q_w"], t["L0_cond_k_w"], t["L0_cond_v_w"], t["L0_cond_out_w"]],
             b=[t["L0_cond_q_b"], t["L0_cond_k_b"], t["L0_cond_v_b"], t["L0_cond_out_b"]],
             ew=t["L0_cond_emb_w"], eb=t["L0_cond_emb_b"], w2=t["L0_cond_sb_norm_w"], b2=t["L0_cond_sb_norm_b"],
             mask=t["mask_BxS_ff1"]),
        dict(H=8, nw=t["L1_cond_ln_w"], nb=t["L1_cond_ln_b"],
             W=[t["L1_cond_Wq"], t["L1_cond_Wk"], t["L1_cond_Wv"], t["L1_cond_W_out"]],
             b=[t["L1_cond_bq"], t["L1_cond_bk"], t["L1_cond_bv"], t["L1_cond_b_out"]],
             ew=t["L1_cond_W_emb"], eb=t["L1_cond_b_emb"], w2=t["L1_cond_ln2_w"], b2=t["L1_cond_ln2_b"],
             mask=t["mask_BxSx1_fk1"].rearrange("b s o -> b (s o)")),
    ]
    H0, H1 = layers[0]["H"], layers[1]["H"]
    DH0, DH1 = D // H0, D // H1
    HC0 = P // DH0
    WQ, WK, WV, WO = range(4)

    middle = nc.dram_tensor("between_layers", [B, T, D], F32, kind="Internal").ap()

    with ExitStack() as ctx:
        def sb(name, shape, dt=F32):
            return ctx.enter_context(nc.sbuf_tensor(name, shape, dt))

        def sem(name):
            return ctx.enter_context(nc.semaphore(name))

        w_hi = sb("w_hi", [P, 4, C, D], F32R)
        w_lo = sb("w_lo", [P, 4, C, D], F32R)
        k_blocks = sb("k_blocks", [P, 2, C, GROUP, HC0, P])
        w_raw = k_blocks[:].rearrange("p a b c d e -> p (a b c d e)").rearrange("p (w c n) -> p w c n", w=4, c=C)
        col = sb("col", [P, 6, C])
        NW, NBI, W2, B2, QB, KB = range(6)
        bias_wide = sb("bias_wide", [P, 4, D])
        film_a = sb("film_a", [P, C, B])
        film_b = sb("film_b", [P, C, B])
        silu_cond = sb("silu_cond", [P, KE, B])
        mask_rows = sb("mask_rows", [B, P])
        mask_parts = sb("mask_parts", [B, 3, P], BF16)
        mask_tmp = sb("mask_tmp", [B, 2, P])
        mask_wide = sb("mask_wide", [P, B * P], BF16)
        ones_parts = sb("ones_parts", [P, P], BF16)
        mask_col = sb("mask_col", [P, B])
        mask_now = sb("mask_now", [P, 1])
        ident = sb("ident", [P, P])
        minus_half = sb("minus_half", [P, 1])
        x_in = sb("x_in", [P, 2, D])
        xn = sb("xn", [P, 2, D])
        stat = sb("stat", [P, 2, 2, 16])
        xt_hi = sb("xt_hi", [P, 2, C, N], F32R)
        xt_lo = sb("xt_lo", [P, 2, C, N], F32R)
        q_t = sb("q_t", [P, 2, C * N])
        v_s = sb("v_s", [P, 2, GROUP, D])
        prob = sb("prob", [P, 2, H0, P])
        emb_ring = prob[:].rearrange("p a h n -> p (a h n)").rearrange("p (k n) -> p k n", k=4)
        prob_t = sb("prob_t", [P, 2, D])
        row_max = sb("row_max", [P, 2, H0])
        row_sum = sb("row_sum", [P, 2, H0])
        y_t = sb("y_t", [P, D])
        norm_b_wide = y_t[:].rearrange("p (c n) -> p c n", c=C)
        y_s = sb("y_s", [P, D])
        yn = sb("yn", [P, 2, D])
        z_a = sb("z_a", [P, D])
        z_s = sb("z_s", [P, 2, D])
        th = sb("th", [P, D])
        s_s = th
        s_hi = sb("s_hi", [P, 2, D], F32R)
        s_lo = sb("s_lo", [P, 2, D], F32R)
        x_res = sb("x_res", [P, 2, D])
        x_out = x_res

        bank = [ctx.enter_context(nc.psum_tensor(f"bank{i}", [P, D], F32)) for i in range(8)]

        BANKS = [dict(X=(4, 5), Q=(6, 2), K=(0, 1), V=(3, 4), PV=(6, 7), Y=(2, 0), H=(6, 6), O=(7, 7)),
                 dict(X=(0, 1), K=(6, 7), V=(0, 6), Q=(2, 4), KT=(0, 2), QT=(1, 3), KV=(4, 4), Y=(5, 1), H=(3, 7), O=(5, 6))]

        def chunks(ap):
            return ap.rearrange("p (c n) -> p c n", c=C)

        k_exp = q_t
        q_exp = k_blocks[:, 0].rearrange("p a b c d -> p (a b c d)")[:, 0:2 * GROUP * D] \
            .rearrange("p (s b d) -> p s b d", s=2, b=GROUP)
        k_tmp = k_blocks[:, 1].rearrange("p a b c d -> p (a b c d)")[:, 0:2 * D].rearrange("p (s d) -> p s d", s=2)
        q_tmp = k_blocks[:, 1].rearrange("p a b c d -> p (a b c d)")[:, 2 * D:3 * D]
        per_seq = prob[:].rearrange("p a h n -> p (a h n)").rearrange("p (j d) -> p j d", d=D)
        k_tok = [per_seq[:, b, :] for b in range(GROUP)]
        q_feat = [per_seq[:, GROUP + b, :] for b in range(GROUP)]
        kv_blocks = [per_seq[:, 2 * GROUP + b, :] for b in range(GROUP)]
        k_max = sb("k_max", [P, 2, 2 * GROUP])
        k_sum = sb("k_sum", [P, 2, 2, 2 * GROUP])
        k_rec = sb("k_rec", [P, 2, 2, 2 * GROUP])
        q_max = sb("q_max", [P, H1])
        q_sum = sb("q_sum", [P, H1])
        q_rec = sb("q_rec", [P, 2, GROUP, H1])
        rec0 = sb("rec0", [P, 2, H0])

        once = sem("once")
        consts = sem("consts")
        Stage.always = (consts, 1)
        cond_in = sem("cond_in")
        cond_dve = sem("cond_dve")
        cond_act = sem("cond_act")
        cond_pe = sem("cond_pe")
        finished = [sem(f"layer{l}_finished") for l in range(2)]

        def stages(names, earlier=0):
            return {n: Stage(sem(n), earlier) for n in names.split()}

        def counted_on(these, earlier):
            return {n: Stage(v.sem, earlier) for n, v in these.items()}

        SETUP = dict(par_in=16 * 9, mask_in=16, mask_moved=16 * len(PART_ROWS), mask_dve=6, mask_pe=1, mask_col_ready=1,
                     beta_wide=1, bias_pe=3, bias_dve=3, scaled=4, w_high=4, w_split=4, raw_free=1, zeroed=1,
                     tr_pe=2, tr_dve=2, emb_pe=KE, emb_dve=2, film_pe=1, film_dve=4,
                     ready_dve=1, ready_act=1, ready_pool=1, ready_pe=1)
        SETUP |= {f"w_in{j}": 16 for j in range(4)} | {f"emb_in{k}": 16 * KE // 4 for k in range(4)}
        STAGES = ("stats aggr rstd_a rstd_b neg_mean xn_full xn_turned xt_high xt_low "
                  "pa_pe pb_pe pa_out pb_out ka_pe kb_pe ka_out kb_out v_pe v_add v_mask mask_now "
                  "y_norm stats2 aggr2 rstd2_a rstd2_b neg_mean2 yn_full h_pe z_a_full z_full tanh_full s_full "
                  "s_high s_low o_pe o_out res_full y_pe")
        only0 = ("s_pe0 s_pe1 s_pe2 s_pe3 smax0 smax1 smax2 smax3 sub0 sub1 sub2 sub3 exp0 exp1 exp2 exp3 "
                 "sum0 sum1 sum2 sum3 rec pt_pe0 pt_pe1 pt_pe2 pt_pe3 pt_out0 pt_out1 pt_out2 pt_out3 pv0 pv1 pv2 pv3 "
                 "pv_out")
        only1 = ("kt_pe qt_pe kt_out qt_out att_pe att_out kbias0 kbias1 kmax0 kmax1 ksub0 ksub1 kexp0 kexp1 ksum0 ksum1 krec "
                 "q_pe q_add qmax qsub qexp qsum qrec")
        both = stages(STAGES)
        moved = {n: [sem(f"{n}{b}") for b in range(GROUP)] for n in ("x_in_full", "res_in", "stored")}
        setup = [{n: Stage(sem(n), 0) for n in SETUP}]
        setup.append({n: Stage(v.sem, SETUP[n]) for n, v in setup[0].items()})
        S = [setup[0] | both | stages(only0), setup[1] | counted_on(both, B) | stages(only1)]
        for l in range(2):
            S[l] |= {n: [Stage(v, B * l) for v in places] for n, places in moved.items()}

        src = [t["x"], middle]
        dst = [middle, out]

        def program(eng, step, claims=None):
            first, last = GROUP, B - 5 * GROUP

            def recount(reg, shift):
                if claims is not None:
                    for b, readers in claims.items():
                        claims[b] = tuple((n, At(reg, at.const + shift)) for n, at in readers)

            def at(c):
                return At(None, c * GROUP)

            step(at(0), None, None, None, 1)
            step(at(1), at(0), None, None, 0)
            step(at(2), at(1), at(0), None, 1)
            with eng.Fori(first, last + 1, 2 * GROUP) as k:
                recount(k, -first)
                step(At(k, 2 * GROUP), At(k, GROUP), At(k, 0), At(k, -1), 0)
                step(At(k, 3 * GROUP), At(k, 2 * GROUP), At(k, GROUP), At(k, GROUP - 1), 1)
            recount(None, last)
            G = B // GROUP
            step(at(G - 1), at(G - 2), at(G - 3), at(G - 3) + (-1), 0)
            step(None, at(G - 1), at(G - 2), at(G - 2) + (-1), 1)
            step(None, None, at(G - 1), at(G - 1) + (-1), 0)
            step(None, None, None, at(G) + (-1), 1)

        def sequence(dram, at):
            if at.reg is None:
                return dram[at.const]
            return dram[bass.ds(at.value(), 1)].rearrange("o t d -> (o t) d")

        def batch_cols(tile, at, width):
            if at.reg is None:
                return tile[:, at.const * width:(at.const + 1) * width]
            return tile[:, bass.ds(at.value() * width, width)]

        def film_of(tile, at):
            if at.reg is None:
                v = tile[:, :, at.const:at.const + 1]
            else:
                v = tile[:, :, bass.ds(at.value(), 1)]
            return v.broadcast_to([P, C, P])

        block = ctx.enter_context(nc.Block())

        @block.sync
        def _(sp):
            for l, L in enumerate(layers):
                s, bk = S[l], BANKS[l]
                if l == 1:
                    sp.wait_ge(finished[0], 4)
                for j, p in enumerate(("nw", "nb", "w2", "b2")):
                    sp.dma_start(col[:, j, :], L[p].rearrange("(c p) -> p c", p=P), allow_slow_non_contiguous=True
                                 ).then_inc(s["par_in"].sem, 16)
                for j in range(4):
                    sp.dma_start(w_raw[:, j], L["W"][j].rearrange("(c p) n -> p c n", p=P)).then_inc(s[f"w_in{j}"].sem, 16)
                    sp.dma_start(bias_wide[:, j, :], L["b"][j].rearrange("(o n) -> o n", o=1).broadcast_to([P, D])
                                 ).then_inc(s["par_in"].sem, 16)
                sp.dma_start(mask_rows[:], L["mask"]).then_inc(s["mask_in"].sem, 16)
                if l == 0:
                    sp.dma_start(x_in[0:B, :, :].rearrange("p a b -> p (a b)"), t["cond_2048"]).then_inc(cond_in, 16)
                sp.dma_start(x_out[0:B].rearrange("p a n -> p (a n)"),
                             L["eb"].rearrange("(o n) -> o n", o=1).broadcast_to([B, 2 * D])).then_inc(s["par_in"].sem, 16)
                for k in range(KE):
                    if k >= 4:
                        sp.wait_ge(*upto(s["emb_pe"], k - 3))
                    sp.dma_start(emb_ring[:, k % 4], L["ew"][k * P:(k + 1) * P, :]).then_inc(s[f"emb_in{k % 4}"].sem, 16)
                sp.wait_ge(*upto(s["mask_dve"], 6))
                for j, row in enumerate(PART_ROWS):
                    sp.dma_start(mask_wide[row:row + 1, :].rearrange("o (b n) -> o b n", b=B),
                                 mask_parts[:, j, :]).then_inc(s["mask_moved"].sem, 16)
                for n in ("ready_dve", "ready_act", "ready_pool", "ready_pe"):
                    sp.wait_ge(*upto(s[n], 1))

                def load_front(f):
                    for b in range(GROUP):
                        sp.wait_ge(*done(s["xn_full"], f + (b - 2)))
                        sp.wait_ge(*done(s["stats"], f + (b - 2)))
                        sp.dma_start(x_in[:, b, :], sequence(src[l], f + b)).then_inc(s["x_in_full"][b].sem, 16)

                def load_back(k):
                    for b in range(GROUP):
                        sp.wait_ge(*landed(s["stored"], k + (-GROUP), b))
                        sp.dma_start(x_res[:, b, :], sequence(src[l], k + b)).then_inc(s["res_in"][b].sem, 16)

                def store(at, b):
                    sp.wait_ge(*done(s["o_out"], at))
                    sp.dma_start(sequence(dst[l], at), x_out[:, b, :]).then_inc(s["stored"][b].sem, 16)

                def step(n, f, k, late, slot):
                    if n:
                        load_front(n)
                    if late:
                        store(late, 1)
                    if k:
                        load_back(k)
                        store(k, 0)

                program(sp, step)
                for b in range(GROUP):
                    sp.wait_ge(*landed(s["stored"], At(None, B - GROUP), b))
                if l == 0:
                    sp.wait_ge(finished[0], 4)

        @block.gpsimd
        def _(pool):
            pool.memset(ident[:], 0.0).then_inc(once, 1)
            pool.wait_ge(once, 1)
            pool.affine_select(out=ident[:], in_=ident[:], compare_op=ALU.not_equal, fill=1.0, base=0,
                               pattern=[[-1, P]], channel_multiplier=1).then_inc(once, 1)
            pool.memset(minus_half[:], -0.5).then_inc(once, 1)
            pool.memset(mask_wide[:], 0.0).then_inc(once, 1)
            pool.memset(ones_parts[:], 0.0).then_inc(once, 1)
            pool.wait_ge(once, 5)
            for r0 in PART_ROWS:
                last = pool.memset(ones_parts[r0:r0 + 1, :], 1.0)
            last.then_inc(once, 1)
            pool.wait_ge(once, 6)
            pool.memset(k_max[:], 0.0).then_inc(consts, 1)
            for l, L in enumerate(layers):
                s, bk = S[l], BANKS[l]
                if l == 1:
                    pool.wait_ge(finished[0], 4)
                pool.wait_ge(*upto(s["raw_free"], 1))
                pool.wait_ge(*upto(s["w_high"], 4))
                pool.wait_ge(*upto(s["bias_pe"], 3))
                if l == 0:
                    pool.memset(k_blocks[:], 0.0).then_inc(s["zeroed"].sem, 1)
                else:
                    pool.wait_ge(*upto(s["emb_pe"], KE))
                    pool.memset(per_seq[:, 2 * GROUP:3 * GROUP, :], 0.0).then_inc(s["zeroed"].sem, 1)
                pool.wait_ge(*upto(s["mask_col_ready"], 1))
                pool.wait_ge(*upto(s["par_in"], 16 * 9))
                pool.wait_ge(*upto(s["zeroed"], 1))
                pool.drain().then_inc(s["ready_pool"].sem, 1)
                for n in ("ready_dve", "ready_act", "ready_pe"):
                    pool.wait_ge(*upto(s[n], 1))

                def rsqrt_norm(b, which, mv, a_in, rs, nm, full, src_ap, dst_ap, at, dst_free):
                    v = stat[:, which, b, :]
                    pool.wait_ge(*done(s[mv], at))
                    pool.nop(nofuse=True)
                    pool.tensor_scalar(v[:, 8:9], v[:, 7:8], EPS, None, ALU.add).then_inc(s[a_in].sem, 1)
                    pool.tensor_scalar(v[:, 10:11], v[:, 6:7], -1.0, None, ALU.mult).then_inc(s[nm].sem, 1)
                    pool.wait_ge(*done(s[a_in], at))
                    pool.tensor_tensor(v[:, 9:10], v[:, 8:9], minus_half[:], ALU.pow).then_inc(s[rs].sem, 1)
                    pool.wait_ge(*done(s[rs], at))
                    pool.wait_ge(*done(s[nm], at))
                    for d in dst_free:
                        pool.wait_ge(*done(d, at + (-2)))
                    pool.nop(nofuse=True)
                    pool.tensor_scalar(dst_ap, src_ap, v[:, 10:11], v[:, 9:10], ALU.add, ALU.mult
                                       ).then_inc(s[full].sem, 1)

                def norm1(f, b):
                    pool.wait_ge(*landed(s["x_in_full"], f, b))
                    rsqrt_norm(b, 0, "aggr", "rstd_a", "rstd_b", "neg_mean", "xn_full",
                               x_in[:, b, :], xn[:, b, :], f + b, [s["xn_turned"]])

                def norm2(k, b):
                    rsqrt_norm(b, 1, "aggr2", "rstd2_a", "rstd2_b", "neg_mean2", "yn_full",
                               y_s[:], yn[:, b, :], k + b, [s["h_pe"]])

                def v_mask(f, slot, b):
                    pool.wait_ge(*done(s["v_mask"], f + (b - 1)))
                    pool.tensor_copy(mask_now[:], mask_at(f + b)).then_inc(s["mask_now"].sem, 1)
                    pool.wait_ge(*done(s["mask_now"], f + b))
                    pool.wait_ge(*done(s["v_add"], f + b))
                    pool.nop(nofuse=True)
                    pool.tensor_scalar(v_s[:, slot, b, :], v_s[:, slot, b, :], mask_now[:], 1.0,
                                       ALU.mult, ALU.mult).then_inc(s["v_mask"].sem, 1)

                def mask_at(at):
                    if at.reg is None:
                        return mask_col[:, at.const:at.const + 1]
                    return mask_col[:, bass.ds(at.value(), 1)]

                def add_shift(k, b):
                    pool.wait_ge(*done(s["z_a_full"], k + b))
                    pool.wait_ge(*done(s["s_full"], k + (b - 2)))
                    pool.tensor_tensor(chunks(z_s[:, b, :]), chunks(z_a[:]), film_of(film_b, k + b), ALU.add
                                       ).then_inc(s["z_full"].sem, 1)

                def residual(k, b):
                    pool.wait_ge(*landed(s["res_in"], k, b))
                    pool.tensor_tensor(x_res[:, b, :], x_res[:, b, :], bias_wide[:, WO, :], ALU.add
                                       ).then_inc(s["res_full"].sem, 1)

                def step(n, f, k, late, slot):
                    if k:
                        residual(k, 0)
                    if l == 0:
                        if n:
                            norm1(n, 0)
                            norm1(n, 1)
                        if k:
                            norm2(k, 0)
                        if f:
                            v_mask(f, slot, 0)
                        if k:
                            add_shift(k, 0)
                            norm2(k, 1)
                        if f:
                            v_mask(f, slot, 1)
                        if k:
                            add_shift(k, 1)
                            residual(k, 1)
                    else:
                        if k:
                            norm2(k, 0)
                        if f:
                            v_mask(f, slot, 0)
                        if k:
                            norm2(k, 1)
                            add_shift(k, 0)
                        if n:
                            norm1(n, 0)
                        if f:
                            v_mask(f, slot, 1)
                        if k:
                            add_shift(k, 1)
                        if n:
                            norm1(n, 1)
                        if k:
                            residual(k, 1)

                program(pool, step)
                if l == 0:
                    pool.wait_ge(*done(s["z_full"], At(None, B - 1)))
                    pool.drain().then_inc(finished[0], 1)

        @block.scalar
        def _(act):
            act.wait_ge(consts, 1)
            act.wait_ge(cond_in, 16)
            act.activation(xn[0:B].rearrange("p a n -> p (a n)"), x_in[0:B].rearrange("p a n -> p (a n)"), ACT.Tanh,
                           scale=0.5).then_inc(cond_act, 1)
            for l, L in enumerate(layers):
                s, bk = S[l], BANKS[l]
                if l == 1:
                    act.wait_ge(finished[0], 4)
                for j in range(4):
                    act.wait_ge(*upto(s["scaled"], j + 1))
                    act.activation(w_hi[:, j], w_raw[:, j], ACT.Copy).then_inc(s["w_high"].sem, 1)
                act.wait_ge(*upto(s["w_high"], 4))
                act.drain().then_inc(s["ready_act"].sem, 1)
                for n in ("ready_dve", "ready_pool", "ready_pe"):
                    act.wait_ge(*upto(s[n], 1))

                def xt_high(f, slot, b):
                    act.wait_ge(*done(s["xn_turned"], f + b))
                    act.wait_ge(*done(s["pb_pe" if l == 0 else "q_pe"], f + (-GROUP - 1)))
                    act.activation(xt_hi[:, slot, :, b * P:(b + 1) * P], chunks(bank[bk["X"][b]][:]), ACT.Copy
                                   ).then_inc(s["xt_high"].sem, 1)

                def q_out(f, slot, pair):
                    act.wait_ge(*done(s["pa_pe" if pair == 0 else "pb_pe"], f))
                    src_bank = bank[bk["Q"][pair]][:].rearrange("p (c n) -> p c n", c=2)
                    if pair == 0:
                        act.wait_ge(*done(s["s_pe3"], f + (-GROUP - 1)))
                    qv = q_t[:, slot, :].rearrange("p (c n) -> p c n", c=C)
                    for j in range(2):
                        c = 2 * pair + j
                        last = act.activation(qv[:, c, :], src_bank[:, j, :], ACT.Identity,
                                              bias=col[:, QB, c:c + 1])
                    last.then_inc(s["pa_out" if pair == 0 else "pb_out"].sem, GROUP)

                def k_out(f, slot, pair):
                    act.wait_ge(*done(s["ka_pe" if pair == 0 else "kb_pe"], f))
                    if pair == 0:
                        act.wait_ge(*done(s["s_pe3"], f + (-GROUP - 1)))
                    src_bank = bank[bk["K"][pair]][:].rearrange("p (c b n) -> p c b n", c=2, b=GROUP)
                    for j in range(2):
                        c = 2 * pair + j
                        for r in range(HC0):
                            rows = slice(DH0 * r, DH0 * (r + 1))
                            last = act.activation(k_blocks[rows, slot, c, :, r, :], src_bank[rows, j], ACT.Identity,
                                                  bias=col[rows, KB, c:c + 1])
                    last.then_inc(s["ka_out" if pair == 0 else "kb_out"].sem, GROUP)

                def exps(k, b):
                    for c in range(C):
                        act.wait_ge(*done(s[f"sub{c}"], k + b))
                        v = prob[:, b, 4 * c:4 * c + 4, :]
                        act.activation(v, v, ACT.Exp).then_inc(s[f"exp{c}"].sem, 1)

                def prob_turned(k, b, some):
                    for c in some:
                        act.wait_ge(*done(s[f"pt_pe{c}"], k + b))
                        if c >= 2:
                            act.wait_ge(*done(s[f"pv{c - 2}"], k + b))
                        else:
                            act.wait_ge(*done(s[f"pv{c + 2}"], k + (b - 1)))
                        act.activation(prob_t[:, c % 2, :], bank[4 + c % 2][:], ACT.Copy).then_inc(s[f"pt_out{c}"].sem, 1)

                def y_t_out(k, b):
                    act.wait_ge(*done(s["pv3"], k + b))
                    act.wait_ge(*done(s["y_pe"], k + (b - 1)))
                    act.activation(y_t[:], bank[bk["PV"][b]][:], ACT.Copy).then_inc(s["pv_out"].sem, 1)

                def tanh(k, b):
                    act.wait_ge(*done(s["z_full"], k + b))
                    act.wait_ge(*done(s["s_low"], k + (b - 1)))
                    act.wait_ge(*done(s["s_high"], k + (b - 1)))
                    act.activation(th[:], z_s[:, b, :], ACT.Tanh, scale=0.5).then_inc(s["tanh_full"].sem, 1)

                def s_high(k, b):
                    act.wait_ge(*done(s["s_full"], k + b))
                    act.wait_ge(*done(s["o_pe"], k + (b - 2)))
                    act.activation(s_hi[:, b, :], s_s[:], ACT.Copy).then_inc(s["s_high"].sem, 1)

                def k_bias(f, slot, pair):
                    act.wait_ge(*done(s["ka_pe" if pair == 0 else "kb_pe"], f))
                    src_bank = bank[bk["K"][pair]][:].rearrange("p (c n) -> p c n", c=2)
                    act.wait_ge(*done(s[f"ksub{pair}"], f + (-GROUP)))
                    kt = k_tmp[:, pair, :].rearrange("p (c n) -> p c n", c=2)
                    for j in range(2):
                        c = 2 * pair + j
                        last = act.activation(kt[:, j, :], src_bank[:, j, :], ACT.Identity,
                                              bias=col[:, KB, c:c + 1])
                    last.then_inc(s[f"kbias{pair}"].sem, GROUP)

                def k_exps(f, slot, pair):
                    act.wait_ge(*done(s[f"ksub{pair}"], f))
                    v = k_exp[:, slot, pair * D:(pair + 1) * D]
                    act.activation(v, v, ACT.Exp).then_inc(s[f"kexp{pair}"].sem, GROUP)

                def q_exps(f, slot, b):
                    act.wait_ge(*done(s["qsub"], f + b))
                    v = q_exp[:, slot, b, :]
                    act.activation(v, v, ACT.Exp).then_inc(s["qexp"].sem, 1)

                def kt_out(k, b):
                    act.wait_ge(*done(s["kt_pe"], k + b))
                    act.wait_ge(*done(s["att_pe"], k + (b - GROUP)))
                    act.activation(k_tok[b], bank[bk["KT"][b]][:], ACT.Copy).then_inc(s["kt_out"].sem, 1)

                def qt_out(k, b):
                    act.wait_ge(*done(s["qt_pe"], k + b))
                    act.wait_ge(*done(s["y_pe"], k + (b - GROUP)))
                    act.activation(q_feat[b], bank[bk["QT"][b]][:], ACT.Copy).then_inc(s["qt_out"].sem, 1)

                def step0(n, f, k, late, slot):
                    if k:
                        exps(k, 0)
                    if f:
                        q_out(f, slot, 0)
                    if k:
                        exps(k, 1)
                        prob_turned(k, 0, range(C))
                        y_t_out(k, 0)
                    if f:
                        k_out(f, slot, 0)
                    if k:
                        prob_turned(k, 1, range(C))
                        y_t_out(k, 1)
                    if f:
                        k_out(f, slot, 1)
                    if k:
                        tanh(k, 0)
                        s_high(k, 0)
                    if f:
                        q_out(f, slot, 1)
                    if n:
                        xt_high(n, 1 - slot, 0)
                        xt_high(n, 1 - slot, 1)
                    if k:
                        tanh(k, 1)
                        s_high(k, 1)

                def step1(n, f, k, late, slot):
                    if k:
                        kt_out(k, 0)
                        qt_out(k, 0)
                        kt_out(k, 1)
                    if f:
                        k_bias(f, slot, 0)
                        k_exps(f, slot, 0)
                    if k:
                        qt_out(k, 1)
                    if f:
                        k_bias(f, slot, 1)
                        k_exps(f, slot, 1)
                    if k:
                        tanh(k, 0)
                    if f:
                        q_exps(f, slot, 0)
                    if k:
                        s_high(k, 0)
                        tanh(k, 1)
                    if f:
                        q_exps(f, slot, 1)
                    if k:
                        s_high(k, 1)
                    if n:
                        xt_high(n, 1 - slot, 0)
                        xt_high(n, 1 - slot, 1)

                program(act, step0 if l == 0 else step1)
                if l == 0:
                    act.wait_ge(*done(s["s_high"], At(None, B - 1)))
                    act.drain().then_inc(finished[0], 1)

        @block.vector
        def _(dve):
            dve.wait_ge(consts, 1)
            flat = lambda v: v[0:B].rearrange("p a n -> p (a n)")
            dve.wait_ge(cond_act, 1)
            dve.scalar_tensor_tensor(out=flat(yn[:]), in0=flat(xn[:]), scalar=1.0, in1=flat(x_in[:]),
                                     op0=ALU.add, op1=ALU.mult).then_inc(cond_dve, 1)
            dve.wait_ge(cond_dve, 1)
            dve.tensor_scalar(flat(z_s[:]), flat(yn[:]), 0.5, None, ALU.mult).then_inc(cond_dve, 1)
            dve.wait_ge(cond_pe, 1)
            dve.tensor_copy(silu_cond[:].rearrange("p k b -> p (k b)"), bank[0][:, 0:KE * B]).then_inc(cond_dve, 1)
            for l, L in enumerate(layers):
                s, bk = S[l], BANKS[l]
                if l == 1:
                    dve.wait_ge(finished[0], 4)
                dve.wait_ge(*upto(s["mask_in"], 16))
                md = s["mask_dve"]
                dve.tensor_scalar(mask_tmp[:, 0, :], mask_rows[:], -1.0, 1.0, ALU.mult, ALU.add).then_inc(md.sem, 1)
                dve.wait_ge(*upto(md, 1))
                dve.tensor_scalar(mask_tmp[:, 1, :], mask_tmp[:, 0, :], MASKED, None, ALU.mult).then_inc(md.sem, 1)
                dve.wait_ge(*upto(md, 2))
                dve.tensor_copy(mask_parts[:, 0, :], mask_tmp[:, 1, :]).then_inc(md.sem, 1)
                dve.wait_ge(*upto(md, 3))
                dve.tensor_tensor(mask_tmp[:, 0, :], mask_tmp[:, 1, :], mask_parts[:, 0, :], ALU.subtract).then_inc(md.sem, 1)
                dve.wait_ge(*upto(md, 4))
                dve.tensor_copy(mask_parts[:, 1, :], mask_tmp[:, 0, :]).then_inc(md.sem, 1)
                dve.wait_ge(*upto(md, 5))
                dve.tensor_tensor(mask_parts[:, 2, :], mask_tmp[:, 0, :], mask_parts[:, 1, :], ALU.subtract).then_inc(md.sem, 1)
                dve.wait_ge(*upto(s["mask_pe"], 1))
                dve.tensor_copy(mask_col[:], bank[5][:, 0:B]).then_inc(s["mask_col_ready"].sem, 1)
                dve.wait_ge(*upto(s["par_in"], 16 * 9))
                dve.tensor_copy(norm_b_wide, col[:, NBI, :].rearrange("p (c o) -> p c o", o=1).broadcast_to([P, C, P])
                                ).then_inc(s["beta_wide"].sem, 1)
                for j in range(4):
                    dve.wait_ge(*upto(s[f"w_in{j}"], 16))
                    if j < 3:
                        dve.wait_ge(*upto(s["bias_pe"], j + 1))
                        dve.tensor_tensor(bias_wide[:, j, :], bias_wide[:, j, :], bank[j][:], ALU.add
                                          ).then_inc(s["bias_dve"].sem, 1)
                        for c in range(C):
                            last = dve.tensor_scalar(w_raw[:, j, c], w_raw[:, j, c], col[:, NW, c:c + 1], None, ALU.mult)
                    else:
                        last = dve.tensor_scalar(w_raw[:, j], w_raw[:, j], 0.5, None, ALU.mult)
                    last.then_inc(s["scaled"].sem, 1)
                    dve.wait_ge(*upto(s["scaled"], j + 1))
                    dve.wait_ge(*upto(s["w_high"], j + 1))
                    dve.tensor_tensor(w_lo[:, j], w_raw[:, j], w_hi[:, j].bitcast(F32), ALU.subtract
                                      ).then_inc(s["w_split"].sem, 1)
                dve.wait_ge(*upto(s["w_split"], 4))
                dve.drain().then_inc(s["raw_free"].sem, 1)
                for j in range(2):
                    dve.wait_ge(*upto(s["tr_pe"], j + 1))
                    dve.tensor_copy(col[:, QB + j, :], chunks(bank[3 + j][:])[:, :, 0]).then_inc(s["tr_dve"].sem, 1)
                e_rows = yn[0:B].rearrange("p a n -> p (a n)")
                eb_rows = x_out[0:B].rearrange("p a n -> p (a n)")
                dve.wait_ge(*upto(s["emb_pe"], KE))
                for h in range(2):
                    dve.tensor_tensor(e_rows[:, h * D:(h + 1) * D], bank[6 + h][0:B, :], eb_rows[:, h * D:(h + 1) * D],
                                      ALU.add).then_inc(s["emb_dve"].sem, 1)
                dve.wait_ge(*upto(s["film_pe"], 1))
                et = xn[:].rearrange("p a n -> p (a n)")[:, 0:2 * C * B].rearrange("p (c b) -> p c b", b=B)
                fd = s["film_dve"]
                dve.tensor_copy(et.rearrange("p c b -> p (c b)"), bank[0][:, 0:2 * C * B]).then_inc(fd.sem, 1)
                dve.wait_ge(*upto(fd, 1))
                wide = lambda i: col[:, i, :].rearrange("p (c o) -> p c o", o=1).broadcast_to([P, C, B])
                dve.scalar_tensor_tensor(out=film_a[:], in0=et[:, 0:C, :], scalar=1.0, in1=wide(W2),
                                         op0=ALU.add, op1=ALU.mult).then_inc(fd.sem, 1)
                dve.scalar_tensor_tensor(out=film_b[:], in0=et[:, 0:C, :], scalar=1.0, in1=wide(B2),
                                         op0=ALU.add, op1=ALU.mult).then_inc(fd.sem, 1)
                dve.wait_ge(*upto(fd, 3))
                dve.tensor_tensor(film_b[:], film_b[:], et[:, C:2 * C, :], ALU.add).then_inc(fd.sem, 1)
                dve.wait_ge(*upto(fd, 4))
                dve.wait_ge(*upto(s["tr_dve"], 2))
                dve.wait_ge(*upto(s["zeroed"], 1))
                dve.drain().then_inc(s["ready_dve"].sem, 1)
                for n in ("ready_pool", "ready_act", "ready_pe"):
                    dve.wait_ge(*upto(s[n], 1))

                def moments(which, b, src_ap, st, ag, at):
                    v = stat[:, which, b, :]
                    dve.bn_stats(v[:, 0:6], src_ap).then_inc(s[st].sem, 1)
                    dve.wait_ge(*done(s[st], at))
                    dve.wait_ge(*done(s["xn_full" if which == 0 else "yn_full"], at + (-2)))
                    dve.nop(nofuse=True)
                    dve.bn_aggr(v[:, 6:8], v[:, 0:6]).then_inc(s[ag].sem, 1)

                def stats1(f, b):
                    dve.wait_ge(*landed(s["x_in_full"], f, b))
                    moments(0, b, x_in[:, b, :], "stats", "aggr", f + b)

                def xt_low(f, slot, b):
                    dve.wait_ge(*done(s["xt_high"], f + b))
                    hs = xt_hi[:, slot, :, b * P:(b + 1) * P]
                    dve.tensor_tensor(xt_lo[:, slot, :, b * P:(b + 1) * P], chunks(bank[bk["X"][b]][:]), hs.bitcast(F32),
                                      ALU.subtract).then_inc(s["xt_low"].sem, 1)

                def softmax(k, b):
                    for c in range(C):
                        sc = bank[c][:].rearrange("p (r n) -> p r n", r=4)
                        mx = row_max[:, b, 4 * c:4 * c + 4]
                        dve.wait_ge(*done(s[f"s_pe{c}"], k + b))
                        dve.tensor_reduce(mx, sc, AX.X, ALU.max).then_inc(s[f"smax{c}"].sem, 1)
                        dve.wait_ge(*done(s[f"smax{c}"], k + b))
                        dve.wait_ge(*done(s[f"pt_pe{c}"], k + (b - 2)))
                        dve.wait_ge(*done(s[f"sum{c}"], k + (b - 2)))
                        dve.tensor_tensor(prob[:, b, 4 * c:4 * c + 4, :], sc,
                                          mx.rearrange("p (r o) -> p r o", o=1).broadcast_to([P, 4, P]),
                                          ALU.subtract).then_inc(s[f"sub{c}"].sem, 1)

                def sums(k, b):
                    for c in range(C):
                        dve.wait_ge(*done(s[f"exp{c}"], k + b))
                        dve.tensor_reduce(row_sum[:, b, 4 * c:4 * c + 4], prob[:, b, 4 * c:4 * c + 4, :], AX.X, ALU.add
                                          ).then_inc(s[f"sum{c}"].sem, 1)
                    for c in range(C):
                        dve.wait_ge(*done(s[f"sum{c}"], k + b))
                    dve.reciprocal(rec0[:, b, :], row_sum[:, b, :]).then_inc(s["rec"].sem, 1)

                def v_add(f, slot, b):
                    dve.wait_ge(*done(s["v_pe"], f + b))
                    dve.wait_ge(*done(s["pv3" if l == 0 else "att_pe"], f + (b - 2 * GROUP)))
                    vb = bank[bk["V"][b]]
                    dve.tensor_tensor(v_s[:, slot, b, :], vb[:], bias_wide[:, WV, :], ALU.add).then_inc(s["v_add"].sem, 1)

                def y_norm(k, kslot, b):
                    dve.wait_ge(*done(s["y_pe"], k + b))
                    dve.wait_ge(*done(s["stats2"], k + (b - 1)))
                    dve.wait_ge(*done(s["yn_full"], k + (b - 1)))
                    if l == 0:
                        dve.wait_ge(*done(s["rec"], k + b))
                        yb, h, rc = bank[bk["Y"][b]], H0, rec0[:, b, :]
                    else:
                        yb, h, rc = bank[bk["Y"][b]], H1, q_rec[:, kslot, b, :]
                        dve.wait_ge(*done(s["qrec"], k + b))
                    hv = lambda ap: ap.rearrange("p (h e) -> p h e", h=h)
                    dve.tensor_tensor(hv(y_s[:]), hv(yb[:]),
                                      rc.rearrange("p (h o) -> p h o", o=1).broadcast_to([P, h, D // h]),
                                      ALU.mult).then_inc(s["y_norm"].sem, 1)
                    dve.wait_ge(*done(s["y_norm"], k + b))
                    moments(1, b, y_s[:], "stats2", "aggr2", k + b)

                def film_scale(k, b):
                    dve.wait_ge(*done(s["h_pe"], k + b))
                    dve.wait_ge(*done(s["z_full"], k + (b - 1)))
                    dve.tensor_tensor(chunks(z_a[:]), chunks(bank[bk["H"][b]][:]), film_of(film_a, k + b), ALU.mult
                                      ).then_inc(s["z_a_full"].sem, 1)

                def silu(k, b):
                    dve.wait_ge(*done(s["tanh_full"], k + b))
                    dve.wait_ge(*done(s["s_high"], k + (b - 1)))
                    dve.wait_ge(*done(s["s_low"], k + (b - 1)))
                    dve.scalar_tensor_tensor(out=s_s[:], in0=th[:], scalar=1.0, in1=z_s[:, b, :],
                                             op0=ALU.add, op1=ALU.mult).then_inc(s["s_full"].sem, 1)

                def s_low_part(k, b):
                    dve.wait_ge(*done(s["s_high"], k + b))
                    dve.wait_ge(*done(s["o_pe"], k + (b - 2)))
                    dve.tensor_tensor(s_lo[:, b, :], s_s[:], s_hi[:, b, :].bitcast(F32), ALU.subtract
                                      ).then_inc(s["s_low"].sem, 1)

                def output(at, b):
                    dve.wait_ge(*done(s["o_pe"], at))
                    dve.wait_ge(*done(s["res_full"], at))
                    dve.tensor_tensor(x_out[:, b, :], bank[bk["O"][b]][:], x_res[:, b, :], ALU.add
                                      ).then_inc(s["o_out"].sem, 1)

                def k_soft(f, slot, pair):
                    dve.wait_ge(*done(s[f"kbias{pair}"], f))
                    kt = k_tmp[:, pair, :].rearrange("p (g n) -> p g n", n=P)
                    km = k_max[:, pair, :]
                    dve.tensor_reduce(km, kt, AX.X, ALU.max).then_inc(s[f"kmax{pair}"].sem, GROUP)
                    dve.wait_ge(*done(s[f"kmax{pair}"], f))
                    dve.wait_ge(*done(s["kt_pe"], f + (-GROUP - 1)))
                    dve.wait_ge(*done(s[f"ksum{pair}"], f + (-2 * GROUP)))
                    dve.tensor_tensor(k_exp[:, slot, pair * D:(pair + 1) * D].rearrange("p (g n) -> p g n", n=P), kt,
                                      km.rearrange("p (g o) -> p g o", o=1).broadcast_to([P, 2 * GROUP, P]),
                                      ALU.subtract).then_inc(s[f"ksub{pair}"].sem, GROUP)

                def k_sums(f, slot):
                    for pair in range(2):
                        dve.wait_ge(*done(s[f"kexp{pair}"], f))
                        dve.tensor_reduce(k_sum[:, slot, pair, :],
                                          k_exp[:, slot, pair * D:(pair + 1) * D].rearrange("p (g n) -> p g n", n=P),
                                          AX.X, ALU.add).then_inc(s[f"ksum{pair}"].sem, GROUP)
                    for pair in range(2):
                        dve.wait_ge(*done(s[f"ksum{pair}"], f))
                    dve.wait_ge(*done(s["att_out"], f + (-GROUP - 1)))
                    dve.reciprocal(k_rec[:, slot].rearrange("p a g -> p (a g)"),
                                   k_sum[:, slot].rearrange("p a g -> p (a g)")).then_inc(s["krec"].sem, GROUP)

                def q_soft(f, slot, b):
                    dve.wait_ge(*done(s["q_pe"], f + b))
                    dve.wait_ge(*done(s["qsub"], f + (b - 1)))
                    dve.tensor_tensor(q_tmp, bank[bk["Q"][b]][:], bias_wide[:, WQ, :], ALU.add).then_inc(s["q_add"].sem, 1)
                    dve.wait_ge(*done(s["q_add"], f + b))
                    qv = q_tmp.rearrange("p (h e) -> p h e", h=H1)
                    dve.tensor_reduce(q_max[:], qv, AX.X, ALU.max).then_inc(s["qmax"].sem, 1)
                    dve.wait_ge(*done(s["qmax"], f + b))
                    dve.wait_ge(*done(s["qt_pe"], f + (b - 2 * GROUP)))
                    dve.wait_ge(*done(s["qsum"], f + (b - 2 * GROUP)))
                    dve.tensor_tensor(q_exp[:, slot, b, :].rearrange("p (h e) -> p h e", h=H1), qv,
                                      q_max[:].rearrange("p (h o) -> p h o", o=1).broadcast_to([P, H1, DH1]),
                                      ALU.subtract).then_inc(s["qsub"].sem, 1)

                def q_sums(f, slot, b):
                    dve.wait_ge(*done(s["qexp"], f + b))
                    dve.wait_ge(*done(s["qrec"], f + (b - 1)))
                    dve.tensor_reduce(q_sum[:], q_exp[:, slot, b, :].rearrange("p (h e) -> p h e", h=H1), AX.X, ALU.add
                                      ).then_inc(s["qsum"].sem, 1)
                    dve.wait_ge(*done(s["qsum"], f + b))
                    dve.wait_ge(*done(s["y_norm"], f + (b - 2 * GROUP)))
                    dve.reciprocal(q_rec[:, slot, b, :], q_sum[:]).then_inc(s["qrec"].sem, 1)

                def kv_out(k, kslot, b):
                    dve.wait_ge(*done(s["att_pe"], k + b))
                    dve.wait_ge(*done(s["y_pe"], k + (b - GROUP)))
                    dve.wait_ge(*done(s["krec"], k))
                    for h in range(2):
                        q2 = slice(DH1 * h, DH1 * (h + 1))
                        rc = k_rec[q2, kslot].rearrange("p a (j g) -> p (a j) g", g=GROUP)[:, :, b:b + 1]
                        last = dve.tensor_tensor(chunks(kv_blocks[b])[q2, :, q2], chunks(bank[bk["KV"][b]][:])[q2, :, q2],
                                                 rc.broadcast_to([DH1, C, DH1]), ALU.mult)
                    last.then_inc(s["att_out"].sem, 1)

                def step0(n, f, k, late, slot):
                    if k:
                        softmax(k, 0)
                        sums(k, 0)
                    if late:
                        output(late, 1)
                    if n:
                        stats1(n, 0)
                        stats1(n, 1)
                    if k:
                        softmax(k, 1)
                        sums(k, 1)
                        y_norm(k, 1 - slot, 0)
                    if f:
                        v_add(f, slot, 0)
                    if k:
                        film_scale(k, 0)
                        y_norm(k, 1 - slot, 1)
                        silu(k, 0)
                        s_low_part(k, 0)
                    if f:
                        v_add(f, slot, 1)
                    if k:
                        output(k, 0)
                        film_scale(k, 1)
                    if n:
                        xt_low(n, 1 - slot, 0)
                        xt_low(n, 1 - slot, 1)
                    if k:
                        silu(k, 1)
                        s_low_part(k, 1)

                def step1(n, f, k, late, slot):
                    if late:
                        output(late, 1)
                    if k:
                        kv_out(k, 1 - slot, 0)
                    if f:
                        k_soft(f, slot, 0)
                    if k:
                        y_norm(k, 1 - slot, 0)
                        kv_out(k, 1 - slot, 1)
                    if f:
                        k_soft(f, slot, 1)
                        v_add(f, slot, 0)
                    if k:
                        y_norm(k, 1 - slot, 1)
                    if n:
                        stats1(n, 0)
                        stats1(n, 1)
                    if k:
                        film_scale(k, 0)
                    if f:
                        q_soft(f, slot, 0)
                        v_add(f, slot, 1)
                    if k:
                        silu(k, 0)
                        film_scale(k, 1)
                        s_low_part(k, 0)
                    if f:
                        k_sums(f, slot)
                        q_soft(f, slot, 1)
                    if k:
                        silu(k, 1)
                        s_low_part(k, 1)
                        output(k, 0)
                    if n:
                        xt_low(n, 1 - slot, 0)
                        xt_low(n, 1 - slot, 1)
                    if f:
                        q_sums(f, slot, 0)
                        q_sums(f, slot, 1)

                program(dve, step0 if l == 0 else step1)
                if l == 0:
                    dve.wait_ge(*done(s["o_out"], At(None, B - 1)))
                    dve.drain().then_inc(finished[0], 1)

        @block.tensor
        def _(pe):
            pe.wait_ge(consts, 1)
            pe.wait_ge(cond_dve, 2)
            for k in range(KE):
                last = pe.transpose(bank[0][:, k * B:(k + 1) * B],
                                    z_s[0:B].rearrange("p a n -> p (a n)")[:, k * P:(k + 1) * P], ident[0:B, 0:B])
            last.then_inc(cond_pe, 1)
            pe.wait_ge(cond_dve, 3)
            for l, L in enumerate(layers):
                s, bk = S[l], BANKS[l]
                if l == 1:
                    pe.wait_ge(finished[0], 4)
                pe.wait_ge(*upto(s["mask_in"], 16))
                pe.transpose(bank[5][:, 0:B], mask_rows[:], ident[0:B, 0:B]).then_inc(s["mask_pe"].sem, 1)
                pe.wait_ge(*upto(s["beta_wide"], 1))
                for j in range(3):
                    pe.wait_ge(*upto(s[f"w_in{j}"], 16))
                    for c in range(C):
                        last = pe.matmul(bank[j][:], norm_b_wide[:, c, :], w_raw[:, j, c, :], start=(c == 0), stop=(c == C - 1))
                    last.then_inc(s["bias_pe"].sem, 1)
                for j in range(2):
                    pe.wait_ge(*upto(s["bias_dve"], j + 1))
                    for c in range(C):
                        last = pe.transpose(bank[3 + j][:, c * P:(c + 1) * P], bias_wide[:, j, c * P:(c + 1) * P], ident[:])
                    last.then_inc(s["tr_pe"].sem, 1)
                for k in range(KE):
                    pe.wait_ge(*upto(s[f"emb_in{k % 4}"], 16 * (k // 4 + 1)))
                    for h in range(2):
                        last = pe.matmul(bank[6 + h][0:B, :], silu_cond[:, k, :], emb_ring[:, k % 4, h * D:(h + 1) * D],
                                         start=(k == 0), stop=(k == KE - 1))
                    last.then_inc(s["emb_pe"].sem, 1)
                pe.wait_ge(*upto(s["emb_dve"], 2))
                pe.wait_ge(*upto(s["bias_dve"], 3))
                for k in range(2 * C):
                    last = pe.transpose(bank[0][:, k * B:(k + 1) * B],
                                        yn[0:B].rearrange("p a n -> p (a n)")[:, k * P:(k + 1) * P], ident[0:B, 0:B])
                last.then_inc(s["film_pe"].sem, 1)
                pe.wait_ge(*upto(s["mask_moved"], 48))
                pe.drain().then_inc(s["ready_pe"].sem, 1)
                for n in ("ready_dve", "ready_act", "ready_pool"):
                    pe.wait_ge(*upto(s[n], 1))

                before = {}

                def claim(b, *readers):
                    for sm, at in before.get(b, ()):
                        pe.wait_ge(*done(s[sm], at))
                    before[b] = readers

                def turn(f, b):
                    claim(bk["X"][b], ("xt_low", f + b))
                    pe.wait_ge(*done(s["xn_full"], f + b))
                    for c in range(C):
                        last = pe.transpose(bank[bk["X"][b]][:, c * P:(c + 1) * P], xn[:, b, c * P:(c + 1) * P], ident[:])
                    last.then_inc(s["xn_turned"].sem, 1)

                def three(o, hi, lo, w_h, w_l, first, stop):
                    pe.matmul(o, hi, w_h, start=first, stop=False)
                    pe.matmul(o, hi, w_l, start=False, stop=False)
                    return pe.matmul(o, lo, w_h, start=False, stop=stop)

                def project(f, slot, w, pair, to, sm, reader, masked=False):
                    claim(to, (reader, f))
                    pe.wait_ge(*done(s["xt_low"], f + (GROUP - 1)))
                    for j in range(2):
                        c = 2 * pair + j
                        o = bank[to][:, j * N:(j + 1) * N]
                        if masked:
                            cols = (mask_wide[:, f.const * P:f.const * P + N] if f.reg is None
                                    else mask_wide[:, bass.ds(f.value() * P, N)])
                            pe.matmul(o, ones_parts[:], cols, start=True, stop=False)
                        for kc in range(C):
                            last = three(o, w_hi[:, w, kc, c * P:(c + 1) * P], w_lo[:, w, kc, c * P:(c + 1) * P],
                                         xt_hi[:, slot, kc, :], xt_lo[:, slot, kc, :],
                                         kc == 0 and not masked, kc == C - 1)
                    last.then_inc(s[sm].sem, GROUP)

                def project_rows(f, slot, b, w, to, sm, reader):
                    claim(to, (reader, f + b))
                    for kc in range(C):
                        last = three(bank[to][:], xt_hi[:, slot, kc, b * P:(b + 1) * P], xt_lo[:, slot, kc, b * P:(b + 1) * P],
                                     w_hi[:, w, kc, :], w_lo[:, w, kc, :], kc == 0, kc == C - 1)
                    last.then_inc(s[sm].sem, 1)

                def values(f, slot, b):
                    project_rows(f, slot, b, WV, bk["V"][b], "v_pe", "v_add")

                def scores(k, kslot, b):
                    qv = q_t[:, kslot, :].rearrange("p (c n) -> p c n", c=C)
                    if b == 0:
                        for n in ("pa_out", "pb_out", "ka_out", "kb_out"):
                            pe.wait_ge(*done(s[n], k))
                    for c in range(C):
                        claim(c, (f"sub{c}", k + b))
                        o = bank[c][:].rearrange("p (r n) -> p r n", r=HC0)
                        mrow = batch_cols(mask_wide, k + b, P).rearrange("p (o n) -> p o n", o=1).broadcast_to([P, HC0, P])
                        pe.matmul(o, ones_parts[:], mrow, start=True, stop=False)
                        pe.matmul(o, qv[:, c, b * P:(b + 1) * P], k_blocks[:, kslot, c, b], start=False, stop=True
                                  ).then_inc(s[f"s_pe{c}"].sem, 1)

                def turn_probs(k, b, c):
                    pe.wait_ge(*done(s[f"exp{c}"], k + b))
                    claim(4 + c % 2, (f"pt_out{c}", k + b))
                    for r in range(HC0):
                        last = pe.transpose(bank[4 + c % 2][:, r * P:(r + 1) * P], prob[:, b, 4 * c + r, :], ident[:])
                    last.then_inc(s[f"pt_pe{c}"].sem, 1)

                def weigh(k, kslot, b):
                    claim(bk["PV"][b], ("pv_out", k + b))
                    pe.wait_ge(*done(s["v_mask"], k + b))
                    for c in range(C):
                        pe.wait_ge(*done(s[f"pt_out{c}"], k + b))
                        for r in range(HC0):
                            h = HC0 * c + r
                            last = pe.matmul(bank[bk["PV"][b]][DH0 * r:DH0 * (r + 1), c * P:(c + 1) * P],
                                             v_s[:, kslot, b, h * DH0:(h + 1) * DH0], prob_t[:, c % 2, r * P:(r + 1) * P],
                                             start=True, stop=True, tile_position=(0, DH0 * r))
                        last.then_inc(s[f"pv{c}"].sem, 1)
                        if c + 2 < C:
                            turn_probs(k, b, c + 2)

                def y_rows(k, b):
                    claim(bk["Y"][b], ("y_norm", k + b))
                    pe.wait_ge(*done(s["pv_out"], k + b))
                    for c in range(C):
                        last = pe.transpose(bank[bk["Y"][b]][:, c * P:(c + 1) * P], y_t[:, c * P:(c + 1) * P], ident[:])
                    last.then_inc(s["y_pe"].sem, 1)

                def turn_yn(k, b):
                    claim(bk["H"][b], ("z_a_full", k + b))
                    pe.wait_ge(*done(s["yn_full"], k + b))
                    for c in range(C):
                        last = pe.transpose(bank[bk["H"][b]][:, c * P:(c + 1) * P], yn[:, b, c * P:(c + 1) * P], ident[:])
                    last.then_inc(s["h_pe"].sem, 1)

                def output(at, b):
                    claim(bk["O"][b], ("o_out", at))
                    pe.wait_ge(*done(s["s_low"], at))
                    for kc in range(C):
                        last = three(bank[bk["O"][b]][:], s_hi[:, b, kc * P:(kc + 1) * P], s_lo[:, b, kc * P:(kc + 1) * P],
                                     w_hi[:, WO, kc, :], w_lo[:, WO, kc, :], kc == 0, kc == C - 1)
                    last.then_inc(s["o_pe"].sem, 1)

                def turn_k(k, kslot, b):
                    claim(bk["KT"][b], ("kt_out", k + b))
                    for pair in range(2):
                        pe.wait_ge(*done(s[f"kexp{pair}"], k))
                    kv = k_exp[:, kslot, :].rearrange("p (c g n) -> p c g n", c=C, g=GROUP)
                    for c in range(C):
                        last = pe.transpose(bank[bk["KT"][b]][:, c * P:(c + 1) * P], kv[:, c, b, :], ident[:])
                    last.then_inc(s["kt_pe"].sem, 1)

                def turn_q(k, kslot, b):
                    claim(bk["QT"][b], ("qt_out", k + b))
                    pe.wait_ge(*done(s["qexp"], k + b))
                    for c in range(C):
                        last = pe.transpose(bank[bk["QT"][b]][:, c * P:(c + 1) * P], q_exp[:, kslot, b, c * P:(c + 1) * P], ident[:])
                    last.then_inc(s["qt_pe"].sem, 1)

                def keys_values(k, kslot, b):
                    claim(bk["KV"][b], ("att_out", k + b))
                    pe.wait_ge(*done(s["kt_out"], k + b))
                    pe.wait_ge(*done(s["v_mask"], k + b))
                    for c in range(C):
                        last = pe.matmul(bank[bk["KV"][b]][:, c * P:(c + 1) * P], k_tok[b][:, c * P:(c + 1) * P],
                                         v_s[:, kslot, b, c * P:(c + 1) * P], start=True, stop=True)
                    last.then_inc(s["att_pe"].sem, 1)

                def query(k, b):
                    claim(bk["Y"][b], ("y_norm", k + b))
                    pe.wait_ge(*done(s["att_out"], k + b))
                    pe.wait_ge(*done(s["qt_out"], k + b))
                    for c in range(C):
                        last = pe.matmul(bank[bk["Y"][b]][:, c * P:(c + 1) * P], q_feat[b][:, c * P:(c + 1) * P],
                                         kv_blocks[b][:, c * P:(c + 1) * P], start=True, stop=True)
                    last.then_inc(s["y_pe"].sem, 1)

                def step0(n, f, k, late, slot):
                    if k:
                        scores(k, 1 - slot, 0)
                    if late:
                        output(late, 1)
                    if f:
                        project(f, slot, WQ, 0, bk["Q"][0], "pa_pe", "pa_out")
                    if k:
                        scores(k, 1 - slot, 1)
                        turn_probs(k, 0, 0)
                        turn_probs(k, 0, 1)
                    if f:
                        project(f, slot, WK, 0, bk["K"][0], "ka_pe", "ka_out")
                    if k:
                        weigh(k, 1 - slot, 0)
                    if f:
                        project(f, slot, WK, 1, bk["K"][1], "kb_pe", "kb_out")
                    if k:
                        turn_probs(k, 1, 0)
                        turn_probs(k, 1, 1)
                        y_rows(k, 0)
                    if f:
                        values(f, slot, 0)
                    if k:
                        weigh(k, 1 - slot, 1)
                        turn_yn(k, 0)
                        y_rows(k, 1)
                    if f:
                        values(f, slot, 1)
                        project(f, slot, WQ, 1, bk["Q"][1], "pb_pe", "pb_out")
                    if k:
                        output(k, 0)
                        turn_yn(k, 1)
                    if n:
                        turn(n, 0)
                        turn(n, 1)

                def step1(n, f, k, late, slot):
                    if k:
                        turn_k(k, 1 - slot, 0)
                        turn_q(k, 1 - slot, 0)
                        turn_k(k, 1 - slot, 1)
                    if late:
                        output(late, 1)
                    if f:
                        project(f, slot, WK, 0, bk["K"][0], "ka_pe", "kbias0", True)
                    if k:
                        turn_q(k, 1 - slot, 1)
                        keys_values(k, 1 - slot, 0)
                    if f:
                        project(f, slot, WK, 1, bk["K"][1], "kb_pe", "kbias1", True)
                    if k:
                        query(k, 0)
                        keys_values(k, 1 - slot, 1)
                    if f:
                        values(f, slot, 0)
                    if k:
                        query(k, 1)
                    if f:
                        project_rows(f, slot, 0, WQ, bk["Q"][0], "q_pe", "q_add")
                    if k:
                        turn_yn(k, 0)
                    if f:
                        values(f, slot, 1)
                    if k:
                        turn_yn(k, 1)
                    if f:
                        project_rows(f, slot, 1, WQ, bk["Q"][1], "q_pe", "q_add")
                    if k:
                        output(k, 0)
                    if n:
                        turn(n, 0)
                        turn(n, 1)

                program(pe, step0 if l == 0 else step1, before)
                if l == 0:
                    pe.drain().then_inc(finished[0], 1)


_OUT = ((32, 128, 512), 'float32')


def kernel(**inputs):
    import numpy as _np
    import concourse.bacc as _bacc
    from concourse import mybir as _mybir
    from concourse.bass_utils import run_bass_kernel_spmd as _run

    nc = _bacc.Bacc("TRN2", target_bir_lowering=False, num_devices=1)
    arrays, args = {}, {}
    for name, value in inputs.items():
        a = _np.ascontiguousarray(value)
        arrays[f"in_{name}_dram"] = a
        args[name] = nc.dram_tensor(f"in_{name}_dram", a.shape, _mybir.dt.from_np(a.dtype), kind="ExternalInput").ap()
    out = nc.dram_tensor("out_0_dram", _OUT[0], _mybir.dt.from_np(_np.dtype(_OUT[1])), kind="ExternalOutput").ap()
    build(nc, args, out)
    r = _run(nc, [arrays], core_ids=[0])
    return r.results[0]["out_0_dram"]
```

```python
from contextlib import ExitStack

import concourse.bass as bass
from concourse import mybir

F32 = mybir.dt.float32
F32R = mybir.dt.float32r
BF16 = mybir.dt.bfloat16
ALU = mybir.AluOpType
ACT = mybir.ActivationFunctionType
AX = mybir.AxisListType

P = 128
GROUP = 2
EPS = 1e-5
MASKED = -1000000.0
PART_ROWS = (0, 32, 64)


class At:

    def __init__(self, reg, const):
        self.reg, self.const = reg, const

    def __add__(self, n):
        return At(self.reg, self.const + n)

    def value(self):
        return self.const if self.reg is None else self.reg + self.const


class Stage:

    always = None

    def __init__(self, sem, earlier):
        self.sem, self.earlier = sem, earlier


def done(stage, at):
    if at.reg is None and at.const < 0:
        return stage.always
    return stage.sem, (at + (1 + stage.earlier)).value()


def landed(stage, group, slot=0):
    if group.reg is None and group.const < 0:
        return stage[slot].always
    return stage[slot].sem, (group + stage[slot].earlier).value() * (16 // GROUP) + 16


def upto(stage, value):
    return stage.sem, stage.earlier + value


def build(nc, t, out):
    B, T, D = t["x"].shape
    TE = t["cond_2048"].shape[1]
    C = D // P
    KE = TE // P
    N = GROUP * P
    assert T == P and B % (2 * GROUP) == 0
    layers = [
        dict(H=16, nw=t["L0_cond_norm_w"], nb=t["L0_cond_norm_b"],
             W=[t["L0_cond_q_w"], t["L0_cond_k_w"], t["L0_cond_v_w"], t["L0_cond_out_w"]],
             b=[t["L0_cond_q_b"], t["L0_cond_k_b"], t["L0_cond_v_b"], t["L0_cond_out_b"]],
             ew=t["L0_cond_emb_w"], eb=t["L0_cond_emb_b"], w2=t["L0_cond_sb_norm_w"], b2=t["L0_cond_sb_norm_b"],
             mask=t["mask_BxS_ff1"]),
        dict(H=8, nw=t["L1_cond_ln_w"], nb=t["L1_cond_ln_b"],
             W=[t["L1_cond_Wq"], t["L1_cond_Wk"], t["L1_cond_Wv"], t["L1_cond_W_out"]],
             b=[t["L1_cond_bq"], t["L1_cond_bk"], t["L1_cond_bv"], t["L1_cond_b_out"]],
             ew=t["L1_cond_W_emb"], eb=t["L1_cond_b_emb"], w2=t["L1_cond_ln2_w"], b2=t["L1_cond_ln2_b"],
             mask=t["mask_BxSx1_fk1"].rearrange("b s o -> b (s o)")),
    ]
    H0, H1 = layers[0]["H"], layers[1]["H"]
    DH0, DH1 = D // H0, D // H1
    HC0 = P // DH0
    WQ, WK, WV, WO = range(4)

    mask_bias = nc.dram_tensor("mask_bias", [B, P], F32, kind="Internal").ap()
    middle = nc.dram_tensor("between_layers", [B, T, D], F32, kind="Internal").ap()

    with ExitStack() as ctx:
        def sb(name, shape, dt=F32):
            return ctx.enter_context(nc.sbuf_tensor(name, shape, dt))

        def sem(name):
            return ctx.enter_context(nc.semaphore(name))

        w_hi = sb("w_hi", [P, 4, C, D], F32R)
        w_lo = sb("w_lo", [P, 4, C, D], F32R)
        k_blocks = sb("k_blocks", [P, 2, C, GROUP, HC0, P])
        k_quarters = k_blocks[:].rearrange("p a b c d e -> p (a b c d e)").rearrange("p (w n) -> p w n", w=4)
        col = sb("col", [P, 6, C])
        NW, NBI, W2, B2, QB, KB = range(6)
        bias_wide = sb("bias_wide", [P, 4, D])
        film_a = sb("film_a", [P, C, B])
        film_b = sb("film_b", [P, C, B])
        silu_cond = sb("silu_cond", [P, KE, B])
        mask_rows = sb("mask_rows", [B, P])
        mask_parts = sb("mask_parts", [B, 3, P], BF16)
        mask_row = sb("mask_row", [P, GROUP, P])
        mask_tmp = mask_row[0:B]
        mask_wide = sb("mask_wide", [P, B * P], BF16)
        ones_parts = sb("ones_parts", [P, P], BF16)
        mask_col = sb("mask_col", [P, B])
        mask_now = sb("mask_now", [P, 1])
        ident = sb("ident", [P, P])
        minus_half = sb("minus_half", [P, 1])
        x_in = sb("x_in", [P, 2, D])
        xn = sb("xn", [P, 2, D])
        stat = sb("stat", [P, 2, 2, 16])
        xt_hi = sb("xt_hi", [P, 2, C, N], F32R)
        xt_lo = sb("xt_lo", [P, 2, C, N], F32R)
        q_t = sb("q_t", [P, 2, C * N])
        v_s = sb("v_s", [P, 2, GROUP, D])
        prob = sb("prob", [P, 2, H0, P])
        emb_ring = prob[:].rearrange("p a h n -> p (a h n)").rearrange("p (k n) -> p k n", k=4)
        raw = [k_quarters[:, 1 + j].rearrange("p (c n) -> p c n", c=C) for j in range(3)] \
            + [emb_ring[:, 0:2].rearrange("p k n -> p (k n)").rearrange("p (c n) -> p c n", c=C)]
        prob_t = sb("prob_t", [P, 2, D])
        row_max = sb("row_max", [P, 2, H0])
        row_sum = sb("row_sum", [P, 2, H0])
        neg_max = sb("neg_max", [P, 2, H0])
        y_t = sb("y_t", [P, D])
        norm_b_wide = y_t[:].rearrange("p (c n) -> p c n", c=C)
        y_s = sb("y_s", [P, D])
        yn = sb("yn", [P, 2, D])
        z_a = sb("z_a", [P, D])
        z_s = sb("z_s", [P, 2, D])
        th = sb("th", [P, D])
        s_s = th
        s_hi = sb("s_hi", [P, 2, D], F32R)
        s_lo = sb("s_lo", [P, 2, D], F32R)
        x_res = sb("x_res", [P, 2, D])
        x_out = x_res

        bank = [ctx.enter_context(nc.psum_tensor(f"bank{i}", [P, D], F32)) for i in range(8)]

        BANKS = [dict(BIAS=(0, 1, 2), TURNED=(3, 6), MASK=7, EMB=(7, 6), FILM=3, X=(5, 4), Q=(6, 2), K=(0, 1), V=(3, 4), PV=(6, 7), Y=(2, 0), H=(6, 6), O=(7, 7)),
                 dict(BIAS=(2, 3, 4), TURNED=(5, 6), MASK=7, EMB=(3, 5), FILM=2, X=(0, 1), K=(6, 7), V=(0, 6), Q=(2, 4), KT=(2, 4), QT=(3, 3), KV=(4, 4), Y=(5, 1), H=(3, 7), O=(5, 7))]

        def chunks(ap):
            return ap.rearrange("p (c n) -> p c n", c=C)

        k_exp = q_t
        q_exp = k_blocks[:, 0].rearrange("p a b c d -> p (a b c d)")[:, 0:2 * GROUP * D] \
            .rearrange("p (s b d) -> p s b d", s=2, b=GROUP)
        k_tmp = k_blocks[:, 1].rearrange("p a b c d -> p (a b c d)")[:, 0:2 * D].rearrange("p (s d) -> p s d", s=2)
        q_tmp = k_blocks[:, 1].rearrange("p a b c d -> p (a b c d)")[:, 2 * D:3 * D]
        per_seq = prob[:].rearrange("p a h n -> p (a h n)").rearrange("p (j d) -> p j d", d=D)
        k_tok = [per_seq[:, b, :] for b in range(GROUP)]
        q_feat = [per_seq[:, GROUP + b, :] for b in range(GROUP)]
        kv_blocks = [per_seq[:, 2 * GROUP + b, :] for b in range(GROUP)]
        k_max = sb("k_max", [P, 2, 2 * GROUP])
        k_sum = sb("k_sum", [P, 2, 2, 2 * GROUP])
        k_rec = sb("k_rec", [P, 2, 2, 2 * GROUP])
        q_max = sb("q_max", [P, H1])
        q_sum = sb("q_sum", [P, H1])
        q_rec = sb("q_rec", [P, 2, GROUP, H1])
        rec0 = sb("rec0", [P, 2, H0])

        once = sem("once")
        consts = sem("consts")
        Stage.always = (consts, 1)
        cond_in = sem("cond_in")
        cond_dve = sem("cond_dve")
        cond_act = sem("cond_act")
        cond_pe = sem("cond_pe")
        finished = [sem(f"layer{l}_finished") for l in range(2)]

        def stages(names, earlier=0):
            return {n: Stage(sem(n), earlier) for n in names.split()}

        def counted_on(these, earlier):
            return {n: Stage(v.sem, earlier) for n, v in these.items()}

        SETUP = dict(norm_in=16 * 2, par_in=16 * 7, mask_in=16, mask_moved=16 * len(PART_ROWS), mask_saved=16, mask_dve=6, mask_pe=1, mask_col_ready=1,
                     beta_wide=1, bias_pe=3, bias_dve=3, w_high=4, w_split=4, zeroed=3,
                     tr_pe=2, tr_dve=2, emb_pe=KE, emb_dve=2, film_pe=1, film_dve=4,
                     ready_dve=1, ready_act=1, ready_pool=1, ready_pe=1)
        SETUP |= {f"w_in{j}": 16 for j in range(4)} | {f"emb_in{k}": 16 * KE // 4 for k in range(4)}
        STAGES = ("stats aggr rstd_a rstd_b neg_mean xn_full xn_turned xt_high xt_low "
                  "pa_pe pb_pe pa_out pb_out ka_pe kb_pe ka_out kb_out v_pe v_add v_mask mask_now "
                  "y_norm stats2 aggr2 rstd2_a rstd2_b neg_mean2 yn_full h_pe z_a_full z_full tanh_full s_full "
                  "s_high s_low o_pe o_out res_full y_pe")
        only0 = ("s_pe0 s_pe1 s_pe2 s_pe3 masked0 masked1 masked2 masked3 smax0 smax1 smax2 smax3 neg0 neg1 neg2 neg3 exp0 exp1 exp2 exp3 "
                 "rec pt_pe0 pt_pe1 pt_pe2 pt_pe3 pt_out0 pt_out1 pt_out2 pt_out3 pv0 pv1 pv2 pv3 "
                 "pv_out")
        only1 = ("kt_pe qt_pe kt_out qt_out att_pe att_out kbias0 kbias1 kmax0 kmax1 ksub0 ksub1 kexp0 kexp1 ksum0 ksum1 krec "
                 "q_pe q_add qmax qsub qexp qsum qrec")
        both = stages(STAGES)
        moved = {n: [sem(f"{n}{b}") for b in range(GROUP)] for n in ("x_in_full", "res_in", "stored", "mask_row_in")}
        setup = [{n: Stage(sem(n), 0) for n in SETUP}]
        setup.append({n: Stage(v.sem, SETUP[n]) for n, v in setup[0].items()})
        S = [setup[0] | both | stages(only0), setup[1] | counted_on(both, B) | stages(only1)]
        for l in range(2):
            S[l] |= {n: [Stage(v, B * l) for v in places] for n, places in moved.items()}

        src = [t["x"], middle]
        dst = [middle, out]

        def program(eng, step, weights, film, claims=None, projected=None):
            first, last = GROUP, B - 5 * GROUP

            def recount(reg, shift):
                if claims is not None:
                    for b, readers in claims.items():
                        claims[b] = tuple((n, At(reg, at.const + shift)) for n, at in readers)

            def at(c):
                return At(None, c * GROUP)

            step(at(0), None, None, None, 1)
            weights()
            step(at(1), at(0), None, None, 0)
            film()
            step(at(2), at(1), at(0), None, 1)
            with eng.Fori(first, last + 1, 2 * GROUP) as k:
                recount(k, -first)
                step(At(k, 2 * GROUP), At(k, GROUP), At(k, 0), At(k, -1), 0)
                step(At(k, 3 * GROUP), At(k, 2 * GROUP), At(k, GROUP), At(k, GROUP - 1), 1)
            recount(None, last)
            G = B // GROUP
            step(at(G - 1), at(G - 2), at(G - 3), at(G - 3) + (-1), 0)
            step(None, at(G - 1), at(G - 2), at(G - 2) + (-1), 1)
            if projected:
                projected()
            step(None, None, at(G - 1), at(G - 1) + (-1), 0)
            step(None, None, None, at(G) + (-1), 1)

        def sequence(dram, at):
            if at.reg is None:
                return dram[at.const]
            return dram[bass.ds(at.value(), 1)].rearrange("o t d -> (o t) d")

        def batch_cols(tile, at, width):
            if at.reg is None:
                return tile[:, at.const * width:(at.const + 1) * width]
            return tile[:, bass.ds(at.value() * width, width)]

        def film_of(tile, at):
            if at.reg is None:
                v = tile[:, :, at.const:at.const + 1]
            else:
                v = tile[:, :, bass.ds(at.value(), 1)]
            return v.broadcast_to([P, C, P])

        block = ctx.enter_context(nc.Block())

        @block.sync
        def _(sp):
            for l, L in enumerate(layers):
                s, bk = S[l], BANKS[l]
                if l == 1:
                    sp.wait_ge(finished[0], 4)

                def load_weight(l, j):
                    sp.dma_start(raw[j], layers[l]["W"][j].rearrange("(c p) n -> p c n", p=P)
                                 ).then_inc(S[l][f"w_in{j}"].sem, 16)

                def load_norm(l):
                    for i, p in ((NBI, "nb"), (NW, "nw")):
                        sp.dma_start(col[:, i, :], layers[l][p].rearrange("(c p) -> p c", p=P),
                                     allow_slow_non_contiguous=True).then_inc(S[l]["norm_in"].sem, 16)

                def load_emb(k):
                    sp.dma_start(emb_ring[:, (k + 2) % 4], L["ew"][k * P:(k + 1) * P, :]
                                 ).then_inc(s[f"emb_in{k % 4}"].sem, 16)

                def weights():
                    sp.dma_start(mask_rows[:], L["mask"]).then_inc(s["mask_in"].sem, 16)
                    if l == 0:
                        for j in range(3):
                            load_weight(0, j)
                        sp.dma_start(prob_t[0:B, :, :].rearrange("p a b -> p (a b)"), t["cond_2048"]).then_inc(cond_in, 16)
                    for j in range(4):
                        sp.dma_start(bias_wide[:, j, :], L["b"][j].rearrange("(o n) -> o n", o=1).broadcast_to([P, D])
                                     ).then_inc(s["par_in"].sem, 16)
                    for i, p in ((W2, "w2"), (B2, "b2")):
                        sp.dma_start(col[:, i, :], L[p].rearrange("(c p) -> p c", p=P), allow_slow_non_contiguous=True
                                     ).then_inc(s["par_in"].sem, 16)
                    sp.dma_start(x_out[0:B].rearrange("p a n -> p (a n)"),
                                 L["eb"].rearrange("(o n) -> o n", o=1).broadcast_to([B, 2 * D])).then_inc(s["par_in"].sem, 16)
                    load_weight(l, WO)
                    load_emb(0)
                    load_emb(1)
                    if l == 0:
                        sp.wait_ge(*upto(s["mask_dve"], 2))
                        sp.dma_start(mask_bias, mask_tmp[:, 1, :]).then_inc(s["mask_saved"].sem, 16)
                    sp.wait_ge(*upto(s["mask_dve"], 6))
                    for j, row in enumerate(PART_ROWS):
                        sp.dma_start(mask_wide[row:row + 1, :].rearrange("o (b n) -> o b n", b=B),
                                     mask_parts[:, j, :]).then_inc(s["mask_moved"].sem, 16)

                def film():
                    sp.wait_ge(*upto(s["w_split"], 4))
                    for k in range(2, KE):
                        if k >= 4:
                            sp.wait_ge(*upto(s["emb_pe"], k - 3))
                        load_emb(k)
                    sp.wait_ge(*upto(s["emb_dve"], 2))

                def projected():
                    sp.wait_ge(*done(s["xn_full"], At(None, B - 1)))
                    sp.wait_ge(*done(s["stats"], At(None, B - 1)))
                    sp.wait_ge(*landed(s["stored"], At(None, 0), 0))
                    sp.wait_ge(*landed(s["stored"], At(None, 0), 1))
                    for b in range(GROUP):
                        sp.dma_start(x_in[:, b, :], middle[b]).then_inc(S[1]["x_in_full"][b].sem, 16)
                    sp.wait_ge(*done(s["s_pe3"], At(None, B - 1)))
                    load_norm(1)
                    for j in range(3):
                        load_weight(1, j)

                def load_front(f):
                    for b in range(GROUP):
                        sp.wait_ge(*done(s["xn_full"], f + (b - 2)))
                        sp.wait_ge(*done(s["stats"], f + (b - 2)))
                        sp.dma_start(x_in[:, b, :], sequence(src[l], f + b)).then_inc(s["x_in_full"][b].sem, 16)

                def load_mask(f):
                    sp.wait_ge(*upto(s["mask_saved"], 16))
                    for b in range(GROUP):
                        sp.wait_ge(*done(s["masked3"], f + (b - 2)))
                        sp.dma_start(mask_row[:, b, :], mask_bias_of(f + b).broadcast_to([P, P])
                                     ).then_inc(s["mask_row_in"][b].sem, 16)

                def mask_bias_of(at):
                    if at.reg is None:
                        return mask_bias[at.const:at.const + 1, :]
                    return mask_bias[bass.ds(at.value(), 1), :]

                def load_back(k):
                    for b in range(GROUP):
                        sp.wait_ge(*landed(s["stored"], k + (-GROUP), b))
                        sp.dma_start(x_res[:, b, :], sequence(src[l], k + b)).then_inc(s["res_in"][b].sem, 16)

                def store(at, b):
                    sp.wait_ge(*done(s["o_out"], at))
                    sp.dma_start(sequence(dst[l], at), x_out[:, b, :]).then_inc(s["stored"][b].sem, 16)

                def step(n, f, k, late, slot):
                    if n and not (l == 1 and n.reg is None and n.const == 0):
                        load_front(n)
                    if late:
                        store(late, 1)
                    if k:
                        load_back(k)
                    if f and l == 0:
                        load_mask(f)
                    if k:
                        store(k, 0)

                if l == 0:
                    load_norm(0)
                program(sp, step, weights, film, projected=projected if l == 0 else None)
                for b in range(GROUP):
                    sp.wait_ge(*landed(s["stored"], At(None, B - GROUP), b))
                if l == 0:
                    sp.wait_ge(finished[0], 4)

        @block.gpsimd
        def _(pool):
            pool.memset(ident[:], 0.0).then_inc(once, 1)
            pool.wait_ge(once, 1)
            pool.affine_select(out=ident[:], in_=ident[:], compare_op=ALU.not_equal, fill=1.0, base=0,
                               pattern=[[-1, P]], channel_multiplier=1).then_inc(once, 1)
            pool.memset(minus_half[:], -0.5).then_inc(once, 1)
            pool.memset(mask_wide[:], 0.0).then_inc(once, 1)
            pool.memset(ones_parts[:], 0.0).then_inc(once, 1)
            pool.wait_ge(once, 5)
            for r0 in PART_ROWS:
                last = pool.memset(ones_parts[r0:r0 + 1, :], 1.0)
            last.then_inc(once, 1)
            pool.wait_ge(once, 6)
            pool.memset(k_max[:], 0.0).then_inc(consts, 1)
            for l, L in enumerate(layers):
                s, bk = S[l], BANKS[l]
                if l == 1:
                    pool.wait_ge(finished[0], 4)

                def weights():
                    if l == 0:
                        pool.memset(k_quarters[:, 0], 0.0).then_inc(s["zeroed"].sem, 1)
                        pool.wait_ge(*upto(s["w_split"], 1))
                        pool.wait_ge(*upto(s["w_high"], 1))
                        pool.wait_ge(*upto(s["bias_pe"], 1))
                        pool.memset(k_quarters[:, 1], 0.0).then_inc(s["zeroed"].sem, 1)
                        pool.wait_ge(*upto(s["zeroed"], 2))
                    pool.wait_ge(*upto(s["mask_col_ready"], 1))
                    pool.wait_ge(*upto(s["par_in"], 16 * 7))
                    pool.drain().then_inc(s["ready_pool"].sem, 1)
                    for n in ("ready_dve", "ready_act", "ready_pe"):
                        pool.wait_ge(*upto(s[n], 1))

                def film():
                    if l == 0:
                        pool.memset(k_quarters[:, 2:4], 0.0).then_inc(s["zeroed"].sem, 1)
                    else:
                        pool.wait_ge(*upto(s["emb_pe"], KE))
                        pool.memset(per_seq[:, 2 * GROUP:3 * GROUP, :], 0.0).then_inc(s["zeroed"].sem, 1)
                    pool.wait_ge(*upto(s["film_dve"], 4))

                def rsqrt_norm(b, which, mv, a_in, rs, nm, full, src_ap, dst_ap, at, dst_free):
                    v = stat[:, which, b, :]
                    pool.wait_ge(*done(s[mv], at))
                    pool.nop(nofuse=True)
                    pool.tensor_scalar(v[:, 8:9], v[:, 7:8], EPS, None, ALU.add).then_inc(s[a_in].sem, 1)
                    pool.tensor_scalar(v[:, 10:11], v[:, 6:7], -1.0, None, ALU.mult).then_inc(s[nm].sem, 1)
                    pool.wait_ge(*done(s[a_in], at))
                    pool.tensor_tensor(v[:, 9:10], v[:, 8:9], minus_half[:], ALU.pow).then_inc(s[rs].sem, 1)
                    pool.wait_ge(*done(s[rs], at))
                    pool.wait_ge(*done(s[nm], at))
                    for d in dst_free:
                        pool.wait_ge(*done(d, at + (-2)))
                    pool.nop(nofuse=True)
                    pool.tensor_scalar(dst_ap, src_ap, v[:, 10:11], v[:, 9:10], ALU.add, ALU.mult
                                       ).then_inc(s[full].sem, 1)

                def norm1(f, b):
                    pool.wait_ge(*landed(s["x_in_full"], f, b))
                    rsqrt_norm(b, 0, "aggr", "rstd_a", "rstd_b", "neg_mean", "xn_full",
                               x_in[:, b, :], xn[:, b, :], f + b, [s["xn_turned"]])

                def norm2(k, b):
                    rsqrt_norm(b, 1, "aggr2", "rstd2_a", "rstd2_b", "neg_mean2", "yn_full",
                               y_s[:], yn[:, b, :], k + b, [s["h_pe"]])

                def v_mask(f, slot, b):
                    pool.wait_ge(*done(s["v_mask"], f + (b - 1)))
                    pool.tensor_copy(mask_now[:], mask_at(f + b)).then_inc(s["mask_now"].sem, 1)
                    pool.wait_ge(*done(s["mask_now"], f + b))
                    pool.wait_ge(*done(s["v_add"], f + b))
                    pool.nop(nofuse=True)
                    pool.tensor_scalar(v_s[:, slot, b, :], v_s[:, slot, b, :], mask_now[:], 1.0,
                                       ALU.mult, ALU.mult).then_inc(s["v_mask"].sem, 1)

                def mask_at(at):
                    if at.reg is None:
                        return mask_col[:, at.const:at.const + 1]
                    return mask_col[:, bass.ds(at.value(), 1)]

                def add_shift(k, b):
                    pool.wait_ge(*done(s["z_a_full"], k + b))
                    pool.wait_ge(*done(s["s_full"], k + (b - 2)))
                    pool.tensor_tensor(chunks(z_s[:, b, :]), chunks(z_a[:]), film_of(film_b, k + b), ALU.add
                                       ).then_inc(s["z_full"].sem, 1)

                def residual(k, b):
                    pool.wait_ge(*landed(s["res_in"], k, b))
                    pool.tensor_tensor(x_res[:, b, :], x_res[:, b, :], bias_wide[:, WO, :], ALU.add
                                       ).then_inc(s["res_full"].sem, 1)

                def step(n, f, k, late, slot):
                    if k:
                        residual(k, 0)
                    if l == 0:
                        if n:
                            norm1(n, 0)
                            norm1(n, 1)
                        if k:
                            norm2(k, 0)
                        if f:
                            v_mask(f, slot, 0)
                        if k:
                            add_shift(k, 0)
                            norm2(k, 1)
                        if f:
                            v_mask(f, slot, 1)
                        if k:
                            add_shift(k, 1)
                            residual(k, 1)
                    else:
                        if k:
                            norm2(k, 0)
                        if f:
                            v_mask(f, slot, 0)
                        if k:
                            norm2(k, 1)
                            add_shift(k, 0)
                        if n:
                            norm1(n, 0)
                        if f:
                            v_mask(f, slot, 1)
                        if k:
                            add_shift(k, 1)
                        if n:
                            norm1(n, 1)
                        if k:
                            residual(k, 1)

                program(pool, step, weights, film)
                if l == 0:
                    pool.wait_ge(*done(s["z_full"], At(None, B - 1)))
                    pool.drain().then_inc(finished[0], 1)

        @block.scalar
        def _(act):
            act.wait_ge(consts, 1)
            for l, L in enumerate(layers):
                s, bk = S[l], BANKS[l]
                if l == 1:
                    act.wait_ge(finished[0], 4)

                def weights():
                    act.wait_ge(*upto(s["norm_in"], 16 * 2))
                    for j in range(3):
                        act.wait_ge(*upto(s[f"w_in{j}"], 16))
                        for c in range(C):
                            last = act.activation(w_hi[:, j, c], raw[j][:, c], ACT.Identity, scale=col[:, NW, c:c + 1])
                        last.then_inc(s["w_high"].sem, 1)
                    if l == 0:
                        act.wait_ge(cond_in, 16)
                        act.activation(z_s[0:B].rearrange("p a n -> p (a n)"), prob_t[0:B].rearrange("p a n -> p (a n)"),
                                       ACT.Tanh, scale=0.5).then_inc(cond_act, 1)
                    act.wait_ge(*upto(s["w_high"], 3))
                    act.drain().then_inc(s["ready_act"].sem, 1)
                    for n in ("ready_dve", "ready_pool", "ready_pe"):
                        act.wait_ge(*upto(s[n], 1))
                    act.wait_ge(*upto(s[f"w_in{WO}"], 16))
                    act.activation(w_hi[:, WO], raw[WO], ACT.Copy, scale=0.5).then_inc(s["w_high"].sem, 1)

                def film():
                    act.wait_ge(*upto(s["emb_pe"], KE))
                    act.wait_ge(*upto(s["zeroed"], 3 if l == 0 else 1))

                def xt_high(f, slot, b):
                    act.wait_ge(*done(s["xn_turned"], f + b))
                    act.wait_ge(*done(s["pb_pe" if l == 0 else "q_pe"], f + (-GROUP - 1)))
                    act.activation(xt_hi[:, slot, :, b * P:(b + 1) * P], chunks(bank[bk["X"][b]][:]), ACT.Copy
                                   ).then_inc(s["xt_high"].sem, 1)

                def q_out(f, slot, pair):
                    act.wait_ge(*done(s["pa_pe" if pair == 0 else "pb_pe"], f))
                    src_bank = bank[bk["Q"][pair]][:].rearrange("p (c n) -> p c n", c=2)
                    if pair == 0:
                        act.wait_ge(*done(s["s_pe3"], f + (-GROUP - 1)))
                    qv = q_t[:, slot, :].rearrange("p (c n) -> p c n", c=C)
                    for j in range(2):
                        c = 2 * pair + j
                        last = act.activation(qv[:, c, :], src_bank[:, j, :], ACT.Identity,
                                              bias=col[:, QB, c:c + 1])
                    last.then_inc(s["pa_out" if pair == 0 else "pb_out"].sem, GROUP)

                def k_out(f, slot, pair, some=(0, 1)):
                    act.wait_ge(*done(s["ka_pe" if pair == 0 else "kb_pe"], f))
                    if pair == 0:
                        act.wait_ge(*done(s["s_pe3"], f + (-GROUP - 1)))
                    src_bank = bank[bk["K"][pair]][:].rearrange("p (c b n) -> p c b n", c=2, b=GROUP)
                    for j in some:
                        c = 2 * pair + j
                        for r in range(HC0):
                            rows = slice(DH0 * r, DH0 * (r + 1))
                            last = act.activation(k_blocks[rows, slot, c, :, r, :], src_bank[rows, j], ACT.Identity,
                                                  bias=col[rows, KB, c:c + 1])
                    if 1 in some:
                        last.then_inc(s["ka_out" if pair == 0 else "kb_out"].sem, GROUP)

                def exps(k, b, some):
                    act.wait_ge(*done(s["rec"], k + (b - 2)))
                    for c in some:
                        act.wait_ge(*done(s[f"neg{c}"], k + b))
                        for h in range(HC0 * c, HC0 * (c + 1)):
                            last = act.activation(prob[:, b, h, :], prob[:, b, h, :], ACT.Exp, bias=neg_max[:, b, h:h + 1],
                                                  accum_out=row_sum[:, b, h:h + 1])
                        last.then_inc(s[f"exp{c}"].sem, 1)

                def prob_turned(k, b, some):
                    for c in some:
                        act.wait_ge(*done(s[f"pt_pe{c}"], k + b))
                        if c >= 2:
                            act.wait_ge(*done(s[f"pv{c - 2}"], k + b))
                        else:
                            act.wait_ge(*done(s[f"pv{c + 2}"], k + (b - 1)))
                        act.activation(prob_t[:, c % 2, :], bank[4 + c % 2][:], ACT.Copy).then_inc(s[f"pt_out{c}"].sem, 1)

                def y_t_out(k, b):
                    act.wait_ge(*done(s["pv3"], k + b))
                    act.wait_ge(*done(s["y_pe"], k + (b - 1)))
                    act.activation(y_t[:], bank[bk["PV"][b]][:], ACT.Copy).then_inc(s["pv_out"].sem, 1)

                def tanh(k, b):
                    act.wait_ge(*done(s["z_full"], k + b))
                    act.wait_ge(*done(s["s_low"], k + (b - 1)))
                    act.wait_ge(*done(s["s_high"], k + (b - 1)))
                    act.activation(th[:], z_s[:, b, :], ACT.Tanh, scale=0.5).then_inc(s["tanh_full"].sem, 1)

                def s_high(k, b):
                    act.wait_ge(*done(s["s_full"], k + b))
                    act.wait_ge(*done(s["o_pe"], k + (b - 2)))
                    act.activation(s_hi[:, b, :], s_s[:], ACT.Copy).then_inc(s["s_high"].sem, 1)

                def k_bias(f, slot, pair):
                    act.wait_ge(*done(s["ka_pe" if pair == 0 else "kb_pe"], f))
                    src_bank = bank[bk["K"][pair]][:].rearrange("p (c n) -> p c n", c=2)
                    act.wait_ge(*done(s[f"ksub{pair}"], f + (-GROUP)))
                    kt = k_tmp[:, pair, :].rearrange("p (c n) -> p c n", c=2)
                    for j in range(2):
                        c = 2 * pair + j
                        last = act.activation(kt[:, j, :], src_bank[:, j, :], ACT.Identity,
                                              bias=col[:, KB, c:c + 1])
                    last.then_inc(s[f"kbias{pair}"].sem, GROUP)

                def k_exps(f, slot, pair):
                    act.wait_ge(*done(s[f"ksub{pair}"], f))
                    v = k_exp[:, slot, pair * D:(pair + 1) * D]
                    act.activation(v, v, ACT.Exp).then_inc(s[f"kexp{pair}"].sem, GROUP)

                def q_exps(f, slot, b):
                    act.wait_ge(*done(s["qsub"], f + b))
                    v = q_exp[:, slot, b, :]
                    act.activation(v, v, ACT.Exp).then_inc(s["qexp"].sem, 1)

                def kt_out(k, b):
                    act.wait_ge(*done(s["kt_pe"], k + b))
                    act.wait_ge(*done(s["att_pe"], k + (b - GROUP)))
                    act.activation(k_tok[b], bank[bk["KT"][b]][:], ACT.Copy).then_inc(s["kt_out"].sem, 1)

                def qt_out(k, b):
                    act.wait_ge(*done(s["qt_pe"], k + b))
                    act.wait_ge(*done(s["y_pe"], k + (b - GROUP)))
                    act.activation(q_feat[b], bank[bk["QT"][b]][:], ACT.Copy).then_inc(s["qt_out"].sem, 1)

                def step0(n, f, k, late, slot):
                    if late:
                        tanh(late + (-1), 1)
                        s_high(late + (-1), 1)
                    if k:
                        exps(k, 0, range(C))
                    if f:
                        q_out(f, slot, 0)
                    if k:
                        exps(k, 1, (0,))
                        prob_turned(k, 0, (0, 1))
                        exps(k, 1, (1,))
                        prob_turned(k, 0, (2, 3))
                        y_t_out(k, 0)
                        exps(k, 1, (2, 3))
                        prob_turned(k, 1, (0, 1))
                    if f:
                        k_out(f, slot, 0, (0,))
                    if k:
                        prob_turned(k, 1, (2, 3))
                        y_t_out(k, 1)
                    if f:
                        k_out(f, slot, 0, (1,))
                    if k:
                        tanh(k, 0)
                    if f:
                        k_out(f, slot, 1)
                    if k:
                        s_high(k, 0)
                    if f:
                        q_out(f, slot, 1)
                    if n:
                        xt_high(n, 1 - slot, 0)
                        xt_high(n, 1 - slot, 1)

                def step1(n, f, k, late, slot):
                    if k:
                        kt_out(k, 0)
                        qt_out(k, 0)
                        kt_out(k, 1)
                    if f:
                        k_bias(f, slot, 0)
                        k_exps(f, slot, 0)
                    if k:
                        qt_out(k, 1)
                    if f:
                        k_bias(f, slot, 1)
                        k_exps(f, slot, 1)
                    if k:
                        tanh(k, 0)
                    if f:
                        q_exps(f, slot, 0)
                    if k:
                        s_high(k, 0)
                        tanh(k, 1)
                        s_high(k, 1)
                    if f:
                        q_exps(f, slot, 1)
                    if n:
                        xt_high(n, 1 - slot, 0)
                        xt_high(n, 1 - slot, 1)

                program(act, step0 if l == 0 else step1, weights, film)
                if l == 0:
                    act.wait_ge(*done(s["s_high"], At(None, B - 1)))
                    act.drain().then_inc(finished[0], 1)

        @block.vector
        def _(dve):
            dve.wait_ge(consts, 1)
            for l, L in enumerate(layers):
                s, bk = S[l], BANKS[l]
                if l == 1:
                    dve.wait_ge(finished[0], 4)

                def cut_mask():
                    dve.wait_ge(*upto(s["mask_in"], 16))
                    md = s["mask_dve"]
                    dve.tensor_scalar(mask_tmp[:, 0, :], mask_rows[:], -1.0, 1.0, ALU.mult, ALU.add).then_inc(md.sem, 1)
                    dve.wait_ge(*upto(md, 1))
                    dve.tensor_scalar(mask_tmp[:, 1, :], mask_tmp[:, 0, :], MASKED, None, ALU.mult).then_inc(md.sem, 1)
                    dve.wait_ge(*upto(md, 2))
                    dve.tensor_copy(mask_parts[:, 0, :], mask_tmp[:, 1, :]).then_inc(md.sem, 1)
                    dve.wait_ge(*upto(md, 3))
                    dve.tensor_tensor(mask_tmp[:, 0, :], mask_tmp[:, 1, :], mask_parts[:, 0, :], ALU.subtract
                                      ).then_inc(md.sem, 1)
                    dve.wait_ge(*upto(md, 4))
                    dve.tensor_copy(mask_parts[:, 1, :], mask_tmp[:, 0, :]).then_inc(md.sem, 1)
                    dve.wait_ge(*upto(md, 5))
                    dve.tensor_tensor(mask_parts[:, 2, :], mask_tmp[:, 0, :], mask_parts[:, 1, :], ALU.subtract
                                      ).then_inc(md.sem, 1)
                    dve.wait_ge(*upto(s["mask_pe"], 1))
                    dve.tensor_copy(mask_col[:], bank[bk["MASK"]][:, 0:B]).then_inc(s["mask_col_ready"].sem, 1)

                def condition():
                    flat = lambda v: v[0:B].rearrange("p a n -> p (a n)")
                    dve.wait_ge(cond_act, 1)
                    dve.scalar_tensor_tensor(out=flat(yn[:]), in0=flat(z_s[:]), scalar=1.0, in1=flat(prob_t[:]),
                                             op0=ALU.add, op1=ALU.mult).then_inc(cond_dve, 1)
                    dve.wait_ge(cond_dve, 1)
                    dve.tensor_scalar(flat(z_s[:]), flat(yn[:]), 0.5, None, ALU.mult).then_inc(cond_dve, 1)

                def weights():
                    cut_mask()
                    for j in range(3):
                        dve.wait_ge(*upto(s["w_high"], j + 1))
                        for c in range(C):
                            last = dve.scalar_tensor_tensor(out=w_lo[:, j, c], in0=raw[j][:, c],
                                                            scalar=col[:, NW, c:c + 1], in1=w_hi[:, j, c].bitcast(F32),
                                                            op0=ALU.mult, op1=ALU.subtract)
                        last.then_inc(s["w_split"].sem, 1)
                    if l == 0:
                        condition()
                    dve.wait_ge(*upto(s["par_in"], 16 * 7))
                    for j in range(3):
                        dve.wait_ge(*upto(s["bias_pe"], j + 1))
                        dve.tensor_tensor(bias_wide[:, j, :], bias_wide[:, j, :], bank[bk["BIAS"][j]][:], ALU.add
                                          ).then_inc(s["bias_dve"].sem, 1)
                    if l == 0:
                        dve.wait_ge(cond_pe, 1)
                        dve.tensor_copy(silu_cond[:].rearrange("p k b -> p (k b)"), bank[bk["TURNED"][1]][:, 0:KE * B]
                                        ).then_inc(cond_dve, 1)
                    for j in range(2):
                        dve.wait_ge(*upto(s["tr_pe"], j + 1))
                        dve.tensor_copy(col[:, QB + j, :], chunks(bank[bk["TURNED"][j]][:])[:, :, 0]
                                        ).then_inc(s["tr_dve"].sem, 1)
                    dve.wait_ge(*upto(s["w_split"], 3))
                    dve.wait_ge(*upto(s["tr_dve"], 2))
                    dve.drain().then_inc(s["ready_dve"].sem, 1)
                    for n in ("ready_pool", "ready_act", "ready_pe"):
                        dve.wait_ge(*upto(s[n], 1))
                    dve.wait_ge(*upto(s["w_high"], 4))
                    dve.scalar_tensor_tensor(out=w_lo[:, WO], in0=raw[WO], scalar=0.5, in1=w_hi[:, WO].bitcast(F32),
                                             op0=ALU.mult, op1=ALU.subtract).then_inc(s["w_split"].sem, 1)

                def film():
                    e_rows = yn[0:B].rearrange("p a n -> p (a n)")
                    eb_rows = x_out[0:B].rearrange("p a n -> p (a n)")
                    dve.wait_ge(*upto(s["emb_pe"], KE))
                    for h in range(2):
                        dve.tensor_tensor(e_rows[:, h * D:(h + 1) * D], bank[bk["EMB"][h]][0:B, :],
                                          eb_rows[:, h * D:(h + 1) * D], ALU.add).then_inc(s["emb_dve"].sem, 1)
                    dve.wait_ge(*upto(s["film_pe"], 1))
                    et = z_s[:].rearrange("p a n -> p (a n)")[:, 0:2 * C * B].rearrange("p (c b) -> p c b", b=B)
                    fd = s["film_dve"]
                    dve.tensor_copy(et.rearrange("p c b -> p (c b)"), bank[bk["FILM"]][:, 0:2 * C * B]).then_inc(fd.sem, 1)
                    dve.wait_ge(*upto(fd, 1))
                    wide = lambda i: col[:, i, :].rearrange("p (c o) -> p c o", o=1).broadcast_to([P, C, B])
                    dve.scalar_tensor_tensor(out=film_a[:], in0=et[:, 0:C, :], scalar=1.0, in1=wide(W2),
                                             op0=ALU.add, op1=ALU.mult).then_inc(fd.sem, 1)
                    dve.scalar_tensor_tensor(out=film_b[:], in0=et[:, 0:C, :], scalar=1.0, in1=wide(B2),
                                             op0=ALU.add, op1=ALU.mult).then_inc(fd.sem, 1)
                    dve.wait_ge(*upto(fd, 3))
                    dve.tensor_tensor(film_b[:], film_b[:], et[:, C:2 * C, :], ALU.add).then_inc(fd.sem, 1)
                    dve.wait_ge(*upto(fd, 4))
                    if l == 1:
                        dve.wait_ge(*upto(s["zeroed"], 1))

                def moments(which, b, src_ap, st, ag, at):
                    v = stat[:, which, b, :]
                    dve.bn_stats(v[:, 0:6], src_ap).then_inc(s[st].sem, 1)
                    dve.wait_ge(*done(s[st], at))
                    dve.wait_ge(*done(s["xn_full" if which == 0 else "yn_full"], at + (-2)))
                    dve.nop(nofuse=True)
                    dve.bn_aggr(v[:, 6:8], v[:, 0:6]).then_inc(s[ag].sem, 1)

                def stats1(f, b):
                    dve.wait_ge(*landed(s["x_in_full"], f, b))
                    moments(0, b, x_in[:, b, :], "stats", "aggr", f + b)

                def xt_low(f, slot, b):
                    dve.wait_ge(*done(s["xt_high"], f + b))
                    hs = xt_hi[:, slot, :, b * P:(b + 1) * P]
                    dve.tensor_tensor(xt_lo[:, slot, :, b * P:(b + 1) * P], chunks(bank[bk["X"][b]][:]), hs.bitcast(F32),
                                      ALU.subtract).then_inc(s["xt_low"].sem, 1)

                def softmax(k, b, some):
                    if 0 in some:
                        dve.wait_ge(*landed(s["mask_row_in"], k, b))
                    row = mask_row[:, b, :].rearrange("p (o n) -> p o n", o=1).broadcast_to([P, HC0, P])
                    for c in some:
                        heads = slice(HC0 * c, HC0 * (c + 1))
                        dve.wait_ge(*done(s[f"s_pe{c}"], k + b))
                        dve.wait_ge(*done(s[f"pt_pe{c}"], k + (b - 2)))
                        dve.tensor_tensor(prob[:, b, heads, :], bank[c][:].rearrange("p (r n) -> p r n", r=HC0), row,
                                          ALU.add).then_inc(s[f"masked{c}"].sem, 1)
                        dve.wait_ge(*done(s[f"masked{c}"], k + b))
                        dve.tensor_reduce(row_max[:, b, heads], prob[:, b, heads, :], AX.X, ALU.max
                                          ).then_inc(s[f"smax{c}"].sem, 1)
                        dve.wait_ge(*done(s[f"smax{c}"], k + b))
                        dve.tensor_scalar(neg_max[:, b, heads], row_max[:, b, heads], -1.0, None, ALU.mult
                                          ).then_inc(s[f"neg{c}"].sem, 1)

                def sums_inverse(k, b):
                    for c in range(C):
                        dve.wait_ge(*done(s[f"exp{c}"], k + b))
                    dve.reciprocal(rec0[:, b, :], row_sum[:, b, :]).then_inc(s["rec"].sem, 1)

                def v_add(f, slot, b):
                    dve.wait_ge(*done(s["v_pe"], f + b))
                    dve.wait_ge(*done(s["pv3" if l == 0 else "att_pe"], f + (b - 2 * GROUP)))
                    vb = bank[bk["V"][b]]
                    dve.tensor_tensor(v_s[:, slot, b, :], vb[:], bias_wide[:, WV, :], ALU.add).then_inc(s["v_add"].sem, 1)

                def y_norm(k, kslot, b):
                    dve.wait_ge(*done(s["y_pe"], k + b))
                    dve.wait_ge(*done(s["stats2"], k + (b - 1)))
                    dve.wait_ge(*done(s["yn_full"], k + (b - 1)))
                    if l == 0:
                        dve.wait_ge(*done(s["rec"], k + b))
                        yb, h, rc = bank[bk["Y"][b]], H0, rec0[:, b, :]
                    else:
                        yb, h, rc = bank[bk["Y"][b]], H1, q_rec[:, kslot, b, :]
                        dve.wait_ge(*done(s["qrec"], k + b))
                    hv = lambda ap: ap.rearrange("p (h e) -> p h e", h=h)
                    dve.tensor_tensor(hv(y_s[:]), hv(yb[:]),
                                      rc.rearrange("p (h o) -> p h o", o=1).broadcast_to([P, h, D // h]),
                                      ALU.mult).then_inc(s["y_norm"].sem, 1)
                    dve.wait_ge(*done(s["y_norm"], k + b))
                    moments(1, b, y_s[:], "stats2", "aggr2", k + b)

                def film_scale(k, b):
                    dve.wait_ge(*done(s["h_pe"], k + b))
                    dve.wait_ge(*done(s["z_full"], k + (b - 1)))
                    dve.tensor_tensor(chunks(z_a[:]), chunks(bank[bk["H"][b]][:]), film_of(film_a, k + b), ALU.mult
                                      ).then_inc(s["z_a_full"].sem, 1)

                def silu(k, b):
                    dve.wait_ge(*done(s["tanh_full"], k + b))
                    dve.wait_ge(*done(s["s_high"], k + (b - 1)))
                    dve.wait_ge(*done(s["s_low"], k + (b - 1)))
                    dve.scalar_tensor_tensor(out=s_s[:], in0=th[:], scalar=1.0, in1=z_s[:, b, :],
                                             op0=ALU.add, op1=ALU.mult).then_inc(s["s_full"].sem, 1)

                def s_low_part(k, b):
                    dve.wait_ge(*done(s["s_high"], k + b))
                    dve.wait_ge(*done(s["o_pe"], k + (b - 2)))
                    dve.tensor_tensor(s_lo[:, b, :], s_s[:], s_hi[:, b, :].bitcast(F32), ALU.subtract
                                      ).then_inc(s["s_low"].sem, 1)

                def output(at, b):
                    dve.wait_ge(*done(s["o_pe"], at))
                    dve.wait_ge(*done(s["res_full"], at))
                    dve.tensor_tensor(x_out[:, b, :], bank[bk["O"][b]][:], x_res[:, b, :], ALU.add
                                      ).then_inc(s["o_out"].sem, 1)

                def k_soft(f, slot, pair):
                    dve.wait_ge(*done(s[f"kbias{pair}"], f))
                    kt = k_tmp[:, pair, :].rearrange("p (g n) -> p g n", n=P)
                    km = k_max[:, pair, :]
                    dve.tensor_reduce(km, kt, AX.X, ALU.max).then_inc(s[f"kmax{pair}"].sem, GROUP)
                    dve.wait_ge(*done(s[f"kmax{pair}"], f))
                    dve.wait_ge(*done(s["kt_pe"], f + (-GROUP - 1)))
                    dve.wait_ge(*done(s[f"ksum{pair}"], f + (-2 * GROUP)))
                    dve.tensor_tensor(k_exp[:, slot, pair * D:(pair + 1) * D].rearrange("p (g n) -> p g n", n=P), kt,
                                      km.rearrange("p (g o) -> p g o", o=1).broadcast_to([P, 2 * GROUP, P]),
                                      ALU.subtract).then_inc(s[f"ksub{pair}"].sem, GROUP)

                def k_sums(f, slot):
                    for pair in range(2):
                        dve.wait_ge(*done(s[f"kexp{pair}"], f))
                        dve.tensor_reduce(k_sum[:, slot, pair, :],
                                          k_exp[:, slot, pair * D:(pair + 1) * D].rearrange("p (g n) -> p g n", n=P),
                                          AX.X, ALU.add).then_inc(s[f"ksum{pair}"].sem, GROUP)
                    for pair in range(2):
                        dve.wait_ge(*done(s[f"ksum{pair}"], f))
                    dve.wait_ge(*done(s["att_out"], f + (-GROUP - 1)))
                    dve.reciprocal(k_rec[:, slot].rearrange("p a g -> p (a g)"),
                                   k_sum[:, slot].rearrange("p a g -> p (a g)")).then_inc(s["krec"].sem, GROUP)

                def q_add(f, b):
                    dve.wait_ge(*done(s["q_pe"], f + b))
                    dve.wait_ge(*done(s["qsub"], f + (b - 1)))
                    dve.tensor_tensor(q_tmp, bank[bk["Q"][b]][:], bias_wide[:, WQ, :], ALU.add).then_inc(s["q_add"].sem, 1)

                def q_soft(f, slot, b):
                    dve.wait_ge(*done(s["q_add"], f + b))
                    qv = q_tmp.rearrange("p (h e) -> p h e", h=H1)
                    dve.tensor_reduce(q_max[:], qv, AX.X, ALU.max).then_inc(s["qmax"].sem, 1)
                    dve.wait_ge(*done(s["qmax"], f + b))
                    dve.wait_ge(*done(s["qt_pe"], f + (b - 2 * GROUP)))
                    dve.wait_ge(*done(s["qsum"], f + (b - 2 * GROUP)))
                    dve.tensor_tensor(q_exp[:, slot, b, :].rearrange("p (h e) -> p h e", h=H1), qv,
                                      q_max[:].rearrange("p (h o) -> p h o", o=1).broadcast_to([P, H1, DH1]),
                                      ALU.subtract).then_inc(s["qsub"].sem, 1)

                def q_sums(f, slot, b):
                    dve.wait_ge(*done(s["qexp"], f + b))
                    dve.wait_ge(*done(s["qrec"], f + (b - 1)))
                    dve.tensor_reduce(q_sum[:], q_exp[:, slot, b, :].rearrange("p (h e) -> p h e", h=H1), AX.X, ALU.add
                                      ).then_inc(s["qsum"].sem, 1)
                    dve.wait_ge(*done(s["qsum"], f + b))
                    dve.wait_ge(*done(s["y_norm"], f + (b - 2 * GROUP)))
                    dve.reciprocal(q_rec[:, slot, b, :], q_sum[:]).then_inc(s["qrec"].sem, 1)

                def kv_out(k, kslot, b):
                    dve.wait_ge(*done(s["att_pe"], k + b))
                    dve.wait_ge(*done(s["y_pe"], k + (b - GROUP)))
                    dve.wait_ge(*done(s["krec"], k))
                    for h in range(2):
                        q2 = slice(DH1 * h, DH1 * (h + 1))
                        rc = k_rec[q2, kslot].rearrange("p a (j g) -> p (a j) g", g=GROUP)[:, :, b:b + 1]
                        last = dve.tensor_tensor(chunks(kv_blocks[b])[q2, :, q2], chunks(bank[bk["KV"][b]][:])[q2, :, q2],
                                                 rc.broadcast_to([DH1, C, DH1]), ALU.mult)
                    last.then_inc(s["att_out"].sem, 1)

                def step0(n, f, k, late, slot):
                    if k:
                        softmax(k, 0, (0,))
                    if late:
                        silu(late + (-1), 1)
                    if k:
                        softmax(k, 0, (1,))
                    if late:
                        s_low_part(late + (-1), 1)
                    if k:
                        softmax(k, 0, (2, 3))
                    if late:
                        output(late, 1)
                    if k:
                        softmax(k, 1, range(C))
                        sums_inverse(k, 0)
                    if n:
                        stats1(n, 0)
                        stats1(n, 1)
                    if k:
                        sums_inverse(k, 1)
                        y_norm(k, 1 - slot, 0)
                    if f:
                        v_add(f, slot, 0)
                    if k:
                        film_scale(k, 0)
                        silu(k, 0)
                    if f:
                        v_add(f, slot, 1)
                    if k:
                        y_norm(k, 1 - slot, 1)
                        s_low_part(k, 0)
                    if n:
                        xt_low(n, 1 - slot, 0)
                        xt_low(n, 1 - slot, 1)
                    if k:
                        output(k, 0)
                        film_scale(k, 1)

                def step1(n, f, k, late, slot):
                    if late:
                        output(late, 1)
                    if k:
                        kv_out(k, 1 - slot, 0)
                    if f:
                        k_soft(f, slot, 0)
                    if k:
                        y_norm(k, 1 - slot, 0)
                        kv_out(k, 1 - slot, 1)
                    if f:
                        k_soft(f, slot, 1)
                        v_add(f, slot, 0)
                    if k:
                        y_norm(k, 1 - slot, 1)
                    if n:
                        stats1(n, 0)
                        stats1(n, 1)
                    if k:
                        film_scale(k, 0)
                    if f:
                        q_add(f, 0)
                        q_soft(f, slot, 0)
                    if k:
                        silu(k, 0)
                    if f:
                        v_add(f, slot, 1)
                    if k:
                        film_scale(k, 1)
                        s_low_part(k, 0)
                    if f:
                        k_sums(f, slot)
                    if k:
                        silu(k, 1)
                    if f:
                        q_add(f, 1)
                    if k:
                        s_low_part(k, 1)
                    if f:
                        q_soft(f, slot, 1)
                    if k:
                        output(k, 0)
                    if n:
                        xt_low(n, 1 - slot, 0)
                        xt_low(n, 1 - slot, 1)
                    if f:
                        q_sums(f, slot, 0)
                        q_sums(f, slot, 1)

                dve.wait_ge(*upto(s["norm_in"], 16 * 2))
                dve.tensor_copy(norm_b_wide, col[:, NBI, :].rearrange("p (c o) -> p c o", o=1).broadcast_to([P, C, P])
                                ).then_inc(s["beta_wide"].sem, 1)
                program(dve, step0 if l == 0 else step1, weights, film)
                if l == 0:
                    dve.wait_ge(*done(s["o_out"], At(None, B - 1)))
                    dve.drain().then_inc(finished[0], 1)

        @block.tensor
        def _(pe):
            pe.wait_ge(consts, 1)
            for l, L in enumerate(layers):
                s, bk = S[l], BANKS[l]
                if l == 1:
                    pe.wait_ge(finished[0], 4)

                def weights():
                    pe.wait_ge(*upto(s["mask_in"], 16))
                    pe.transpose(bank[bk["MASK"]][:, 0:B], mask_rows[:], ident[0:B, 0:B]).then_inc(s["mask_pe"].sem, 1)
                    pe.wait_ge(*upto(s["beta_wide"], 1))
                    for j in range(3):
                        pe.wait_ge(*upto(s[f"w_in{j}"], 16))
                        for c in range(C):
                            last = pe.matmul(bank[bk["BIAS"][j]][:], norm_b_wide[:, c, :], raw[j][:, c],
                                             start=(c == 0), stop=(c == C - 1))
                        last.then_inc(s["bias_pe"].sem, 1)
                    if l == 0:
                        pe.wait_ge(cond_dve, 2)
                        for k in range(KE):
                            last = pe.transpose(bank[bk["TURNED"][1]][:, k * B:(k + 1) * B],
                                                z_s[0:B].rearrange("p a n -> p (a n)")[:, k * P:(k + 1) * P],
                                                ident[0:B, 0:B])
                        last.then_inc(cond_pe, 1)
                    for j in range(2):
                        pe.wait_ge(*upto(s["bias_dve"], j + 1))
                        if l == 0 and j == 1:
                            pe.wait_ge(cond_dve, 3)
                        for c in range(C):
                            last = pe.transpose(bank[bk["TURNED"][j]][:, c * P:(c + 1) * P],
                                                bias_wide[:, j, c * P:(c + 1) * P], ident[:])
                        last.then_inc(s["tr_pe"].sem, 1)
                    pe.wait_ge(*upto(s["mask_moved"], 48))
                    pe.drain().then_inc(s["ready_pe"].sem, 1)
                    for n in ("ready_dve", "ready_act", "ready_pool"):
                        pe.wait_ge(*upto(s[n], 1))

                def film():
                    for h in range(2):
                        claim(bk["EMB"][h])
                    for k in range(KE):
                        pe.wait_ge(*upto(s[f"emb_in{k % 4}"], 16 * (k // 4 + 1)))
                        for h in range(2):
                            last = pe.matmul(bank[bk["EMB"][h]][0:B, :], silu_cond[:, k, :],
                                             emb_ring[:, (k + 2) % 4, h * D:(h + 1) * D], start=(k == 0), stop=(k == KE - 1))
                        last.then_inc(s["emb_pe"].sem, 1)
                    claim(bk["FILM"])
                    pe.wait_ge(*upto(s["emb_dve"], 2))
                    for k in range(2 * C):
                        last = pe.transpose(bank[bk["FILM"]][:, k * B:(k + 1) * B],
                                            yn[0:B].rearrange("p a n -> p (a n)")[:, k * P:(k + 1) * P], ident[0:B, 0:B])
                    last.then_inc(s["film_pe"].sem, 1)
                    pe.wait_ge(*upto(s["film_dve"], 1))
                    pe.wait_ge(*upto(s["w_split"], 4))
                    pe.wait_ge(*upto(s["w_high"], 4))

                before = {}

                def claim(b, *readers):
                    for sm, at in before.get(b, ()):
                        pe.wait_ge(*done(s[sm], at))
                    before[b] = readers

                def turn(f, b):
                    claim(bk["X"][b], ("xt_low", f + b))
                    pe.wait_ge(*done(s["xn_full"], f + b))
                    for c in range(C):
                        last = pe.transpose(bank[bk["X"][b]][:, c * P:(c + 1) * P], xn[:, b, c * P:(c + 1) * P], ident[:])
                    last.then_inc(s["xn_turned"].sem, 1)

                def three(o, hi, lo, w_h, w_l, first, stop):
                    pe.matmul(o, hi, w_h, start=first, stop=False)
                    pe.matmul(o, hi, w_l, start=False, stop=False)
                    return pe.matmul(o, lo, w_h, start=False, stop=stop)

                def project(f, slot, w, pair, to, sm, reader, masked=False):
                    claim(to, (reader, f))
                    pe.wait_ge(*done(s["xt_low"], f + (GROUP - 1)))
                    for j in range(2):
                        c = 2 * pair + j
                        o = bank[to][:, j * N:(j + 1) * N]
                        if masked:
                            cols = (mask_wide[:, f.const * P:f.const * P + N] if f.reg is None
                                    else mask_wide[:, bass.ds(f.value() * P, N)])
                            pe.matmul(o, ones_parts[:], cols, start=True, stop=False)
                        for kc in range(C):
                            last = three(o, w_hi[:, w, kc, c * P:(c + 1) * P], w_lo[:, w, kc, c * P:(c + 1) * P],
                                         xt_hi[:, slot, kc, :], xt_lo[:, slot, kc, :],
                                         kc == 0 and not masked, kc == C - 1)
                    last.then_inc(s[sm].sem, GROUP)

                def project_rows(f, slot, b, w, to, sm, reader):
                    claim(to, (reader, f + b))
                    for kc in range(C):
                        last = three(bank[to][:], xt_hi[:, slot, kc, b * P:(b + 1) * P], xt_lo[:, slot, kc, b * P:(b + 1) * P],
                                     w_hi[:, w, kc, :], w_lo[:, w, kc, :], kc == 0, kc == C - 1)
                    last.then_inc(s[sm].sem, 1)

                def values(f, slot, b):
                    project_rows(f, slot, b, WV, bk["V"][b], "v_pe", "v_add")

                def scores(k, kslot, b):
                    qv = q_t[:, kslot, :].rearrange("p (c n) -> p c n", c=C)
                    if b == 0:
                        for n in ("pa_out", "pb_out", "ka_out", "kb_out"):
                            pe.wait_ge(*done(s[n], k))
                    for c in range(C):
                        claim(c, (f"masked{c}", k + b))
                        o = bank[c][:].rearrange("p (r n) -> p r n", r=HC0)
                        pe.matmul(o, qv[:, c, b * P:(b + 1) * P], k_blocks[:, kslot, c, b], start=True, stop=True
                                  ).then_inc(s[f"s_pe{c}"].sem, 1)

                def turn_probs(k, b, c):
                    pe.wait_ge(*done(s[f"exp{c}"], k + b))
                    claim(4 + c % 2, (f"pt_out{c}", k + b))
                    for r in range(HC0):
                        last = pe.transpose(bank[4 + c % 2][:, r * P:(r + 1) * P], prob[:, b, 4 * c + r, :], ident[:])
                    last.then_inc(s[f"pt_pe{c}"].sem, 1)

                def weigh(k, kslot, b, between):
                    claim(bk["PV"][b], ("pv_out", k + b))
                    pe.wait_ge(*done(s["v_mask"], k + b))
                    for c in range(C):
                        pe.wait_ge(*done(s[f"pt_out{c}"], k + b))
                        for r in range(HC0):
                            h = HC0 * c + r
                            last = pe.matmul(bank[bk["PV"][b]][DH0 * r:DH0 * (r + 1), c * P:(c + 1) * P],
                                             v_s[:, kslot, b, h * DH0:(h + 1) * DH0], prob_t[:, c % 2, r * P:(r + 1) * P],
                                             start=True, stop=True, tile_position=(0, DH0 * r))
                        last.then_inc(s[f"pv{c}"].sem, 1)
                        if c + 2 < C:
                            turn_probs(k, b, c + 2)
                        if c == C - 2:
                            between()

                def y_rows(k, b):
                    claim(bk["Y"][b], ("y_norm", k + b))
                    pe.wait_ge(*done(s["pv_out"], k + b))
                    for c in range(C):
                        last = pe.transpose(bank[bk["Y"][b]][:, c * P:(c + 1) * P], y_t[:, c * P:(c + 1) * P], ident[:])
                    last.then_inc(s["y_pe"].sem, 1)

                def turn_yn(k, b):
                    claim(bk["H"][b], ("z_a_full", k + b))
                    pe.wait_ge(*done(s["yn_full"], k + b))
                    for c in range(C):
                        last = pe.transpose(bank[bk["H"][b]][:, c * P:(c + 1) * P], yn[:, b, c * P:(c + 1) * P], ident[:])
                    last.then_inc(s["h_pe"].sem, 1)

                def output(at, b):
                    claim(bk["O"][b], ("o_out", at))
                    pe.wait_ge(*done(s["s_low"], at))
                    for kc in range(C):
                        last = three(bank[bk["O"][b]][:], s_hi[:, b, kc * P:(kc + 1) * P], s_lo[:, b, kc * P:(kc + 1) * P],
                                     w_hi[:, WO, kc, :], w_lo[:, WO, kc, :], kc == 0, kc == C - 1)
                    last.then_inc(s["o_pe"].sem, 1)

                def turn_k(k, kslot, b):
                    claim(bk["KT"][b], ("kt_out", k + b))
                    for pair in range(2):
                        pe.wait_ge(*done(s[f"kexp{pair}"], k))
                    kv = k_exp[:, kslot, :].rearrange("p (c g n) -> p c g n", c=C, g=GROUP)
                    for c in range(C):
                        last = pe.transpose(bank[bk["KT"][b]][:, c * P:(c + 1) * P], kv[:, c, b, :], ident[:])
                    last.then_inc(s["kt_pe"].sem, 1)

                def turn_q(k, kslot, b):
                    claim(bk["QT"][b], ("qt_out", k + b))
                    pe.wait_ge(*done(s["qexp"], k + b))
                    for c in range(C):
                        last = pe.transpose(bank[bk["QT"][b]][:, c * P:(c + 1) * P], q_exp[:, kslot, b, c * P:(c + 1) * P], ident[:])
                    last.then_inc(s["qt_pe"].sem, 1)

                def keys_values(k, kslot, b):
                    claim(bk["KV"][b], ("att_out", k + b))
                    pe.wait_ge(*done(s["kt_out"], k + b))
                    pe.wait_ge(*done(s["v_mask"], k + b))
                    for c in range(C):
                        last = pe.matmul(bank[bk["KV"][b]][:, c * P:(c + 1) * P], k_tok[b][:, c * P:(c + 1) * P],
                                         v_s[:, kslot, b, c * P:(c + 1) * P], start=True, stop=True)
                    last.then_inc(s["att_pe"].sem, 1)

                def query(k, b):
                    claim(bk["Y"][b], ("y_norm", k + b))
                    pe.wait_ge(*done(s["att_out"], k + b))
                    pe.wait_ge(*done(s["qt_out"], k + b))
                    for c in range(C):
                        last = pe.matmul(bank[bk["Y"][b]][:, c * P:(c + 1) * P], q_feat[b][:, c * P:(c + 1) * P],
                                         kv_blocks[b][:, c * P:(c + 1) * P], start=True, stop=True)
                    last.then_inc(s["y_pe"].sem, 1)

                def step0(n, f, k, late, slot):
                    if k:
                        scores(k, 1 - slot, 0)
                    if f:
                        project(f, slot, WQ, 0, bk["Q"][0], "pa_pe", "pa_out")
                    if late:
                        output(late, 1)
                    if k:
                        scores(k, 1 - slot, 1)
                        turn_probs(k, 0, 0)
                        turn_probs(k, 0, 1)
                    if f:
                        project(f, slot, WK, 0, bk["K"][0], "ka_pe", "ka_out")
                    if k:
                        weigh(k, 1 - slot, 0, lambda: turn_probs(k, 1, 0))
                    if f:
                        project(f, slot, WK, 1, bk["K"][1], "kb_pe", "kb_out")
                    if k:
                        turn_probs(k, 1, 1)
                        y_rows(k, 0)
                    if f:
                        values(f, slot, 0)
                    if k:
                        weigh(k, 1 - slot, 1, lambda: turn_yn(k, 0))
                    if f:
                        values(f, slot, 1)
                    if k:
                        y_rows(k, 1)
                    if f:
                        project(f, slot, WQ, 1, bk["Q"][1], "pb_pe", "pb_out")
                    if n:
                        turn(n, 0)
                        turn(n, 1)
                    if k:
                        output(k, 0)
                        turn_yn(k, 1)

                def step1(n, f, k, late, slot):
                    if k:
                        turn_k(k, 1 - slot, 0)
                        turn_q(k, 1 - slot, 0)
                        turn_k(k, 1 - slot, 1)
                    if late:
                        output(late, 1)
                    if f:
                        project(f, slot, WK, 0, bk["K"][0], "ka_pe", "kbias0", True)
                    if k:
                        turn_q(k, 1 - slot, 1)
                        keys_values(k, 1 - slot, 0)
                    if f:
                        project(f, slot, WK, 1, bk["K"][1], "kb_pe", "kbias1", True)
                    if k:
                        query(k, 0)
                        keys_values(k, 1 - slot, 1)
                    if f:
                        values(f, slot, 0)
                    if k:
                        query(k, 1)
                    if f:
                        project_rows(f, slot, 0, WQ, bk["Q"][0], "q_pe", "q_add")
                    if k:
                        turn_yn(k, 0)
                    if f:
                        values(f, slot, 1)
                    if k:
                        turn_yn(k, 1)
                    if f:
                        project_rows(f, slot, 1, WQ, bk["Q"][1], "q_pe", "q_add")
                    if n:
                        turn(n, 0)
                    if k:
                        output(k, 0)
                    if n:
                        turn(n, 1)

                program(pe, step0 if l == 0 else step1, weights, film, before)
                if l == 0:
                    pe.drain().then_inc(finished[0], 1)


_OUT = ((32, 128, 512), 'float32')


def kernel(**inputs):
    import numpy as _np
    import concourse.bacc as _bacc
    from concourse import mybir as _mybir
    from concourse.bass_utils import run_bass_kernel_spmd as _run

    nc = _bacc.Bacc("TRN2", target_bir_lowering=False, num_devices=1)
    arrays, args = {}, {}
    for name, value in inputs.items():
        a = _np.ascontiguousarray(value)
        arrays[f"in_{name}_dram"] = a
        args[name] = nc.dram_tensor(f"in_{name}_dram", a.shape, _mybir.dt.from_np(a.dtype), kind="ExternalInput").ap()
    out = nc.dram_tensor("out_0_dram", _OUT[0], _mybir.dt.from_np(_np.dtype(_OUT[1])), kind="ExternalOutput").ap()
    build(nc, args, out)
    r = _run(nc, [arrays], core_ids=[0])
    return r.results[0]["out_0_dram"]
```
